# Optimizing a Trainium2 kernel written in Bass

```python
import numpy as np
import jax
import jax.numpy as jnp

def _softmax(x, axis=-1):
    return jax.nn.softmax(x, axis=axis)

def _gelu(x):
    return jax.nn.gelu(x, approximate=True)

def _silu(x):
    return jax.nn.silu(x)

def _sigmoid(x):
    return jax.nn.sigmoid(x)

def _layernorm(x, axis=-1, eps=1e-05):
    m = jnp.mean(x, axis=axis, keepdims=True)
    v = jnp.var(x, axis=axis, keepdims=True)
    return (x - m) / jnp.sqrt(v + eps)

def _scatter_add(tgt, idx, src, axis=0):
    return tgt.at[idx].add(src)

def _segment_sum(src, seg, n):
    return jax.ops.segment_sum(src, seg, n)
kernel_name = 'mk_gnn_resnorm_d4_gnn_r64_5955bf'

def setup_inputs(seed: int=0):
    np.random.seed(seed)
    _w = jnp.asarray

    def _rec_inputs():
        import jax
        import jax.numpy as jnp
        _gk = jax.random.key(seed)
        x = -0.0005121 + 1.001 * jax.random.normal(jax.random.fold_in(_gk, 1), (50000, 64), jnp.float32)
        src = jax.random.randint(jax.random.fold_in(_gk, 2), (25000,), 0, 50000, jnp.int32)
        dst = jnp.minimum((50000 * jax.random.uniform(jax.random.fold_in(_gk, 3), (25000,)) ** 2.0).astype(jnp.int32), 49999)
        _o = jnp.argsort(dst, stable=True)
        src = src[_o]
        dst = dst[_o]
        edge_attr_16 = -5.3897e-05 + 0.999841 * jax.random.normal(jax.random.fold_in(_gk, 12), (25000, 16), jnp.float32)
        edge_attr_3 = 0.000669165 + 0.999965 * jax.random.normal(jax.random.fold_in(_gk, 13), (25000, 3), jnp.float32)
        edge_type_8 = jax.random.randint(jax.random.fold_in(_gk, 15), (25000,), 0, 8, jnp.int32)
        node_type_2 = jax.random.randint(jax.random.fold_in(_gk, 16), (50000,), 0, 2, jnp.int32)
        return (x, src, dst, edge_attr_16, edge_attr_3, edge_type_8, node_type_2)
    x, src, dst, edge_attr_16, edge_attr_3, edge_type_8, node_type_2 = _rec_inputs()

    def _L0_gnn_setup():
        import jax, jax.numpy as jnp
        import numpy as np
        N_NODES = 50000
        N_EDGES = 25000
        D_NODE = 64
        D_EDGE = 16
        HEADS = 4
        ATT_F = 16
        LN_EPS = 1e-06
        key = jax.random.key(seed)
        ks = jax.random.split(key, 9)
        nodes = jax.random.normal(ks[0], (N_NODES, D_NODE), dtype=jnp.float32)
        edges = jax.random.normal(ks[1], (N_EDGES, D_EDGE), dtype=jnp.float32)
        receivers = jax.random.randint(ks[2], (N_EDGES,), 0, N_NODES)
        senders = jax.random.randint(ks[3], (N_EDGES,), 0, N_NODES)
        W = jax.random.normal(ks[4], (HEADS, ATT_F, D_NODE), dtype=jnp.float32) * np.sqrt(2.0 / D_NODE)
        W_edge = jax.random.normal(ks[5], (HEADS, ATT_F, D_EDGE), dtype=jnp.float32) * np.sqrt(2.0 / D_EDGE)
        a = jax.random.normal(ks[6], (HEADS, 3 * ATT_F), dtype=jnp.float32) * np.sqrt(2.0 / (HEADS + 3 * ATT_F))
        ln_scale = jnp.ones((HEADS * ATT_F,), dtype=jnp.float32)
        ln_bias = jnp.zeros((HEADS * ATT_F,), dtype=jnp.float32)
        return {'nodes': nodes, 'edges': edges, 'receivers': receivers, 'senders': senders, 'W': W, 'W_edge': W_edge, 'a': a, 'ln_scale': ln_scale, 'ln_bias': ln_bias}
    _L0_gnn_all = _L0_gnn_setup()
    _L0_gnn_in = {k: v for k, v in _L0_gnn_all.items() if k in ('W', 'W_edge', 'a', 'ln_scale', 'ln_bias')}
    del _L0_gnn_all

    def _L1_gnn_setup():
        import jax, jax.numpy as jnp
        import numpy as np
        N_NODES = 50000
        N_EDGES = 12500
        IN_NF = 64
        HID_NF = 64
        OUT_NF = 64

        def _linear_init(key, fan_in, fan_out):
            kw, kb = jax.random.split(key)
            bound = 1.0 / np.sqrt(fan_in)
            W = jax.random.uniform(kw, (fan_in, fan_out), jnp.float32, -bound, bound)
            b = jax.random.uniform(kb, (fan_out,), jnp.float32, -bound, bound)
            return (W, b)
        key = jax.random.key(seed)
        ks = jax.random.split(key, 9)
        h = jax.random.normal(ks[0], (N_NODES, IN_NF), jnp.float32)
        edges_index = jax.random.randint(ks[1], (2, N_EDGES), 0, N_NODES, jnp.int64)
        coord_diff = jax.random.normal(ks[2], (N_EDGES, 3), jnp.float32)
        We1, be1 = _linear_init(ks[3], 2 * IN_NF + 1, HID_NF)
        We2, be2 = _linear_init(ks[4], HID_NF, HID_NF)
        Wa, ba = _linear_init(ks[5], HID_NF, 1)
        Wn1, bn1 = _linear_init(ks[6], HID_NF + IN_NF, HID_NF)
        Wn2, bn2 = _linear_init(ks[7], HID_NF, OUT_NF)
        return {'h': h, 'edges_index': edges_index, 'coord_diff': coord_diff, 'We1': We1, 'be1': be1, 'We2': We2, 'be2': be2, 'Wa': Wa, 'ba': ba, 'Wn1': Wn1, 'bn1': bn1, 'Wn2': Wn2, 'bn2': bn2}
    _L1_gnn_all = _L1_gnn_setup()
    _L1_gnn_in = {k: v for k, v in _L1_gnn_all.items() if k in ('We1', 'be1', 'We2', 'be2', 'Wa', 'ba', 'Wn1', 'bn1', 'Wn2', 'bn2')}
    del _L1_gnn_all

    def _L2_gnn_setup():
        import jax, jax.numpy as jnp
        import numpy as np
        N_NODES = 100000
        N_EDGES = 25000
        D = 64
        NUM_GROUPS = 2
        key = jax.random.key(seed)
        k_h, k_ws, k_wg, k_src, k_dst, k_grp = jax.random.split(key, 6)
        h = jax.random.normal(k_h, (N_NODES, D), dtype=jnp.float32)
        W_self = jax.random.normal(k_ws, (D, D), dtype=jnp.float32) * (1.0 / np.sqrt(D))
        W_groups = jax.random.normal(k_wg, (NUM_GROUPS, D, D), dtype=jnp.float32) * (1.0 / np.sqrt(D))
        src = jax.random.randint(k_src, (N_EDGES,), 0, N_NODES, dtype=jnp.int32)
        dst = jax.random.randint(k_dst, (N_EDGES,), 0, N_NODES, dtype=jnp.int32)
        group_labels = jax.random.randint(k_grp, (N_NODES,), 0, NUM_GROUPS, dtype=jnp.int32)
        return {'h': h, 'W_self': W_self, 'W_groups': W_groups, 'src': src, 'dst': dst, 'group_labels': group_labels}
    _L2_gnn_all = _L2_gnn_setup()
    _L2_gnn_in = {k: v for k, v in _L2_gnn_all.items() if k in ('W_self', 'W_groups')}
    del _L2_gnn_all

    def _L3_gnn_setup():
        import jax, jax.numpy as jnp
        import numpy as np
        NEG_SLOPE = 0.2

        def _gat_relation(x, src, dst, mask, N, Wr, a_src, a_dst, br):
            h = x @ Wr
            s = h @ a_src
            d = h @ a_dst
            e = jax.nn.leaky_relu(s[src] + d[dst], negative_slope=NEG_SLOPE)
            e = jnp.where(mask, e, -jnp.inf)
            m = jax.ops.segment_max(e, dst, num_segments=N)
            w = jnp.where(mask, jnp.exp(e - m[dst]), 0.0)
            denom = jax.ops.segment_sum(w, dst, num_segments=N)
            alpha = w / denom[dst]
            msg = alpha[:, None] * h[src]
            return jax.ops.segment_sum(msg, dst, num_segments=N) + br
        key = jax.random.key(seed)
        ks = jax.random.split(key, 9)
        N, E, D, F, R = (100000, 25000, 64, 64, 8)
        x = jax.random.normal(ks[0], (N, D), dtype=jnp.float32)
        edge_index = jax.random.randint(ks[1], (2, E), 0, N, dtype=jnp.int32)
        edge_type = jax.random.randint(ks[2], (E,), 0, R, dtype=jnp.int32)
        W_self = jax.random.normal(ks[3], (D, F), dtype=jnp.float32) * 0.1
        b_self = jax.random.normal(ks[4], (F,), dtype=jnp.float32) * 0.1
        W = jax.random.normal(ks[5], (R, D, F), dtype=jnp.float32) * 0.1
        att_src = jax.random.normal(ks[6], (R, F), dtype=jnp.float32) * 0.1
        att_dst = jax.random.normal(ks[7], (R, F), dtype=jnp.float32) * 0.1
        bias = jax.random.normal(ks[8], (R, F), dtype=jnp.float32) * 0.1
        return {'x': x, 'edge_index': edge_index, 'edge_type': edge_type, 'W_self': W_self, 'b_self': b_self, 'W': W, 'att_src': att_src, 'att_dst': att_dst, 'bias': bias}
    _L3_gnn_all = _L3_gnn_setup()
    _L3_gnn_in = {k: v for k, v in _L3_gnn_all.items() if k in ('W_self', 'b_self', 'W', 'att_src', 'att_dst', 'bias')}
    del _L3_gnn_all
    return {'x': x, 'src': src, 'dst': dst, 'edge_attr_16': edge_attr_16, 'edge_attr_3': edge_attr_3, 'edge_type_8': edge_type_8, 'node_type_2': node_type_2, 'L0_gnn_W': _L0_gnn_in['W'], 'L0_gnn_W_edge': _L0_gnn_in['W_edge'], 'L0_gnn_a': _L0_gnn_in['a'], 'L0_gnn_ln_scale': _L0_gnn_in['ln_scale'], 'L0_gnn_ln_bias': _L0_gnn_in['ln_bias'], 'L1_gnn_We1': _L1_gnn_in['We1'], 'L1_gnn_be1': _L1_gnn_in['be1'], 'L1_gnn_We2': _L1_gnn_in['We2'], 'L1_gnn_be2': _L1_gnn_in['be2'], 'L1_gnn_Wa': _L1_gnn_in['Wa'], 'L1_gnn_ba': _L1_gnn_in['ba'], 'L1_gnn_Wn1': _L1_gnn_in['Wn1'], 'L1_gnn_bn1': _L1_gnn_in['bn1'], 'L1_gnn_Wn2': _L1_gnn_in['Wn2'], 'L1_gnn_bn2': _L1_gnn_in['bn2'], 'L2_gnn_W_self': _L2_gnn_in['W_self'], 'L2_gnn_W_groups': _L2_gnn_in['W_groups'], 'L3_gnn_W_self': _L3_gnn_in['W_self'], 'L3_gnn_b_self': _L3_gnn_in['b_self'], 'L3_gnn_W': _L3_gnn_in['W'], 'L3_gnn_att_src': _L3_gnn_in['att_src'], 'L3_gnn_att_dst': _L3_gnn_in['att_dst'], 'L3_gnn_bias': _L3_gnn_in['bias']}

def reference(x, src, dst, edge_attr_16, edge_attr_3, edge_type_8, node_type_2, L0_gnn_W, L0_gnn_W_edge, L0_gnn_a, L0_gnn_ln_scale, L0_gnn_ln_bias, L1_gnn_We1, L1_gnn_be1, L1_gnn_We2, L1_gnn_be2, L1_gnn_Wa, L1_gnn_ba, L1_gnn_Wn1, L1_gnn_bn1, L1_gnn_Wn2, L1_gnn_bn2, L2_gnn_W_self, L2_gnn_W_groups, L3_gnn_W_self, L3_gnn_b_self, L3_gnn_W, L3_gnn_att_src, L3_gnn_att_dst, L3_gnn_bias):
    import jax
    import jax.numpy as jnp

    def _L0_gnn_ref(nodes, edges, receivers, senders, W, W_edge, a, ln_scale, ln_bias):
        import jax, jax.numpy as jnp
        import numpy as np
        N_NODES = 50000
        N_EDGES = 25000
        D_NODE = 64
        D_EDGE = 16
        HEADS = 4
        ATT_F = 16
        LN_EPS = 1e-06
        n = nodes.shape[0]
        self_idx = jnp.arange(n)
        r = jnp.concatenate([receivers, self_idx], axis=0)
        s = jnp.concatenate([senders, self_idx], axis=0)
        e = jnp.concatenate([edges, jnp.zeros((n, edges.shape[1]), edges.dtype)], axis=0)
        Wn = jnp.einsum('hfi,ni->nhf', W, nodes)
        Ws = Wn[s]
        Wr = Wn[r]
        We = jnp.einsum('hfi,ei->ehf', W_edge, e)
        a_s, a_r, a_e = jnp.split(a, 3, axis=-1)
        msg = jnp.einsum('ehf,hf->eh', Ws, a_s) + jnp.einsum('ehf,hf->eh', Wr, a_r) + jnp.einsum('ehf,hf->eh', We, a_e)
        lm = jax.nn.leaky_relu(msg)
        seg_max = jax.ops.segment_max(lm, r, num_segments=n)
        z = lm - seg_max[r]
        exp_z = jnp.exp(z)
        norm = jax.ops.segment_sum(exp_z, r, num_segments=n)
        alpha = exp_z / norm[r]
        att_msg = alpha[:, :, None] * Ws
        aggr = jax.ops.segment_sum(att_msg, r, num_segments=n)
        out = aggr.reshape(n, -1)
        out = jax.nn.elu(out)
        mean = jnp.mean(out, axis=-1, keepdims=True)
        var = jnp.mean(jnp.square(out - mean), axis=-1, keepdims=True)
        out = (out - mean) * jax.lax.rsqrt(var + LN_EPS)
        out = out * ln_scale + ln_bias
        return out

    def _L1_gnn_ref(h, edges_index, coord_diff, We1, be1, We2, be2, Wa, ba, Wn1, bn1, Wn2, bn2):
        import jax, jax.numpy as jnp
        import numpy as np
        N_NODES = 50000
        N_EDGES = 12500
        IN_NF = 64
        HID_NF = 64
        OUT_NF = 64

        def _linear_init(key, fan_in, fan_out):
            kw, kb = jax.random.split(key)
            bound = 1.0 / np.sqrt(fan_in)
            W = jax.random.uniform(kw, (fan_in, fan_out), jnp.float32, -bound, bound)
            b = jax.random.uniform(kb, (fan_out,), jnp.float32, -bound, bound)
            return (W, b)
        row = edges_index[0]
        col = edges_index[1]
        radial = jnp.sum(coord_diff ** 2, axis=1, keepdims=True)
        edge_in = jnp.concatenate([h[row], h[col], radial], axis=1)
        e = jax.nn.silu(edge_in @ We1 + be1)
        e = jax.nn.silu(e @ We2 + be2)
        att = jax.nn.sigmoid(e @ Wa + ba)
        e = e * att
        agg = jax.ops.segment_sum(e, row, num_segments=h.shape[0])
        node_in = jnp.concatenate([h, agg], axis=1)
        out = jax.nn.silu(node_in @ Wn1 + bn1) @ Wn2 + bn2
        return out

    def _L2_gnn_ref(h, W_self, W_groups, src, dst, group_labels):
        import jax, jax.numpy as jnp
        import numpy as np
        N_NODES = 100000
        N_EDGES = 25000
        D = 64
        NUM_GROUPS = 2
        n_nodes = h.shape[0]
        num_groups = W_groups.shape[0]
        h_self = h @ W_self.T
        h_src = jnp.take(h, src, axis=0)
        g_src = jnp.take(group_labels, src, axis=0)
        h_agg = jnp.zeros((n_nodes, W_groups.shape[1]), dtype=h.dtype)
        for i in range(num_groups):
            masked = jnp.where((g_src == i)[:, None], h_src, 0.0)
            seg = jax.ops.segment_sum(masked, dst, num_segments=n_nodes)
            h_agg = h_agg + seg @ W_groups[i].T
        return h_self + h_agg

    def _L3_gnn_ref(x, edge_index, edge_type, W_self, b_self, W, att_src, att_dst, bias):
        import jax, jax.numpy as jnp
        import numpy as np
        NEG_SLOPE = 0.2

        def _gat_relation(x, src, dst, mask, N, Wr, a_src, a_dst, br):
            h = x @ Wr
            s = h @ a_src
            d = h @ a_dst
            e = jax.nn.leaky_relu(s[src] + d[dst], negative_slope=NEG_SLOPE)
            e = jnp.where(mask, e, -jnp.inf)
            m = jax.ops.segment_max(e, dst, num_segments=N)
            w = jnp.where(mask, jnp.exp(e - m[dst]), 0.0)
            denom = jax.ops.segment_sum(w, dst, num_segments=N)
            alpha = w / denom[dst]
            msg = alpha[:, None] * h[src]
            return jax.ops.segment_sum(msg, dst, num_segments=N) + br
        N = x.shape[0]
        R = W.shape[0]
        loops = jnp.arange(N, dtype=edge_index.dtype)
        src = jnp.concatenate([edge_index[0], loops])
        dst = jnp.concatenate([edge_index[1], loops])
        ones_loops = jnp.ones((N,), dtype=bool)
        out = x @ W_self + b_self
        for r in range(R):
            mask = jnp.concatenate([edge_type == r, ones_loops])
            out = out + _gat_relation(x, src, dst, mask, N, W[r], att_src[r], att_dst[r], bias[r])
        return out
    edge_index = jnp.stack([src, dst])
    x = _layernorm(x + _L0_gnn_ref(x, edge_attr_16, dst, src, L0_gnn_W, L0_gnn_W_edge, L0_gnn_a, L0_gnn_ln_scale, L0_gnn_ln_bias), axis=-1)
    x = _layernorm(x + _L1_gnn_ref(x, edge_index, edge_attr_3, L1_gnn_We1, L1_gnn_be1, L1_gnn_We2, L1_gnn_be2, L1_gnn_Wa, L1_gnn_ba, L1_gnn_Wn1, L1_gnn_bn1, L1_gnn_Wn2, L1_gnn_bn2), axis=-1)
    x = _layernorm(x + _L2_gnn_ref(x, L2_gnn_W_self, L2_gnn_W_groups, src, dst, node_type_2), axis=-1)
    x = _layernorm(x + _L3_gnn_ref(x, edge_index, edge_type_8, L3_gnn_W_self, L3_gnn_b_self, L3_gnn_W, L3_gnn_att_src, L3_gnn_att_dst, L3_gnn_bias), axis=-1)
    return x

_drawn_inputs = setup_inputs


def setup_inputs(seed=0):
    import zlib

    import numpy as np

    out = dict(_drawn_inputs(seed))
    spreads = {'L0_gnn_ln_scale': (1.0, 0.2), 'L0_gnn_ln_bias': (0.0, 0.1)}
    factors = {'edge_attr_3': 8.0,
     'L1_gnn_We1': 8.0,
     'L1_gnn_be1': 38.153,
     'L1_gnn_We2': 8.0,
     'L1_gnn_be2': 37.666,
     'L1_gnn_Wa': 8.0,
     'L1_gnn_bn1': 3.26,
     'L3_gnn_att_dst': 13.372}
    for name, (base, spread) in spreads.items():
        noise = np.random.default_rng([zlib.crc32(name.encode()), seed]).standard_normal(out[name].shape)
        drawn = base * np.exp(spread * noise) if base else spread * noise
        out[name] = jnp.asarray(drawn.astype(out[name].dtype))
    for name, factor in factors.items():
        out[name] = (out[name] * factor).astype(out[name].dtype)
    return out
```

```python
from contextlib import ExitStack

import concourse.bass as bass
from concourse import mybir

F32 = mybir.dt.float32
BF16 = mybir.dt.bfloat16
I32 = mybir.dt.int32
ALU = mybir.AluOpType
ACT = mybir.ActivationFunctionType
AX = mybir.AxisListType

N = 50000
E = 25000
D = 64
P = 125
EJ = E // P
NK = N // P
G = 4
CH = EJ // G
NG = 8
NCH = NK // NG
R = 8
H = 4
HF = 16
LO = 256
HB = 98
REC = 8
SRC, DST, TYPE, RADIAL, ATT = 0, 1, 2, 3, 4
BIG = 1.0e30
SKIP = 1.0e6
assert P * EJ == E and P * NK == N and 2 * HB * LO >= N and CH % 2 == 0 and NCH % 2 == 0


class Count:

    def __init__(self, sem):
        self.sem, self.n = sem, 0

    def up(self, ins):
        self.n += 1
        return ins.then_inc(self.sem, 1)

    def here(self, eng):
        eng.wait_ge(self.sem, self.n)


class LoopCount:

    def __init__(self, sem, per, base=0, g=None):
        self.sem, self.per, self.base, self.n, self.g = sem, per, base, 0, g

    def up(self, ins):
        self.n += 1
        assert self.n <= self.per
        return ins.then_inc(self.sem, 1)

    def here(self, eng, i):
        eng.wait_ge(self.sem, i * self.per + (self.base + self.n))
        if self.g:
            self.g.passed(eng)

    def at(self, i, n):
        return i * self.per + (self.base + n)


class Graph:

    def __init__(self, nc, args, ctx):
        self.nc, self.ctx, self.a = nc, ctx, args
        self.sems, self.raised = {"waits_passed": ctx.enter_context(nc.semaphore("waits_passed"))}, []

    def sem(self, name):
        if name not in self.sems:
            self.sems[name] = self.ctx.enter_context(self.nc.semaphore(name))
        self.raised.append(self.sems[name])
        return self.sems[name]

    def once(self, name):
        return self.ctx.enter_context(self.nc.semaphore(name))

    def passed(self, eng):
        eng.sem_inc(self.sems["waits_passed"], 1)

    def clear(self):
        with self.nc.Block() as block:
            @block.sync
            def _(sp):
                for s in self.raised:
                    sp.sem_clear(s)
                sp.sem_clear(self.sems["waits_passed"])
        self.raised = []

    def sb(self, name, shape, dt=F32, ctx=None):
        t = (ctx or self.ctx).enter_context(self.nc.sbuf_tensor(name, shape, dt))
        return t

    def ps(self, name, shape, dt=F32, ctx=None):
        return ctx.enter_context(self.nc.psum_tensor(name, shape, dt))


def weights(g):
    g.ident = g.sb("ident", [128, 128])
    g.identb = g.sb("identb", [128, 128], BF16)
    g.ones = g.sb("ones", [128, 128])
    g.w0 = g.sb("w0", [128, D + 2 * H])
    g.n1 = g.sb("n1", [128, D])
    g.n3 = g.sb("n3", [128, D])
    g.n4 = g.sb("n4", [128, D])
    g.w1a = g.sb("w1a", [128, D])
    g.w1r = g.sb("w1r", [P, D])
    g.be1 = g.sb("be1", [D, 1])
    g.w2 = g.sb("w2", [D, D])
    g.be2 = g.sb("be2", [D, 1])
    g.wa = g.sb("wa", [D, D])
    g.ba = g.sb("ba", [D, 1])
    g.wn1 = g.sb("wn1", [128, D])
    g.bn1 = g.sb("bn1", [D, 1])
    g.wn2 = g.sb("wn2", [D + 1, D])
    g.wg = g.sb("wg", [128, D])
    g.w3 = g.sb("w3", [128, R * D])
    g.w3s = g.sb("w3s", [128, 2 * R])
    g.b4 = g.sb("b4", [1, NG * D])
    g.lnw = g.sb("lnw", [P, 2, D])
    g.label = g.sb("label", [P, NK])


def load_and_constants(g):
    nc, a = g.nc, g.a
    ld = g.sem("inputs_loaded")
    pc, vc, tc = g.sem("prep_pool"), g.sem("prep_vector"), g.sem("prep_tensor")
    pool_n, v_n, t_n = Count(pc), Count(vc), Count(tc)

    with ExitStack() as ctx:
        sb = lambda n, s, d=F32: g.sb(n, s, d, ctx)
        wd = sb("wd", [D, 2, D]); acol = sb("acol", [D, 3]); bd = sb("bd", [D, H])
        abd = sb("abd", [D, 3, H]); we = sb("we", [D, HF]); wea = sb("wea", [D, H, HF])
        wvb = sb("wvb", [P, H, HF]); wacol = sb("wacol", [D, 1])
        ws2 = sb("ws2", [D, D]); wg2 = sb("wg2", [D, 2, D])
        att3 = sb("att3", [128, R * D]); t3 = sb("t3", [128, R * D]); u3 = sb("u3", [128, 2 * R])
        ws3 = sb("ws3", [128, D]); wsum = sb("wsum", [128, D])
        brow = sb("brow", [1, (R + 1) * D]); bsum = sb("bsum", [1, D])
        lab_i = sb("lab_i", [P, NK], I32)
        ea = sb("ea", [P, EJ, 16]); ea3 = sb("ea3", [P, EJ, 3]); tmp = sb("tmp", [P, EJ, 16])
        si = sb("si", [P, EJ], I32); di = sb("di", [P, EJ], I32); ti = sb("ti", [P, EJ], I32)
        hl = sb("hl", [P, 4, EJ], I32); iot = sb("iot", [P, LO], I32)
        shift = sb("shift", [D, 128])
        ps = g.ps("prep_ps", [128, 512], F32, ctx)
        ps2 = g.ps("prep_ps2", [128, 512], F32, ctx)
        ps3 = g.ps("prep_ps3", [128, 512], F32, ctx)
        L = [0]
        PREP = 9

        with nc.Block() as block:
            @block.sync
            def _(sp):
                def load(dst, src, short=False):
                    L[0] += 16
                    sp.dma_start(dst, src, allow_slow_non_contiguous=short).then_inc(ld, 16)
                row = lambda ap: ap.rearrange("(a n) -> a n", a=1)
                col = lambda ap: ap.rearrange("(n a) -> n a", a=1)
                load(si[:, :], a["src"].rearrange("(p j) -> p j", p=P))
                load(di[:, :], a["dst"].rearrange("(p j) -> p j", p=P))
                load(ti[:, :], a["edge_type_8"].rearrange("(p j) -> p j", p=P))
                load(ea[:, :, :], a["edge_attr_16"].rearrange("(p j) d -> p j d", p=P))
                load(ea3[:, :, :], a["edge_attr_3"].rearrange("(p j) d -> p j d", p=P))
                load(lab_i[:, :], a["node_type_2"].rearrange("(p k) -> p k", p=P))
                w2d = a["L0_gnn_W"].rearrange("h f i -> (h f) i")
                for b in range(2):
                    load(wd[:, b, :], w2d)
                for h in range(H):
                    load(acol[h * HF:(h + 1) * HF, :], a["L0_gnn_a"][h, :].rearrange("(s f) -> f s", f=HF), True)
                load(we[:, :], a["L0_gnn_W_edge"].rearrange("h f i -> (h f) i"))
                for b, n in enumerate(("L0_gnn_ln_scale", "L0_gnn_ln_bias")):
                    load(g.lnw[:, b, :], row(a[n]).broadcast_to([P, D]))
                load(g.w1a[:, :], a["L1_gnn_We1"][0:2 * D, :])
                load(g.w1r[:, :], a["L1_gnn_We1"][2 * D:2 * D + 1, :].broadcast_to([P, D]))
                load(g.be1[:, :], col(a["L1_gnn_be1"]))
                load(g.w2[:, :], a["L1_gnn_We2"])
                load(g.be2[:, :], col(a["L1_gnn_be2"]))
                load(wacol[:, :], a["L1_gnn_Wa"])
                load(g.ba[:, :], row(a["L1_gnn_ba"]).broadcast_to([D, 1]))
                load(g.wn1[:, :], a["L1_gnn_Wn1"])
                load(g.bn1[:, :], col(a["L1_gnn_bn1"]))
                load(g.wn2[0:D, :], a["L1_gnn_Wn2"])
                load(g.wn2[D:D + 1, :], row(a["L1_gnn_bn2"]))
                load(ws2[:, :], a["L2_gnn_W_self"])
                load(wg2[:, :, :], a["L2_gnn_W_groups"].rearrange("g o i -> o g i"))
                w3v = a["L3_gnn_W"].rearrange("r d f -> d r f")
                for b in range(2):
                    load(g.w3[b * D:(b + 1) * D, :].rearrange("p (r f) -> p r f", r=R), w3v)
                    load(ws3[b * D:(b + 1) * D, :], a["L3_gnn_W_self"])
                load(att3[0:D, :], a["L3_gnn_att_src"].rearrange("r f -> (r f)").rearrange("(a n) -> a n", a=1).broadcast_to([D, R * D]))
                load(att3[D:128, :], a["L3_gnn_att_dst"].rearrange("r f -> (r f)").rearrange("(a n) -> a n", a=1).broadcast_to([D, R * D]))
                load(brow[:, 0:D], row(a["L3_gnn_b_self"]))
                load(brow[:, D:], a["L3_gnn_bias"].rearrange("r f -> (r f)").rearrange("(a n) -> a n", a=1))

            @block.gpsimd
            def _(pool):
                pool_n.up(pool.memset(g.ones[:, :], 1.0))
                pool_n.up(pool.memset(g.ident[:, :], 0.0))
                pool_n.up(pool.memset(bd[:, :], 1.0))
                pool_n.up(pool.memset(shift[:, :], 0.0))
                pool_n.up(pool.iota(iot[:, :], pattern=[[1, LO]], base=0, channel_multiplier=0))
                pool_n.here(pool)
                pool_n.up(pool.affine_select(out=g.ident[:, :], in_=g.ident[:, :], compare_op=ALU.not_equal,
                                             fill=1.0, base=0, pattern=[[-1, 128]], channel_multiplier=1))
                pool_n.up(pool.affine_select(out=shift[:, :], in_=shift[:, :], compare_op=ALU.not_equal,
                                             fill=1.0, base=D, pattern=[[-1, 128]], channel_multiplier=1))
                pool_n.up(pool.affine_select(out=bd[:, :], in_=bd[:, :], compare_op=ALU.is_ge, fill=0.0, base=0,
                                             pattern=[[-HF, H]], channel_multiplier=1))
                pool_n.here(pool)
                pool_n.up(pool.affine_select(out=bd[:, :], in_=bd[:, :], compare_op=ALU.is_ge, fill=0.0,
                                             base=HF - 1, pattern=[[HF, H]], channel_multiplier=-1))

            steps = {}

            @block.vector
            def _(v):
                def up(ins):
                    v_n.up(ins)
                v.wait_ge(pc, PREP)
                v.wait_ge(ld, L[0])
                up(v.tensor_copy(g.identb[:, :], g.ident[:, :]))
                for k in range(3):
                    up(v.tensor_scalar(abd[:, k, :], bd[:, :], acol[:, k:k + 1], None, ALU.mult))
                v_n.here(v)
                up(v.tensor_tensor(wea[:, :, :], we[:, :].unsqueeze(1).broadcast_to([D, H, HF]),
                                   abd[:, 2, :].unsqueeze(2).broadcast_to([D, H, HF]), ALU.mult))
                up(v.tensor_copy(g.wa[:, :], wacol[:, 0:1].broadcast_to([D, D])))
                up(v.tensor_tensor(t3[:, :], g.w3[:, :], att3[:, :], ALU.mult))
                v_n.here(v)
                up(v.tensor_reduce(u3[:, 0:R], t3[:, :].rearrange("p (r f) -> p r f", r=R), AX.X, ALU.add))
                v_n.here(v)
                steps["small"] = v_n.n
                up(v.tensor_copy(g.rec[:, :, SRC], si[:, :]))
                up(v.tensor_copy(g.rec[:, :, DST], di[:, :]))
                up(v.tensor_copy(g.rec[:, :, TYPE], ti[:, :]))
                up(v.tensor_copy(g.label[:, :], lab_i[:, :]))
                up(v.tensor_tensor(ea3[:, :, :], ea3[:, :, :], ea3[:, :, :], ALU.mult))
                v_n.here(v)
                up(v.tensor_reduce(g.rec[:, :, RADIAL], ea3[:, :, :], AX.X, ALU.add))
                for s, idx in enumerate((di, si)):
                    up(v.tensor_scalar(hl[:, 2 * s, :], idx[:, :], 8, None, ALU.logical_shift_right))
                    up(v.tensor_scalar(hl[:, 2 * s + 1, :], idx[:, :], LO - 1, None, ALU.bitwise_and))
                up(v.memset(g.keys[:, :, EJ:], 0.0))
                up(v.tensor_copy(g.iota[:, :], iot[:, :]))
                up(v.tensor_copy(g.iotaf[:, :], iot[0:P, 0:R]))
                v_n.here(v)
                up(v.tensor_copy(g.keys[:, :, 0:EJ], hl[:, :, :]))
                v.wait_ge(tc, 3)
                up(v.tensor_copy(g.w0[0:D, 0:D], ps[0:D, 0:D]))
                up(v.tensor_scalar(g.w0[D:128, 0:D], ps[D:128, 0:D], -1.0, None, ALU.mult))
                up(v.tensor_copy(g.w0[0:D, D:D + H], ps2[0:D, 0:H]))
                up(v.tensor_copy(g.w0[D:128, D:D + H], ps2[D:128, H:2 * H]))
                up(v.memset(g.w0[0:D, D + H:], 0.0))
                up(v.tensor_copy(g.w0[D:128, D + H:], ps2[D:128, 0:H]))
                up(v.tensor_copy(wvb[:, :, :], ps3[0:P, 0:D].rearrange("p (h k) -> p h k", h=H)))
                up(v.tensor_copy(g.n1[0:D, :], ps[0:D, 0:D]))
                for m in (g.n1, g.n3, g.n4):
                    up(v.tensor_copy(m[D:128, :], g.ident[D:128, D:128]))
                v_n.here(v)
                up(v.tensor_tensor(g.w0[D:128, D + H:], g.w0[D:128, D + H:], g.w0[D:128, D:D + H], ALU.add))
                steps["ps_free"] = v_n.n
                for h in range(H):
                    up(v.tensor_tensor(tmp[:, :, :], ea[:, :, :],
                                       wvb[:, h, :].unsqueeze(1).broadcast_to([P, EJ, 16]), ALU.mult))
                    v_n.here(v)
                    up(v.tensor_reduce(g.rec[:, :, ATT + h], tmp[:, :, :], AX.X, ALU.add))
                    v_n.here(v)
                v.wait_ge(tc, 6)
                up(v.tensor_copy(g.wg[:, :], ps2[:, 0:D]))
                up(v.tensor_tensor(g.n3[0:D, :], ps[0:D, 0:D], g.ident[0:D, 0:D], ALU.add))
                up(v.tensor_copy(g.w3s[0:D, 0:R], u3[0:D, 0:R]))
                up(v.memset(g.w3s[0:D, R:], 0.0))
                up(v.tensor_copy(g.w3s[D:128, 0:R], u3[D:128, 0:R]))
                up(v.tensor_tensor(g.w3s[D:128, R:], ps3[D:128, 0:R], u3[D:128, 0:R], ALU.add))
                up(v.tensor_reduce(wsum[0:D, :], g.w3[0:D, :].rearrange("p (r f) -> p f r", r=R), AX.X, ALU.add))
                up(v.tensor_reduce(bsum[:, :], brow[:, :].rearrange("p (r f) -> p f r", r=R + 1), AX.X, ALU.add))
                v_n.here(v)
                up(v.tensor_scalar(g.w3[D:128, :], g.w3[D:128, :], -1.0, None, ALU.mult))
                up(v.tensor_tensor(wsum[0:D, :], wsum[0:D, :], ws3[0:D, :], ALU.add))
                up(v.tensor_copy(g.b4[:, :].rearrange("p (k d) -> p k d", k=NG),
                                 bsum[:, :].unsqueeze(1).broadcast_to([1, NG, D])))
                v_n.here(v)
                up(v.tensor_tensor(g.n4[0:D, :], wsum[0:D, :], g.ident[0:D, 0:D], ALU.add))

            @block.tensor
            def _(t):
                t.wait_ge(pc, PREP)
                t.wait_ge(ld, L[0])
                t.wait_ge(vc, steps["small"])
                t_n.up(t.transpose(ps[:, 0:D], wd[:, :, :].rearrange("p b i -> p (b i)"), g.ident[0:D, 0:D]))
                t_n.up(t.matmul(ps2[:, 0:2 * H], wd[:, :, :].rearrange("p b i -> p (b i)"),
                                abd[:, 0:2, :].rearrange("p k h -> p (k h)"), start=True, stop=True))
                t_n.up(t.matmul(ps3[0:P, 0:D], g.ones[0:D, 0:P], wea[:, :, :].rearrange("p h k -> p (h k)"),
                                start=True, stop=True))
                t.wait_ge(vc, steps["ps_free"])
                t_n.up(t.transpose(ps2[:, 0:D], wg2[:, :, :].rearrange("p g i -> p (g i)"), g.ident[0:D, 0:D]))
                t_n.up(t.transpose(ps[0:D, 0:D], ws2[:, :], g.ident[0:D, 0:D]))
                t_n.up(t.matmul(ps3[:, 0:R], shift[:, :], u3[0:D, 0:R], start=True, stop=True))


def histogram(g):
    sem = g.sem
    onehot, used, filled, zeroed = sem("hist_onehot"), sem("hist_used"), sem("hist_filled"), sem("hist_zeros")
    vc, tc = sem("base_vector"), sem("base_tensor")
    with ExitStack() as ctx:
        hi = [g.sb(f"h_hi{b}", [P, 2, 2 * HB], BF16, ctx) for b in range(2)]
        lo = [g.sb(f"h_lo{b}", [P, 2, LO], BF16, ctx) for b in range(2)]
        zero = g.sb("h_zero", [P, 512], BF16, ctx)
        incl = g.sb("incl", [HB, 2, 2, LO], F32, ctx)
        total = g.sb("row_total", [HB, 2, 2], F32, ctx)
        prev = g.sb("row_prev", [HB, 2, 2], F32, ctx)
        before = g.sb("before", [HB, HB], F32, ctx)
        cnt = [g.ps(f"count{s}", [HB, 512], F32, ctx) for s in range(2)]
        rows = g.ps("rows", [HB, 4], F32, ctx)
        with g.nc.Block() as block:
            @block.vector
            def _(v):
                v.memset(zero[:, :], 0.0).then_inc(zeroed, 1)
                v.sem_inc(used, 2)
                with v.Fori(0, EJ // 2) as i:
                    for b in range(2):
                        j = i * 2 + b
                        v.wait_ge(used, j + 1)
                        for s in range(2):
                            v.tensor_scalar(hi[b][:, s, :], g.iota[:, 0:2 * HB],
                                            g.keys[:, 2 * s, bass.ds(j, 1)], None, ALU.is_equal)
                            last = v.tensor_scalar(lo[b][:, s, :], g.iota[:, :],
                                                   g.keys[:, 2 * s + 1, bass.ds(j, 1)], None, ALU.is_equal)
                        last.then_inc(onehot, 1)
                n = Count(vc)
                n.up(v.memset(prev[:, :, :], 0.0))
                v.wait_ge(filled, 1)
                n.here(v)
                for s in range(2):
                    for h in range(2):
                        n.up(v.tensor_tensor_scan(incl[:, s, h, :], g.ones[0:HB, 0:1].broadcast_to([HB, LO]),
                                                  cnt[s][:, h * LO:(h + 1) * LO], 0.0, ALU.mult, ALU.add))
                n.here(v)
                n.up(v.tensor_copy(total[:, :, :], incl[:, :, :, LO - 1]))
                n.here(v)
                n.up(v.tensor_copy(prev[:, :, 1], total[:, :, 0]))
                v.wait_ge(tc, 1)
                for s in range(2):
                    n.up(v.tensor_tensor(g.base[:, s, :], incl[:, s, :, :].rearrange("p h l -> p (h l)"),
                                         cnt[s][:, :], ALU.subtract))
                n.here(v)
                for s in range(2):
                    for h in range(2):
                        k = 2 * s + h
                        n.up(v.tensor_scalar(g.base[:, s, h * LO:(h + 1) * LO],
                                             g.base[:, s, h * LO:(h + 1) * LO], rows[:, k:k + 1], None, ALU.add))

            @block.gpsimd
            def _(pool):
                n = Count(g.sem("before_mask"))
                n.up(pool.memset(before[:, :], 1.0))
                n.here(pool)
                n.up(pool.affine_select(out=before[:, :], in_=before[:, :], compare_op=ALU.is_gt, fill=0.0,
                                        base=0, pattern=[[1, HB]], channel_multiplier=-1))
                g.before_sem = n.sem
                n.up(pool.memset(g.strict[:, :], 1.0))
                n.here(pool)
                n.up(pool.affine_select(out=g.strict[:, :], in_=g.strict[:, :], compare_op=ALU.is_gt, fill=0.0,
                                        base=0, pattern=[[1, P]], channel_multiplier=-1))

            @block.tensor
            def _(t):
                t.wait_ge(zeroed, 1)
                for s in range(2):
                    t.matmul(cnt[s][:, :], zero[:, 0:HB], zero[:, :], start=True, stop=False,
                             skip_group_check=True)
                with t.Fori(0, EJ // 2) as i:
                    for b in range(2):
                        t.wait_ge(onehot, i * 2 + b + 1)
                        for s in range(2):
                            for h in range(2):
                                last = t.matmul(cnt[s][:, h * LO:(h + 1) * LO], hi[b][:, s, h * HB:(h + 1) * HB],
                                                lo[b][:, s, :], start=False, stop=False, skip_group_check=True)
                        last.then_inc(used, 1)
                for s in range(2):
                    last = t.matmul(cnt[s][:, :], zero[:, 0:HB], zero[:, :], start=False, stop=True,
                                    skip_group_check=True)
                last.then_inc(filled, 1)
                t.wait_ge(g.before_sem, 2)
                t.wait_ge(vc, 7)
                t.matmul(rows[:, :], before[:, :], total[:, :, :].rearrange("p s h -> p (s h)"),
                         start=True, stop=False)
                t.matmul(rows[:, :], g.ones[0:HB, 0:HB], prev[:, :, :].rearrange("p s h -> p (s h)"),
                         start=False, stop=True).then_inc(tc, 1)


def rank_and_scatter(g):
    sem = g.sem
    onehot, counted = sem("rank_onehot"), sem("rank_counted")
    turned, turned_out = [sem(f"rank_turned{s}") for s in range(2)], [sem(f"rank_turned_out{s}") for s in range(2)]
    same, masked = [sem(f"rank_same{s}") for s in range(2)], [sem(f"rank_masked{s}") for s in range(2)]
    table_up, table_out = [sem(f"table_up{s}") for s in range(2)], [sem(f"table_out{s}") for s in range(2)]
    looked, placed = [sem(f"rank_looked{s}") for s in range(2)], sem("rank_placed")
    summed = sem("rank_summed")
    staged, sent = sem("rank_staged"), [g.once(f"rank_sent{b}") for b in range(2)]
    x_in, x_out, zeroed = [sem(f"x_in{b}") for b in range(2)], [sem(f"x_out{b}") for b in range(2)], sem("cp_zero")
    RC = 4
    with ExitStack() as ctx:
        hi = [g.sb(f"r_hi{b}", [P, 2, 2 * HB], BF16, ctx) for b in range(2)]
        lo = [g.sb(f"r_lo{b}", [P, 2, LO], BF16, ctx) for b in range(2)]
        hit = [g.sb(f"hi_t{s}", [HB, 2, P], F32, ctx) for s in range(2)]
        hitb = [g.sb(f"hi_tb{s}", [HB, 2, P], BF16, ctx) for s in range(2)]
        tab = [g.sb(f"tab_sb{s}", [HB, 512], F32, ctx) for s in range(2)]
        eq = [g.sb(f"eq{s}", [P, P], BF16, ctx) for s in range(2)]
        junk = g.sb("rank_junk", [P, LO], F32, ctx)
        one = g.sb("one_place", [P, 2], F32, ctx)
        place = g.sb("place", [P, 2, EJ], F32, ctx)
        pidx = [g.sb(f"pidx{b}", [P, 2, RC], I32, ctx) for b in range(2)]
        stage = [g.sb(f"rstage{b}", [P, RC, REC], F32, ctx) for b in range(2)]
        cp = [g.sb(f"cp{b}", [P, 8, 2, D], F32, ctx) for b in range(2)]
        t_ps = [g.ps(f"hit_ps{s}", [HB, 2, 128], BF16, ctx) for s in range(2)]
        e_ps = [g.ps(f"eq_ps{s}", [P, P], F32, ctx) for s in range(2)]
        l_ps = [g.ps(f"look_ps{s}", [P, LO], F32, ctx) for s in range(2)]
        tab_ps = [g.ps(f"tab_ps{s}", [HB, 512], F32, ctx) for s in range(2)]
        xin = g.a["x"].rearrange("(p k) d -> p k d", p=P)
        t0 = g.tab[0].rearrange("(p k t) d -> p k t d", p=P, t=2)
        with g.nc.Block() as block:
            @block.vector
            def _(v):
                n = Count(zeroed)
                n.up(v.memset(cp[0][:, :, 1, :], 0.0))
                n.up(v.memset(cp[1][:, :, 1, :], 0.0))
                v.sem_inc(counted, 2)
                with v.Fori(0, EJ // 2) as i:
                    for b in range(2):
                        j = i * 2 + b
                        v.wait_ge(counted, j + 1)
                        for s in range(2):
                            v.tensor_scalar(hi[b][:, s, :], g.iota[:, 0:2 * HB],
                                            g.keys[:, 2 * s, bass.ds(j, 1)], None, ALU.is_equal)
                            v.tensor_scalar(lo[b][:, s, :], g.iota[:, :],
                                            g.keys[:, 2 * s + 1, bass.ds(j, 1)], None, ALU.is_equal
                                            ).then_inc(onehot, 1)
                        for s in range(2):
                            v.wait_ge(same[s], j + 1)
                            v.tensor_tensor(eq[s][:, :], e_ps[s][:, :], g.strict[:, :], ALU.mult
                                            ).then_inc(masked[s], 1)
                        for s in range(2):
                            v.wait_ge(looked[s], j + 1)
                            v.wait_ge(placed, j * 2 + s)
                            v.tensor_tensor_reduce(junk[:, :], l_ps[s][:, :], lo[b][:, s, :], 1.0, 0.0,
                                                   ALU.mult, ALU.add, one[:, s:s + 1]).then_inc(summed, 1)
                            v.wait_ge(summed, j * 2 + s + 1)
                            v.tensor_copy(place[:, s, bass.ds(j, 1)], one[:, s:s + 1]).then_inc(placed, 1)

            @block.tensor
            def _(t):
                for s in range(2):
                    t.matmul(tab_ps[s][:, :], g.ident[0:HB, 0:HB], g.base[:, s, :], start=True, stop=False,
                             skip_group_check=True).then_inc(table_up[s], 1)
                with t.Fori(0, EJ // 2) as i:
                    for b in range(2):
                        j = i * 2 + b
                        for s in range(2):
                            t.wait_ge(onehot, j * 2 + s + 1)
                            t.transpose(t_ps[s][:, 0, 0:P], hi[b][:, s, 0:HB], g.identb[0:P, 0:P])
                            t.transpose(t_ps[s][:, 1, 0:P], hi[b][:, s, HB:2 * HB], g.identb[0:P, 0:P]
                                        ).then_inc(turned[s], 1)
                        for s in range(2):
                            t.wait_ge(turned_out[s], j * 2 + 2)
                            t.matmul(e_ps[s][:, :], hitb[s][:, 0, :], hitb[s][:, 0, :], start=True, stop=False)
                            t.matmul(e_ps[s][:, :], hitb[s][:, 1, :], hitb[s][:, 1, :], start=False, stop=True
                                     ).then_inc(same[s], 1)
                        for s in range(2):
                            t.wait_ge(table_out[s], j + 1)
                            t.wait_ge(placed, j * 2)
                            t.matmul(l_ps[s][:, :], hit[s][:, 0, :], tab[s][:, 0:LO], start=True, stop=False)
                            t.matmul(l_ps[s][:, :], hit[s][:, 1, :], tab[s][:, LO:], start=False, stop=False)
                            for h in range(2):
                                last = t.matmul(tab_ps[s][:, h * LO:(h + 1) * LO],
                                                hi[b][:, s, h * HB:(h + 1) * HB], lo[b][:, s, :],
                                                start=False, stop=False, skip_group_check=True)
                            last.then_inc(table_up[s], 1)
                        for s in range(2):
                            t.wait_ge(masked[s], j + 1)
                            last = t.matmul(l_ps[s][:, :], eq[s][:, :], lo[b][:, s, :], start=False, stop=True)
                            last.then_inc(looked[s], 1)
                        t.wait_ge(placed, j * 2 + 2)
                        t.sem_inc(counted, 1)

            @block.scalar
            def _(a):
                with a.Fori(0, EJ) as j:
                    for s in range(2):
                        a.wait_ge(turned[s], j + 1)
                        a.wait_ge(table_up[s], j + 1)
                        a.activation(hit[s][:, :, :], t_ps[s][:, :, 0:P], ACT.Copy).then_inc(turned_out[s], 1)
                        a.activation(hitb[s][:, :, :], t_ps[s][:, :, 0:P], ACT.Copy).then_inc(turned_out[s], 1)
                    for s in range(2):
                        a.activation(tab[s][:, :], tab_ps[s][:, :], ACT.Copy).then_inc(table_out[s], 1)

            @block.gpsimd
            def _(pool):
                n = LoopCount(staged, 6, g=g)
                with pool.Fori(0, EJ // (2 * RC)) as i:
                    for b in range(2):
                        c = i * 2 + b
                        pool.wait_ge(placed, c * (2 * RC) + 2 * RC)
                        g.passed(pool)
                        pool.wait_ge(sent[b], i * (32 * RC))
                        g.passed(pool)
                        for s in range(2):
                            n.up(pool.tensor_copy(pidx[b][:, s, :], place[:, s, bass.ds(c * RC, RC)]))
                        n.up(pool.tensor_copy(stage[b][:, :, :], g.rec[:, bass.ds(c * RC, RC), :]))
                        n.here(pool, i)
                        for s in range(2):
                            for k in range(RC):
                                pool.indirect_dma_start(
                                    out=g.sorted[s][:, :],
                                    out_offset=bass.IndirectOffsetOnAxis(ap=pidx[b][:, s, k:k + 1], axis=0),
                                    in_=stage[b][:, k, :], in_offset=None,
                                    bounds_check=E - 1, oob_is_err=False).then_inc(sent[b], 16)
                for b in range(2):
                    pool.wait_ge(sent[b], EJ * 16)

            @block.sync
            def _(sp):
                sp.wait_ge(zeroed, 2)
                with sp.Fori(0, NK // 16) as i:
                    for b in range(2):
                        k = i * 16 + 8 * b
                        sp.wait_ge(x_out[b], i * 16)
                        sp.dma_start(cp[b][:, :, 0, :], xin[:, bass.ds(k, 8), :]).then_inc(x_in[b], 16)
                    for b in range(2):
                        k = i * 16 + 8 * b
                        sp.wait_ge(x_in[b], i * 16 + 16)
                        sp.dma_start(t0[:, bass.ds(k, 8), :, :], cp[b][:, :, :, :]).then_inc(x_out[b], 16)
                for b in range(2):
                    sp.wait_ge(x_out[b], NK // 16 * 16)


def read_orders(g):
    ld, pc, vc = g.sem("orders_loaded"), g.sem("orders_pool"), g.sem("orders_vector")
    with ExitStack() as ctx:
        nxt = [g.sb(f"next{s}", [P, 1], F32, ctx) for s in range(2)]
        prv = [g.sb(f"prev{s}", [P, 1], F32, ctx) for s in range(2)]
        rec = [g.sb(f"sorted_rec{s}", [P, EJ, REC], F32, ctx) for s in range(2)]
        same = g.sb("same_next", [P, EJ], F32, ctx)
        rowf = g.sb("rowf", [P, EJ], F32, ctx)
        with g.nc.Block() as block:
            @block.gpsimd
            def _(pool):
                for s in range(2):
                    pool.memset(nxt[s][:, :], -1.0).then_inc(pc, 1)
                    pool.memset(prv[s][:, :], -1.0).then_inc(pc, 1)

            @block.sync
            def _(sp):
                sp.wait_ge(pc, 4)
                for s, f in ((0, DST), (1, SRC)):
                    flat = g.sorted[s].rearrange("(p j) r -> p j r", p=P)
                    sp.dma_start(rec[s][:, :, :], flat).then_inc(ld, 16)
                    sp.dma_start(prv[s][1:P, :], flat[0:P - 1, EJ - 1, f:f + 1],
                                 allow_slow_non_contiguous=True).then_inc(ld, 16)
                    sp.dma_start(nxt[s][0:P - 1, :], flat[1:P, 0, f:f + 1],
                                 allow_slow_non_contiguous=True).then_inc(ld, 16)

            @block.vector
            def _(v):
                n = Count(vc)
                v.wait_ge(ld, 96)
                for s, f in ((0, DST), (1, SRC)):
                    key = rec[s][:, :, f]
                    for k, e in ((0, SRC), (1, DST)):
                        n.up(v.tensor_copy(g.row1[s][:, k, :], rec[s][:, :, e]))
                        n.up(v.tensor_scalar(g.row2[s][:, k, :], rec[s][:, :, e], 2.0, None, ALU.mult))
                    n.up(v.tensor_tensor(g.cont[s][:, 1:], key[:, 1:], key[:, 0:EJ - 1], ALU.is_equal))
                    n.up(v.tensor_tensor(g.cont[s][:, 0:1], key[:, 0:1], prv[s][:, :], ALU.is_equal))
                    n.here(v)
                    n.up(v.tensor_tensor(same[:, 0:EJ - 1], key[:, 0:EJ - 1], key[:, 1:], ALU.is_equal))
                    n.up(v.tensor_tensor(same[:, EJ - 1:], key[:, EJ - 1:], nxt[s][:, :], ALU.is_equal))
                    n.up(v.tensor_scalar(rowf[:, :], key, 2.0, 1.0, ALU.mult, ALU.add))
                    n.here(v)
                    n.up(v.scalar_tensor_tensor(rowf[:, :], same[:, :], SKIP, rowf[:, :], ALU.mult, ALU.add))
                    if s == 0:
                        n.up(v.tensor_copy(g.goes_on[:, :], same[:, :]))
                    n.here(v)
                    n.up(v.tensor_copy(g.out_row[s][:, :], rowf[:, :]))
                    n.up(v.tensor_tensor_scan(g.open[s][:, :], g.cont[s][:, :], g.ones[0:P, 0:1].broadcast_to([P, EJ]),
                                              1.0, ALU.mult, ALU.mult))
                    n.here(v)
                n.up(v.tensor_copy(g.etype[:, :], rec[0][:, :, TYPE]))
                n.up(v.tensor_copy(g.radial[:, :], rec[1][:, :, RADIAL]))
                n.up(v.tensor_copy(g.attn[:, :, :], rec[0][:, :, ATT:ATT + H].rearrange("p j h -> p h j")))
                n.here(v)


def gather(pool, g, name, rows, table, i, b, c, idx, dst, free, ready, n, sides, width=D):
    pool.wait_ge(free, c + 1)
    g.passed(pool)
    for k in range(sides):
        n.up(pool.tensor_copy(idx[:, k, :], rows[:, k, bass.ds(c * G, G)]))
    n.here(pool, i)
    for t in range(G):
        for k in range(sides):
            pool.indirect_dma_start(out=dst[:, t, k * width:(k + 1) * width], out_offset=None, in_=table,
                                    in_offset=bass.IndirectOffsetOnAxis(ap=idx[:, k, t:t + 1], axis=0),
                                    bounds_check=2 * N - 1 if table is not g.x_rows else N - 1,
                                    oob_is_err=False).then_inc(ready[b], 16)


def edges(g, layer):
    sem = lambda n: g.sem(f"{n}_e")
    row_free, row_ready, copied = sem("rows_free"), [g.once(f"rows_ready{b}_e{layer}") for b in range(2)], sem("idx_copied")
    turned, turned_out, turned_free = sem("turned"), sem("turned_out"), sem("turned_free")
    made, made_free = sem("made"), sem("made_free")
    order = 1 if layer == 1 else 0
    sides = 1 if layer == 2 else 2
    with ExitStack() as ctx:
        sb = lambda n, s, d=F32: g.sb(f"{n}_e{layer}", s, d, ctx)
        ps = lambda n, s, d=F32: g.ps(f"{n}_e{layer}", s, d, ctx)
        idx = [sb(f"idx{b}", [P, 2, G], I32) for b in range(2)]
        rows = [sb(f"rows{b}", [P, G, 2 * D]) for b in range(2)]
        xt = [sb(f"xt{b}", [128, G * P]) for b in range(2)]
        tp = [ps(f"tp{b}", [128, G * P]) for b in range(2)]
        src_rows = (g.row1 if layer == 0 else g.row2)[order]
        table = {0: g.x_rows, 1: g.tab[1], 3: g.tab[3]}.get(layer)
        if layer == 0:
            W = D + 2 * H
            out = [ps(f"out{b}", [P, G, W]) for b in range(2)]
        if layer == 1:
            out = [ps(f"out{b}", [P, G, D]) for b in range(2)]
            h_ps = [ps(f"h{k}", [D, G * P]) for k in range(3)]
            s_sb = [sb(f"s{k}", [D, G * P]) for k in range(3)]
            msg = sb("msg", [D, G * P])
            diag = [sb(f"diag{b}", [P, G, P]) for b in range(2)]
            hidden, hidden_out, diag_ready, msg_ready = sem("hidden"), sem("hidden_out"), sem("diag"), sem("msg")
        if layer == 2:
            lrow = [sb(f"lrow{b}", [P, G, g.LW]) for b in range(2)]
            pick = sb("pick", [P, 2, G])
            out = [ps(f"out{b}", [P, G, D]) for b in range(2)]
            masked, picked = sem("masked"), sem("picked")
        if layer == 3:
            hr = [ps(f"hr{b}", [P, R * D]) for b in range(2)]
            sc = [ps(f"sc{b}", [P, G, 2 * R]) for b in range(2)]
            prod = [sb(f"prod{b}", [P, R * D]) for b in range(2)]
            pick = [sb(f"pick{b}", [P, G, R]) for b in range(2)]
            psc = sb("psc", [P, 2, G, R])
            hr_ready, hr_free, step = sem("hr_ready"), sem("hr_free"), sem("select_steps")

        with g.nc.Block() as block:
            @block.gpsimd
            def _(pool):
                n = LoopCount(copied, 2 * sides, g=g)
                with pool.Fori(0, CH // 2) as i:
                    for b in range(2):
                        gather(pool, g, layer, src_rows if layer != 2 else g.row1[0],
                               table if layer != 2 else g.labelled[:, :], i, b, i * 2 + b,
                               idx[b], rows[b] if layer != 2 else lrow[b], row_free, row_ready, n, sides,
                               D if layer != 2 else g.LW)

            @block.tensor
            def _(t):
                if layer != 2:
                    t.sem_inc(row_free, 2)
                t.sem_inc(turned_free, 2)
                with t.Fori(0, CH // 2) as i:
                    for b in range(2):
                        c = i * 2 + b
                        if layer == 2:
                            t.wait_ge(masked, c + 1)
                        else:
                            t.wait_ge(row_ready[b], i * (32 * G) + 32 * G)
                        for k in range(G):
                            last = t.transpose(tp[b][:, k * P:(k + 1) * P], rows[b][:, k, :], g.ident[0:P, 0:P])
                        last.then_inc(turned, 1)
                        if layer != 2:
                            t.wait_ge(turned, c + 1)
                            t.sem_inc(row_free, 1)
                        t.wait_ge(turned_out, c + 1)
                        if layer == 0:
                            t.wait_ge(made_free, c + 1)
                            for k in range(G):
                                last = t.matmul(out[b][:, k, :], xt[b][:, k * P:(k + 1) * P], g.w0[:, :],
                                                start=True, stop=True)
                            last.then_inc(made, 1)
                            t.wait_ge(made, c + 1)
                            t.sem_inc(turned_free, 1)
                        if layer == 1:
                            t.wait_ge(diag_ready, c + 1)
                            t.matmul(h_ps[0][:, :], g.w1a[:, :], xt[b][:, :], start=True, stop=False)
                            t.matmul(h_ps[0][:, :], g.w1r[:, :], diag[b][:, :, :].rearrange("p k e -> p (k e)"),
                                     start=False, stop=True).then_inc(hidden, 1)
                            t.wait_ge(hidden, c * 3 + 1)
                            t.sem_inc(turned_free, 1)
                            for k, w in ((1, g.w2), (2, g.wa)):
                                t.wait_ge(hidden_out, c * 3 + k)
                                g.passed(t)
                                t.matmul(h_ps[k][:, :], w[:, :], s_sb[k - 1][:, :], start=True, stop=True
                                         ).then_inc(hidden, 1)
                            t.wait_ge(msg_ready, c + 1)
                            t.wait_ge(made_free, c + 1)
                            g.passed(t)
                            for k in range(G):
                                last = t.transpose(out[b][:, k, :], msg[:, k * P:(k + 1) * P], g.ident[0:D, 0:D])
                            last.then_inc(made, 1)
                        if layer == 2:
                            t.wait_ge(made_free, c + 1)
                            for k in range(G):
                                last = t.matmul(out[b][:, k, :], xt[b][:, k * P:(k + 1) * P], g.wg[:, :],
                                                start=True, stop=True)
                            last.then_inc(made, 1)
                            t.wait_ge(made, c + 1)
                            t.sem_inc(turned_free, 1)
                        if layer == 3:
                            t.wait_ge(made_free, c + 1)
                            for k in range(G):
                                last = t.matmul(sc[b][:, k, :], xt[b][:, k * P:(k + 1) * P], g.w3s[:, :],
                                                start=True, stop=True)
                            last.then_inc(made, 1)
                            for k in range(G):
                                t.wait_ge(hr_free, c * G + k + 1)
                                t.matmul(hr[k % 2][:, :], xt[b][:, k * P:(k + 1) * P], g.w3[:, :],
                                         start=True, stop=True).then_inc(hr_ready, 1)
                            t.wait_ge(hr_ready, c * G + G)
                            t.sem_inc(turned_free, 1)

            @block.scalar
            def _(a):
                with a.Fori(0, CH // 2) as i:
                    for b in range(2):
                        c = i * 2 + b
                        a.wait_ge(turned, c + 1)
                        a.wait_ge(turned_free, c + 1)
                        a.activation(xt[b][:, :], tp[b][:, :], ACT.Copy).then_inc(turned_out, 1)
                        if layer == 1:
                            for k, (bias, func) in enumerate(((g.be1, ACT.Silu), (g.be2, ACT.Silu), (g.ba, ACT.Sigmoid))):
                                a.wait_ge(hidden, c * 3 + k + 1)
                                if k > 0:
                                    a.wait_ge(msg_ready, c)
                                a.activation(s_sb[k][:, :], h_ps[k][:, :], func, bias=bias[:, 0:1]
                                             ).then_inc(hidden_out, 1)

            @block.vector
            def _(v):
                v.sem_inc(made_free, 2)
                if layer == 2:
                    v.sem_inc(row_free, 2)
                if layer == 3:
                    v.sem_inc(hr_free, 2)
                    n = LoopCount(step, 2 * (3 + 2 * G))
                if layer == 2:
                    n = LoopCount(picked, 4)
                with v.Fori(0, CH // 2) as i:
                    for b in range(2):
                        c = i * 2 + b
                        at = bass.ds(c * G, G)
                        if layer == 1:
                            v.tensor_tensor(diag[b][:, :, :], g.ident[0:P, 0:P].unsqueeze(1).broadcast_to([P, G, P]),
                                            g.radial[:, at].unsqueeze(2).broadcast_to([P, G, P]), ALU.mult
                                            ).then_inc(diag_ready, 1)
                            v.wait_ge(hidden_out, c * 3 + 3)
                            v.wait_ge(made, c)
                            v.tensor_tensor(msg[:, :], s_sb[1][:, :], s_sb[2][:, :], ALU.mult).then_inc(msg_ready, 1)
                        if layer == 2:
                            v.wait_ge(row_ready[b], i * (16 * G) + 16 * G)
                            v.wait_ge(turned, c)
                            for k in range(2):
                                n.up(v.tensor_scalar(pick[:, k, :], lrow[b][:, :, D], float(k), None, ALU.is_equal))
                            n.here(v, i)
                            for k in range(2):
                                last = v.tensor_tensor(rows[b][:, :, k * D:(k + 1) * D], lrow[b][:, :, 0:D],
                                                       pick[:, k, :].unsqueeze(2).broadcast_to([P, G, D]), ALU.mult)
                            last.then_inc(masked, 1)
                            v.wait_ge(masked, c + 1)
                            v.sem_inc(row_free, 1)
                        v.wait_ge(made, c + 1)
                        if layer == 0:
                            v.tensor_copy(g.val[:, at, :], out[b][:, :, 0:D])
                            v.tensor_copy(g.score[:, :, at], out[b][:, :, D:].rearrange("p j h -> p h j")
                                          ).then_inc(made_free, 1)
                        if layer in (1, 2):
                            v.tensor_copy(g.val[:, at, :], out[b][:, :, :]).then_inc(made_free, 1)
                        if layer == 3:
                            n.up(v.tensor_tensor(pick[b][:, :, :], g.iotaf[:, 0:R].unsqueeze(1).broadcast_to([P, G, R]),
                                                 g.etype[:, at].unsqueeze(2).broadcast_to([P, G, R]), ALU.is_equal))
                            n.here(v, i)
                            for k in range(2):
                                last = v.tensor_tensor(psc[:, k, :, :], sc[b][:, :, k * R:(k + 1) * R],
                                                       pick[b][:, :, :], ALU.mult)
                            n.up(last)
                            n.here(v, i)
                            v.sem_inc(made_free, 1)
                            n.up(v.tensor_reduce(g.score[:, 0:2, at], psc[:, :, :, :], AX.X, ALU.add))
                            for k in range(G):
                                v.wait_ge(hr_ready, c * G + k + 1)
                                n.up(v.tensor_tensor(prod[k % 2][:, :].rearrange("p (r f) -> p r f", r=R),
                                                     hr[k % 2][:, :].rearrange("p (r f) -> p r f", r=R),
                                                     pick[b][:, k, :].unsqueeze(2).broadcast_to([P, R, D]),
                                                     ALU.mult))
                                n.here(v, i)
                                v.sem_inc(hr_free, 1)
                                n.up(v.tensor_reduce(g.val[:, bass.ds(c * G + k, 1), :].rearrange("p a f -> p (a f)"),
                                                     prod[k % 2][:, :].rearrange("p (r f) -> p f r", r=R),
                                                     AX.X, ALU.add))
                                n.here(v, i)


def carry_on(eng, n, turned, g, k, A, B, C, out, a_sb, row, a_ps, b_ps, c_ps, op0, op1, init, back=False):
    n.here(eng)
    g.carries.append(n.n)
    eng.wait_ge(turned, 2 * k + 1)
    n.up(eng.tensor_copy(a_sb[0:C, :], a_ps[0:C, 0:P]))
    n.up(eng.memset(row[0:C, :], init))
    n.here(eng)
    if back:
        n.up(eng.tensor_tensor_scan(row[0:C, P - 1::-1], a_sb[0:C, P - 1::-1], b_ps[0:C, P - 1::-1],
                                    init, op0, op1))
    else:
        n.up(eng.tensor_tensor_scan(row[0:C, 1:P + 1], a_sb[0:C, :], b_ps[0:C, 0:P], init, op0, op1))
    g.carries.append(n.n)
    eng.wait_ge(turned, 2 * k + 2)
    n.up(eng.tensor_copy(out, c_ps[0:P, 0:C]))
    n.here(eng)


def turn_carries(t, g, vec, turned, sizes, A, B, row, a_ps, b_ps, c_ps):
    for k, (C, back) in enumerate(sizes):
        t.wait_ge(vec, g.carries[2 * k])
        t.transpose(a_ps[0:C, 0:P], A[:, 0:C], g.ident[0:P, 0:P])
        t.transpose(b_ps[0:C, 0:P], B[:, 0:C], g.ident[0:P, 0:P]).then_inc(turned, 1)
        t.wait_ge(vec, g.carries[2 * k + 1])
        off = 1 if back else 0
        t.transpose(c_ps[0:P, 0:C], row[0:C, off:off + P], g.ident[0:C, 0:C]).then_inc(turned, 1)


def segments(g, layer):
    order = 1 if layer == 1 else 0
    vec, sca, ten, scans = [g.sem(f"{n}_m") for n in ("vector", "scalar", "tensor", "scans")]
    g.carries = []
    BC = lambda ap, *s: ap.broadcast_to(list(s))
    with ExitStack() as ctx:
        sb = lambda n, s, d=F32: g.sb(f"{n}_m{layer}", s, d, ctx)
        A, B, a_sb, row = sb("A", [P, D]), sb("B", [P, D]), sb("a_sb", [D, P]), sb("row", [D, P + 1])
        a_ps, b_ps, c_ps = [g.ps(f"{n}_m{layer}", [128, 128], F32, ctx) for n in ("a_ps", "b_ps", "c_ps")]
        cont, opn = g.cont[order], g.open[order]
        if layer == 0:
            C = H
            lm, es, m, d = sb("lm", [P, C, EJ]), sb("es", [P, C, EJ]), sb("m", [P, C, EJ + 1]), sb("d", [P, C, EJ])
            w, wself, fac, z, cm = (sb("w", [P, C, EJ]), sb("ws", [P, C, EJ]), sb("fac", [P, C, EJ]),
                                    sb("z", [P, C, EJ]), sb("cm", [P, C]))
            drop, lowered, first = sb("drop", [P, EJ]), sb("lowered", [P, EJ]), sb("first", [P, EJ])
            sizes = [(H, False), (H, False), (D, False)]
        if layer == 3:
            C = R
            mask, neg, y = sb("mask", [P, R, EJ]), sb("neg", [P, R, EJ]), sb("y", [P, R, EJ])
            f = sb("f", [P, R, EJ])
            lm, es, sel = sb("lm", [P, EJ]), sb("es", [P, EJ]), sb("sel", [P, EJ])
            w, drop, lowered, cm = sb("w", [P, EJ]), sb("drop", [P, EJ]), sb("lowered", [P, EJ]), sb("cm", [P, R])
            ends, cback = sb("ends", [P, EJ]), sb("cback", [P, R])
            openb = sb("openb", [P, EJ])
            sizes = [(R, False), (R, True), (R, False), (R, True), (D, False)]
        if layer in (1, 2):
            sizes = [(D, False)]

        with g.nc.Block() as block:
            @block.vector
            def _(v):
                n = Count(vec)
                acts = [0]

                def scalar_done():
                    acts[0] += 1
                    v.wait_ge(sca, acts[0])

                def up(ins):
                    n.up(ins)
                    n.here(v)

                def carry(out, Cn, op0, op1, init, back=False):
                    k = len(g.carries) // 2
                    carry_on(v, n, ten, g, k, A, B, Cn, out, a_sb, row, a_ps, b_ps, c_ps, op0, op1, init, back)

                def leaky(out, ap, slope):
                    up(v.scalar_tensor_tensor(out, ap, slope, ap, ALU.mult, ALU.max))

                if layer == 0:
                    up(v.tensor_tensor(lm[:, :, :], g.score[:, 0:H, :], g.attn[:, :, :], ALU.add))
                    leaky(lm[:, :, :], lm[:, :, :], 0.01)
                    leaky(es[:, :, :], g.score[:, H:, :], 0.01)
                    up(v.tensor_tensor(d[:, :, :], lm[:, :, :], es[:, :, :], ALU.max))
                    up(v.tensor_scalar(drop[:, :], cont[:, :], 1.0, BIG, ALU.subtract, ALU.mult))
                    up(v.tensor_scalar(lowered[:, :], opn[:, :], 1.0, BIG, ALU.subtract, ALU.mult))
                    up(v.tensor_scalar(first[:, :], cont[:, :], -1.0, 1.0, ALU.mult, ALU.add))
                    for h in range(H):
                        up(v.tensor_tensor_scan(m[:, h, 1:], drop[:, :], d[:, h, :], -BIG, ALU.add, ALU.max))
                    up(v.tensor_copy(A[:, 0:H], BC(lowered[:, EJ - 1:], P, H)))
                    up(v.tensor_copy(B[:, 0:H], m[:, :, EJ]))
                    carry(cm[:, :], H, ALU.add, ALU.max, -BIG)
                    for h in range(H):
                        up(v.scalar_tensor_tensor(m[:, h, 1:], lowered[:, :], cm[:, h:h + 1], m[:, h, 1:],
                                                  ALU.add, ALU.max))
                    up(v.tensor_copy(m[:, :, 0], cm[:, :]))
                    up(v.tensor_tensor(fac[:, :, :], m[:, :, 0:EJ], m[:, :, 1:], ALU.subtract))
                    up(v.tensor_scalar(fac[:, :, :], fac[:, :, :], 0.0, None, ALU.min))
                    up(v.tensor_tensor(w[:, :, :], lm[:, :, :], m[:, :, 1:], ALU.subtract))
                    up(v.tensor_tensor(wself[:, :, :], es[:, :, :], m[:, :, 1:], ALU.subtract))
                    g.exp_in = n.n
                    scalar_done()
                    up(v.tensor_tensor(fac[:, :, :], fac[:, :, :], BC(cont[:, :].unsqueeze(1), P, H, EJ), ALU.mult))
                    up(v.tensor_tensor(d[:, :, :], wself[:, :, :], BC(first[:, :].unsqueeze(1), P, H, EJ), ALU.mult))
                    up(v.tensor_tensor(d[:, :, :], d[:, :, :], w[:, :, :], ALU.add))
                    for h in range(H):
                        up(v.tensor_tensor_scan(z[:, h, :], fac[:, h, :], d[:, h, :], 0.0, ALU.mult, ALU.add))
                        up(v.tensor_tensor_scan(g.reach[:, h, :], fac[:, h, :], BC(g.ones[0:P, 0:1], P, EJ),
                                                1.0, ALU.mult, ALU.mult))
                    up(v.tensor_copy(A[:, 0:H], g.reach[:, :, EJ - 1]))
                    up(v.tensor_copy(B[:, 0:H], z[:, :, EJ - 1]))
                    carry(cm[:, :], H, ALU.mult, ALU.add, 0.0)
                    for h in range(H):
                        up(v.scalar_tensor_tensor(z[:, h, :], g.reach[:, h, :], cm[:, h:h + 1], z[:, h, :],
                                                  ALU.mult, ALU.add))
                    up(v.reciprocal(g.rz[:, :, :], z[:, :, :]))
                    for h in range(H):
                        part = g.val[:, :, h * HF:(h + 1) * HF]
                        up(v.tensor_tensor(part, part, BC(w[:, h, :].unsqueeze(2), P, EJ, HF), ALU.mult))
                if layer == 3:
                    leaky(lm[:, :], g.score[:, 0, :], 0.2)
                    leaky(es[:, :], g.score[:, 1, :], 0.2)
                    up(v.tensor_tensor(sel[:, :], lm[:, :], es[:, :], ALU.max))
                    up(v.tensor_tensor(mask[:, :, :], BC(g.iotaf[:, 0:R].unsqueeze(2), P, R, EJ),
                                       BC(g.etype[:, :].unsqueeze(1), P, R, EJ), ALU.is_equal))
                    up(v.tensor_scalar(neg[:, :, :], mask[:, :, :], 1.0, BIG, ALU.subtract, ALU.mult))
                    up(v.tensor_tensor(y[:, :, :], mask[:, :, :], BC(sel[:, :].unsqueeze(1), P, R, EJ), ALU.mult))
                    up(v.tensor_tensor(y[:, :, :], y[:, :, :], neg[:, :, :], ALU.add))
                    up(v.tensor_scalar(drop[:, :], cont[:, :], 1.0, BIG, ALU.subtract, ALU.mult))
                    up(v.tensor_scalar(lowered[:, :], opn[:, :], 1.0, BIG, ALU.subtract, ALU.mult))
                    up(v.tensor_scalar(ends[:, :], g.goes_on[:, :], -1.0, 1.0, ALU.mult, ALU.add))
                    up(v.tensor_tensor_scan(openb[:, ::-1], g.goes_on[:, ::-1], BC(g.ones[0:P, 0:1], P, EJ),
                                            1.0, ALU.mult, ALU.mult))

                    def to_all_edges():
                        up(v.tensor_tensor(f[:, :, :], f[:, :, :], BC(ends[:, :].unsqueeze(1), P, R, EJ), ALU.mult))
                        for r in range(R):
                            up(v.tensor_tensor_scan(y[:, r, ::-1], g.goes_on[:, ::-1], f[:, r, ::-1], 0.0,
                                                    ALU.mult, ALU.add))
                        up(v.tensor_copy(A[:, 0:R], BC(openb[:, 0:1], P, R)))
                        up(v.tensor_copy(B[:, 0:R], y[:, :, 0]))
                        carry(cback[:, :], R, ALU.mult, ALU.add, 0.0, back=True)
                        for r in range(R):
                            up(v.scalar_tensor_tensor(y[:, r, :], openb[:, :], cback[:, r:r + 1], y[:, r, :],
                                                      ALU.mult, ALU.add))
                        up(v.tensor_tensor(y[:, :, :], y[:, :, :], mask[:, :, :], ALU.mult))
                        up(v.tensor_reduce(sel[:, :], y[:, :, :].rearrange("p r j -> p j r"), AX.X, ALU.add))

                    for r in range(R):
                        up(v.tensor_tensor_scan(f[:, r, :], drop[:, :], y[:, r, :], -BIG, ALU.add, ALU.max))
                    up(v.tensor_copy(A[:, 0:R], BC(lowered[:, EJ - 1:], P, R)))
                    up(v.tensor_copy(B[:, 0:R], f[:, :, EJ - 1]))
                    carry(cm[:, :], R, ALU.add, ALU.max, -BIG)
                    for r in range(R):
                        up(v.scalar_tensor_tensor(f[:, r, :], lowered[:, :], cm[:, r:r + 1], f[:, r, :],
                                                  ALU.add, ALU.max))
                    to_all_edges()
                    up(v.tensor_tensor(w[:, :], lm[:, :], sel[:, :], ALU.subtract))
                    up(v.tensor_tensor(es[:, :], es[:, :], sel[:, :], ALU.subtract))
                    g.exp_in = n.n
                    scalar_done()
                    up(v.tensor_tensor(y[:, :, :], mask[:, :, :], BC(w[:, :].unsqueeze(1), P, R, EJ), ALU.mult))
                    for r in range(R):
                        up(v.tensor_tensor_scan(f[:, r, :], cont[:, :], y[:, r, :], 0.0, ALU.mult, ALU.add))
                    up(v.tensor_copy(A[:, 0:R], BC(opn[:, EJ - 1:], P, R)))
                    up(v.tensor_copy(B[:, 0:R], f[:, :, EJ - 1]))
                    carry(cm[:, :], R, ALU.mult, ALU.add, 0.0)
                    for r in range(R):
                        up(v.scalar_tensor_tensor(f[:, r, :], opn[:, :], cm[:, r:r + 1], f[:, r, :],
                                                  ALU.mult, ALU.add))
                    to_all_edges()
                    up(v.tensor_tensor(sel[:, :], sel[:, :], es[:, :], ALU.add))
                    up(v.reciprocal(sel[:, :], sel[:, :]))
                    up(v.tensor_tensor(w[:, :], w[:, :], sel[:, :], ALU.mult))
                    up(v.tensor_tensor(g.val[:, :, :], g.val[:, :, :], BC(w[:, :].unsqueeze(2), P, EJ, D), ALU.mult))

                flat = g.val[:, :, :].rearrange("p j f -> p f j")
                if layer == 0:
                    for h in range(H):
                        with v.Fori(0, HF) as k:
                            col = flat[:, bass.ds(k + h * HF, 1), :].rearrange("p a j -> p (a j)")
                            v.tensor_tensor_scan(col, fac[:, h, :], col, 0.0, ALU.mult, ALU.add).then_inc(scans, 1)
                else:
                    with v.Fori(0, D) as k:
                        col = flat[:, bass.ds(k, 1), :].rearrange("p a j -> p (a j)")
                        v.tensor_tensor_scan(col, cont[:, :], col, 0.0, ALU.mult, ALU.add).then_inc(scans, 1)
                v.wait_ge(scans, D)
                if layer == 0:
                    up(v.tensor_copy(A[:, :].rearrange("p (h f) -> p h f", h=H),
                                     BC(g.reach[:, :, EJ - 1:], P, H, HF)))
                else:
                    up(v.tensor_copy(A[:, :], BC(opn[:, EJ - 1:], P, D)))
                up(v.tensor_copy(B[:, :], g.val[:, EJ - 1, :]))
                carry(g.carry[:, :], D, ALU.mult, ALU.add, 0.0)

            @block.scalar
            def _(a):
                if layer == 0:
                    a.wait_ge(vec, g.exp_in)
                    for x in (fac, w, wself):
                        last = a.activation(x[:, :, :], x[:, :, :], ACT.Exp)
                    last.then_inc(sca, 1)
                if layer == 3:
                    a.wait_ge(vec, g.exp_in)
                    for x in (w, es):
                        last = a.activation(x[:, :], x[:, :], ACT.Exp)
                    last.then_inc(sca, 1)

            @block.tensor
            def _(t):
                turn_carries(t, g, vec, ten, sizes, A, B, row, a_ps, b_ps, c_ps)


def scatter(g, layer):
    order = 1 if layer == 1 else 0
    step, staged, sent = g.sem("step_s"), g.sem("staged_s"), [g.once(f"sent{b}_s{layer}") for b in range(2)]
    copied = g.sem("idx_s")
    opn = g.open[order]
    with ExitStack() as ctx:
        stage = [g.sb(f"stage{b}_s{layer}", [P, G, D], F32, ctx) for b in range(2)]
        idx = [g.sb(f"idx{b}_s{layer}", [P, G], I32, ctx) for b in range(2)]
        with g.nc.Block() as block:
            @block.vector
            def _(v):
                n = LoopCount(step, 2 * (3 if layer == 0 else 2))
                with v.Fori(0, CH // 2) as i:
                    for b in range(2):
                        c = i * 2 + b
                        at = bass.ds(c * G, G)
                        v.wait_ge(sent[b], i * (16 * G))
                        if layer == 0:
                            for h in range(H):
                                f = slice(h * HF, (h + 1) * HF)
                                last = v.tensor_tensor(stage[b][:, :, f],
                                                       g.carry[:, f].unsqueeze(1).broadcast_to([P, G, HF]),
                                                       g.reach[:, h, at].unsqueeze(2).broadcast_to([P, G, HF]), ALU.mult)
                            n.up(last)
                        else:
                            n.up(v.tensor_tensor(stage[b][:, :, :], g.carry[:, :].unsqueeze(1).broadcast_to([P, G, D]),
                                                 opn[:, at].unsqueeze(2).broadcast_to([P, G, D]), ALU.mult))
                        n.here(v, i)
                        n.up(v.tensor_tensor(stage[b][:, :, :], stage[b][:, :, :], g.val[:, at, :], ALU.add))
                        n.here(v, i)
                        if layer == 0:
                            for h in range(H):
                                f = slice(h * HF, (h + 1) * HF)
                                last = v.tensor_tensor(stage[b][:, :, f], stage[b][:, :, f],
                                                       g.rz[:, h, at].unsqueeze(2).broadcast_to([P, G, HF]), ALU.mult)
                            n.up(last)
                            n.here(v, i)
                        v.sem_inc(staged, 1)

            @block.gpsimd
            def _(pool):
                n = LoopCount(copied, 2, g=g)
                with pool.Fori(0, CH // 2) as i:
                    for b in range(2):
                        c = i * 2 + b
                        pool.wait_ge(sent[b], i * (16 * G))
                        g.passed(pool)
                        n.up(pool.tensor_copy(idx[b][:, :], g.out_row[order][:, bass.ds(c * G, G)]))
                        n.here(pool, i)
                        pool.wait_ge(staged, c + 1)
                        g.passed(pool)
                        for k in range(G):
                            pool.indirect_dma_start(out=g.tab[layer],
                                                    out_offset=bass.IndirectOffsetOnAxis(ap=idx[b][:, k:k + 1], axis=0),
                                                    in_=stage[b][:, k, :], in_offset=None,
                                                    bounds_check=2 * N - 1, oob_is_err=False).then_inc(sent[b], 16)
                for b in range(2):
                    pool.wait_ge(sent[b], EJ * 8)


def nodes(g, layer):
    sem = lambda n: g.sem(f"{n}_n")
    row_in, row_free, turned, turned_out = [sem(f"in{b}") for b in range(2)], sem("free"), sem("turned"), sem("turned_out")
    made, made_free, step, sca, pst = sem("made"), sem("made_free"), sem("steps"), sem("squares"), sem("pool")
    y_done, sent = sem("y_done"), [g.once(f"sent{b}_n{layer}") for b in range(2)]
    zeroed, relu_done = sem("zeroed"), sem("relu_done")
    norms = 2 if layer == 0 else 1
    HG = NG // 2
    with ExitStack() as ctx:
        sb = lambda n, s, d=F32: g.sb(f"{n}_n{layer}", s, d, ctx)
        ps = lambda n, s, d=F32: g.ps(f"{n}_n{layer}", s, d, ctx)
        rows = [sb(f"rows{b}", [P, NG, 2 * D]) for b in range(2)]
        xt = [sb(f"xt{k}", [128, HG * P]) for k in range(2)]
        tp = [ps(f"tp{k}", [128, HG * P]) for k in range(2)]
        out = [ps(f"out{b}", [P, NG, D]) for b in range(2)]
        cd, sq, st = sb("cd", [P, NG, D]), sb("sq", [P, NG, D]), sb("st", [P, 4, NG])
        q, rs, mh = sb("q", [P, NG]), sb("rs", [P, NG]), sb("minus_half", [P, NG])
        y = [sb(f"y{b}", [P, NG, 2, D]) for b in range(2)]
        if layer == 0:
            e, u = sb("e", [P, NG, D]), sb("u", [P, NG, D])
        if layer == 1:
            h_ps = [ps(f"h{k}", [D, HG * P]) for k in range(2)]
            h_sb = [sb(f"hs{k}", [D + 1, HG * P]) for k in range(2)]
            lab = [sb(f"lab{b}", [P, NG, g.LW]) for b in range(2)]
            hidden, hidden_out, one_row = sem("hidden"), sem("hidden_out"), sem("one_row")
            lab_done, lab_sent = sem("lab_done"), [g.once(f"lab_sent{b}") for b in range(2)]
        rhs = {0: g.n1, 2: g.n3, 3: g.n4}.get(layer)
        src = g.tab[layer].rearrange("(p k t) d -> p k (t d)", p=P, t=2)
        if layer < 3:
            dst = g.tab[layer + 1].rearrange("(p k t) d -> p k t d", p=P, t=2)
        else:
            dst = g.out.rearrange("(p k) d -> p k d", p=P)

        with g.nc.Block() as block:
            @block.sync
            def _(sp):
                with sp.Fori(0, NCH // 2) as i:
                    for b in range(2):
                        sp.wait_ge(row_free, i * 2 + b + 1)
                        sp.dma_start(rows[b][:, :, :], src[:, bass.ds((i * 2 + b) * NG, NG), :]).then_inc(row_in[b], 16)

            @block.tensor
            def _(t):
                if layer == 1:
                    t.wait_ge(one_row, 2)
                with t.Fori(0, NCH // 2) as i:
                    for b in range(2):
                        c = i * 2 + b
                        t.wait_ge(row_in[b], i * 16 + 16)
                        for k in range(2):
                            for j in range(HG):
                                last = t.transpose(tp[k][:, j * P:(j + 1) * P], rows[b][:, k * HG + j, :],
                                                   g.ident[0:P, 0:P])
                            last.then_inc(turned, 1)
                        if layer == 1:
                            for k in range(2):
                                t.wait_ge(turned_out, c * 2 + k + 1)
                                t.matmul(h_ps[k][:, :], g.wn1[:, :], xt[k][:, :], start=True, stop=True
                                         ).then_inc(hidden, 1)
                        t.wait_ge(made_free, c + 1)
                        for k in range(2):
                            if layer == 1:
                                t.wait_ge(hidden_out, c * 2 + k + 1)
                            else:
                                t.wait_ge(turned_out, c * 2 + k + 1)
                            for j in range(HG):
                                o = out[b][:, k * HG + j, :]
                                e0 = slice(j * P, (j + 1) * P)
                                if layer == 1:
                                    t.matmul(o, h_sb[k][:, e0], g.wn2[:, :], start=True, stop=False)
                                    last = t.matmul(o, xt[k][0:D, e0], g.ident[0:D, 0:D], start=False, stop=True)
                                elif layer == 3:
                                    t.matmul(o, g.ones[0:1, 0:P], g.b4[:, 0:D], start=True, stop=False)
                                    last = t.matmul(o, xt[k][:, e0], rhs[:, :], start=False, stop=True)
                                else:
                                    last = t.matmul(o, xt[k][:, e0], rhs[:, :], start=True, stop=True)
                        last.then_inc(made, 1)

            @block.scalar
            def _(a):
                with a.Fori(0, NCH // 2) as i:
                    for b in range(2):
                        c = i * 2 + b
                        for k in range(2):
                            a.wait_ge(turned, c * 2 + k + 1)
                            a.wait_ge(made, c)
                            a.activation(xt[k][:, :], tp[k][:, :], ACT.Copy).then_inc(turned_out, 1)
                        if layer == 1:
                            for k in range(2):
                                a.wait_ge(hidden, c * 2 + k + 1)
                                a.activation(h_sb[k][0:D, :], h_ps[k][:, :], ACT.Silu, bias=g.bn1[:, 0:1]
                                             ).then_inc(hidden_out, 1)
                        if layer == 0:
                            a.wait_ge(made, c + 1)
                            a.wait_ge(step, c * g.node_steps[layer])
                            a.activation(e[:, :, :], out[b][:, :, :], ACT.Relu, scale=-1.0).then_inc(relu_done, 1)
                            a.wait_ge(relu_done, c + 1)
                            a.activation(e[:, :, :], e[:, :, :], ACT.Exp, scale=-1.0).then_inc(sca, 1)
                        for k in range(norms):
                            a.wait_ge(step, c * g.node_steps[layer] + g.centred[layer][k])
                            a.activation(sq[:, :, :], cd[:, :, :], ACT.Square).then_inc(sca, 1)

            @block.vector
            def _(v):
                v.sem_inc(row_free, 2)
                v.sem_inc(made_free, 2)
                if layer == 1:
                    for k in range(2):
                        v.memset(h_sb[k][D:D + 1, :], 1.0).then_inc(one_row, 1)
                n = LoopCount(step, 2 * g.node_steps[layer])
                per_s = 3 if layer == 0 else 1
                B3 = [P, NG, D]

                def norm(i, c, x, k, b):
                    n.up(v.tensor_reduce(st[:, 0, :], x, AX.X, ALU.add)); n.here(v, i)
                    n.up(v.tensor_scalar(st[:, 1, :], st[:, 0, :], -1.0 / D, None, ALU.mult)); n.here(v, i)
                    v.wait_ge(y_done, c * norms + k)
                    n.up(v.tensor_tensor(cd[:, :, :], x, st[:, 1, :].unsqueeze(2).broadcast_to(B3), ALU.add))
                    assert n.n == b * g.node_steps[layer] + g.centred[layer][k]
                    v.wait_ge(sca, c * per_s + per_s - norms + k + 1)
                    n.up(v.tensor_reduce(q[:, :], sq[:, :, :], AX.X, ALU.add)); n.here(v, i)

                with v.Fori(0, NCH // 2) as i:
                    for b in range(2):
                        c = i * 2 + b
                        v.wait_ge(made, c + 1)
                        if layer == 0:
                            v.wait_ge(sca, c * 3 + 1)
                            n.up(v.scalar_tensor_tensor(u[:, :, :], e[:, :, :], -1.0, out[b][:, :, :],
                                                        ALU.add, ALU.max))
                            n.here(v, i)
                            v.sem_inc(made_free, 1)
                            norm(i, c, u[:, :, :], 0, b)
                            v.wait_ge(y_done, c * 2 + 1)
                            n.up(v.tensor_tensor(u[:, :, :], y[b][:, :, 0, :],
                                                 g.lnw[:, 0, :].unsqueeze(1).broadcast_to(B3), ALU.mult)); n.here(v, i)
                            n.up(v.tensor_tensor(u[:, :, :], u[:, :, :],
                                                 g.lnw[:, 1, :].unsqueeze(1).broadcast_to(B3), ALU.add)); n.here(v, i)
                            v.wait_ge(turned, c * 2 + 2)
                            n.up(v.tensor_tensor(u[:, :, :], u[:, :, :], rows[b][:, :, 0:D], ALU.add))
                            n.here(v, i)
                            v.sem_inc(row_free, 1)
                            norm(i, c, u[:, :, :], 1, b)
                        else:
                            norm(i, c, out[b][:, :, :], 0, b)
                            v.wait_ge(turned, c * 2 + 2)
                            v.sem_inc(made_free, 1)
                            v.sem_inc(row_free, 1)

            @block.gpsimd
            def _(pool):
                m = Count(zeroed)
                m.up(pool.memset(mh[:, :], -0.5))
                for b in range(2):
                    m.up(pool.memset(y[b][:, :, 1, :], 0.0))
                    if layer == 1:
                        m.up(pool.memset(lab[b][:, :, :], 0.0))
                m.here(pool)
                n = LoopCount(pst, 4 * norms, g=g)
                with pool.Fori(0, NCH // 2) as i:
                    for b in range(2):
                        c = i * 2 + b
                        for k in range(norms):
                            eps = 1e-6 if layer == 0 and k == 0 else 1e-5
                            pool.wait_ge(step, c * g.node_steps[layer] + g.centred[layer][k] + 1)
                            g.passed(pool)
                            n.up(pool.tensor_scalar(rs[:, :], q[:, :], 1.0 / D, eps, ALU.mult, ALU.add)); n.here(pool, i)
                            n.up(pool.tensor_tensor(rs[:, :], rs[:, :], mh[:, :], ALU.pow)); n.here(pool, i)
                            pool.wait_ge(sent[b], i * 16)
                            g.passed(pool)
                            pool.tensor_tensor(y[b][:, :, 0, :], cd[:, :, :],
                                               rs[:, :].unsqueeze(2).broadcast_to([P, NG, D]), ALU.mult
                                               ).then_inc(y_done, 1)
                        pool.wait_ge(y_done, c * norms + norms)
                        g.passed(pool)
                        if layer == 1:
                            pool.wait_ge(lab_sent[b], i * 16)
                            g.passed(pool)
                            pool.tensor_copy(lab[b][:, :, 0:D], y[b][:, :, 0, :])
                            pool.tensor_copy(lab[b][:, :, D:D + 1], g.label[:, bass.ds(c * NG, NG)].unsqueeze(2)
                                             ).then_inc(lab_done, 1)
                            pool.wait_ge(lab_done, c + 1)
                            g.passed(pool)
                            pool.dma_start(g.labelled.rearrange("(p k) d -> p k d", p=P)[:, bass.ds(c * NG, NG), :],
                                           lab[b][:, :, :]).then_inc(lab_sent[b], 16)
                        if layer < 3:
                            pool.dma_start(dst[:, bass.ds(c * NG, NG), :, :], y[b][:, :, :, :]).then_inc(sent[b], 16)
                        else:
                            pool.dma_start(dst[:, bass.ds(c * NG, NG), :], y[b][:, :, 0, :]).then_inc(sent[b], 16)
                for b in range(2):
                    pool.wait_ge(sent[b], NCH * 8)
                    if layer == 1:
                        pool.wait_ge(lab_sent[b], NCH * 8)


def build(nc, args, out, tables, labelled, sorted_, layers=4):
    with ExitStack() as ctx:
        g = Graph(nc, args, ctx)
        g.x_rows, g.out, g.tab, g.labelled, g.sorted = args["x"], out, tables, labelled, sorted_
        g.LW = labelled.shape[1]
        g.node_steps = {0: 12, 1: 4, 2: 4, 3: 4}
        g.centred = {0: (4, 11), 1: (3,), 2: (3,), 3: (3,)}
        g.row1 = [g.sb(f"row1_{s}", [P, 2, EJ], I32) for s in range(2)]
        g.row2 = [g.sb(f"row2_{s}", [P, 2, EJ], I32) for s in range(2)]
        g.out_row = [g.sb(f"out_row{s}", [P, EJ], I32) for s in range(2)]
        g.cont = [g.sb(f"cont{s}", [P, EJ]) for s in range(2)]
        g.open = [g.sb(f"open{s}", [P, EJ]) for s in range(2)]
        g.goes_on = g.sb("goes_on", [P, EJ])
        g.etype, g.radial, g.attn = g.sb("etype", [P, EJ]), g.sb("radial", [P, EJ]), g.sb("attn", [P, H, EJ])
        g.iotaf = g.sb("iotaf", [P, R])
        weights(g)
        with ExitStack() as sorting:
            g.rec = g.sb("rec", [P, EJ, REC], F32, sorting)
            g.keys = g.sb("keys", [P, 4, EJ + 1], F32, sorting)
            g.iota = g.sb("iota", [P, LO], BF16, sorting)
            g.base = g.sb("base", [HB, 2, 2 * LO], F32, sorting)
            g.strict = g.sb("strict", [P, P], F32, sorting)
            load_and_constants(g)
            histogram(g)
            rank_and_scatter(g)
        read_orders(g)
        g.clear()
        g.val = g.sb("val", [P, EJ, D])
        g.score = g.sb("score", [P, 2 * H, EJ])
        g.reach, g.rz, g.carry = g.sb("reach", [P, H, EJ]), g.sb("rz", [P, H, EJ]), g.sb("carry", [P, D])
        for layer in range(layers):
            for phase in (edges, segments, scatter, nodes):
                phase(g, layer)
                g.clear()


def kernel(**inputs):
    import numpy as _np
    import concourse.bacc as _bacc
    from concourse import mybir as _mybir
    from concourse.bass_utils import run_bass_kernel_spmd as _run

    nc = _bacc.Bacc("TRN2", target_bir_lowering=False, num_devices=1)
    arrays, args = {}, {}
    for name, value in inputs.items():
        arr = _np.ascontiguousarray(value)
        arrays[f"in_{name}"] = arr
        args[name] = nc.dram_tensor(f"in_{name}", arr.shape, _mybir.dt.from_np(arr.dtype), kind="ExternalInput").ap()
    out = nc.dram_tensor("out_0", (N, D), F32, kind="ExternalOutput").ap()
    tables = [nc.dram_tensor(f"table{k}", (2 * N, D), F32, kind="Internal").ap() for k in range(4)]
    labelled = nc.dram_tensor("labelled", (N, 72), F32, kind="Internal").ap()
    sorted_ = [nc.dram_tensor(f"sorted{k}", (E, REC), F32, kind="Internal").ap() for k in range(2)]
    build(nc, args, out, tables, labelled, sorted_)
    r = _run(nc, [arrays], core_ids=[0])
    return r.results[0]["out_0"]
```

```python
from contextlib import ExitStack

import concourse.bass as bass
from concourse import mybir

F32 = mybir.dt.float32
BF16 = mybir.dt.bfloat16
I32 = mybir.dt.int32
ALU = mybir.AluOpType
ACT = mybir.ActivationFunctionType
AX = mybir.AxisListType

N = 50000
E = 25000
D = 64
P = 125
EJ = E // P
NK = N // P
G = 4
CH = EJ // G
NG = 8
NCH = NK // NG
R = 8
H = 4
HF = 16
LO = 256
HB = 98
REC = 8
SRC, DST, TYPE, RADIAL, ATT = 0, 1, 2, 3, 4
BIG = 1.0e30
SKIP = 1.0e6
assert P * EJ == E and P * NK == N and 2 * HB * LO >= N and CH % 2 == 0 and NCH % 2 == 0


class Count:

    def __init__(self, sem):
        self.sem, self.n = sem, 0

    def up(self, ins):
        self.n += 1
        return ins.then_inc(self.sem, 1)

    def here(self, eng):
        eng.wait_ge(self.sem, self.n)


class LoopCount:

    def __init__(self, sem, per, base=0, g=None):
        self.sem, self.per, self.base, self.n, self.g = sem, per, base, 0, g

    def up(self, ins):
        self.n += 1
        assert self.n <= self.per
        return ins.then_inc(self.sem, 1)

    def here(self, eng, i):
        eng.wait_ge(self.sem, i * self.per + (self.base + self.n))
        if self.g:
            self.g.passed(eng)

    def at(self, i, n):
        return i * self.per + (self.base + n)


class Graph:

    def __init__(self, nc, args, ctx):
        self.nc, self.ctx, self.a = nc, ctx, args
        self.sems, self.raised = {"waits_passed": ctx.enter_context(nc.semaphore("waits_passed"))}, []

    def sem(self, name):
        if name not in self.sems:
            self.sems[name] = self.ctx.enter_context(self.nc.semaphore(name))
        self.raised.append(self.sems[name])
        return self.sems[name]

    def once(self, name):
        return self.ctx.enter_context(self.nc.semaphore(name))

    def passed(self, eng):
        eng.sem_inc(self.sems["waits_passed"], 1)

    def clear(self):
        with self.nc.Block() as block:
            @block.sync
            def _(sp):
                for s in self.raised:
                    sp.sem_clear(s)
                sp.sem_clear(self.sems["waits_passed"])
        self.raised = []

    def sb(self, name, shape, dt=F32, ctx=None):
        t = (ctx or self.ctx).enter_context(self.nc.sbuf_tensor(name, shape, dt))
        return t

    def ps(self, name, shape, dt=F32, ctx=None):
        return ctx.enter_context(self.nc.psum_tensor(name, shape, dt))


def weights(g):
    g.ident = g.sb("ident", [128, 128])
    g.identb = g.sb("identb", [128, 128], BF16)
    g.ones = g.sb("ones", [128, 128])
    g.w0 = g.sb("w0", [128, D + 2 * H])
    g.n1p, g.wn1x, g.wn1g, g.wn2p, g.n3p, g.n4p = [g.sb(n, [128, 128]) for n in
                                                   ("n1p", "wn1x", "wn1g", "wn2p", "n3p", "n4p")]
    g.bn1p = g.sb("bn1p", [128, 1])
    g.onesb = g.sb("onesb", [3, P], BF16)
    g.bn2c = g.sb("bn2c", [3, NG, D], BF16)
    g.b4c = g.sb("b4c", [3, NG, D], BF16)
    g.w1a = g.sb("w1a", [128, D])
    g.w1r = g.sb("w1r", [P, D])
    g.be1 = g.sb("be1", [D, 1])
    g.w2 = g.sb("w2", [D, D])
    g.be2 = g.sb("be2", [D, 1])
    g.wa = g.sb("wa", [D, D])
    g.ba = g.sb("ba", [D, 1])
    g.wg = g.sb("wg", [128, D])
    g.w3 = g.sb("w3", [128, R * D])
    g.w3s = g.sb("w3s", [128, 2 * R])
    g.lnw = g.sb("lnw", [P, 2, D])
    g.label = g.sb("label", [P, NK])


def load_and_constants(g):
    nc, a = g.nc, g.a
    ld = g.sem("inputs_loaded")
    pc, vc, tc = g.sem("prep_pool"), g.sem("prep_vector"), g.sem("prep_tensor")
    pool_n, v_n, t_n = Count(pc), Count(vc), Count(tc)

    with ExitStack() as ctx:
        sb = lambda n, s, d=F32: g.sb(n, s, d, ctx)
        wd = sb("wd", [D, 2, D]); acol = sb("acol", [D, 3]); bd = sb("bd", [D, H])
        abd = sb("abd", [D, 3, H]); we = sb("we", [D, HF]); wea = sb("wea", [D, H, HF])
        wvb = sb("wvb", [P, H, HF]); wacol = sb("wacol", [D, 1])
        ws2 = sb("ws2", [D, 2, D]); wg2 = sb("wg2", [D, 2, D])
        att3 = sb("att3", [128, R * D]); t3 = sb("t3", [128, R * D]); u3 = sb("u3", [128, 2 * R])
        ws3 = sb("ws3", [128, D]); wsum = sb("wsum", [128, D])
        brow = sb("brow", [3, (R + 1) * D]); bsum = sb("bsum", [3, D])
        piece, pieces = sb("piece", [3, D], BF16), sb("pieces", [3, D])
        wn1h, wn2h, bn2 = sb("wn1h", [128, 2, D]), sb("wn2h", [128, D]), sb("bn2", [3, D])
        half_w, means = sb("half_w", [128, 3, D]), sb("means", [128, 16])
        lab_i = sb("lab_i", [P, NK], I32)
        ea = sb("ea", [P, EJ, 16]); ea3 = sb("ea3", [P, EJ, 3]); tmp = sb("tmp", [P, EJ, 16])
        si = sb("si", [P, EJ], I32); di = sb("di", [P, EJ], I32); ti = sb("ti", [P, EJ], I32)
        hl = sb("hl", [P, 4, EJ], I32); iot = sb("iot", [P, LO], I32)
        shift = sb("shift", [D, 128])
        ps = g.ps("prep_ps", [128, 512], F32, ctx)
        ps2 = g.ps("prep_ps2", [128, 512], F32, ctx)
        ps3 = g.ps("prep_ps3", [128, 512], F32, ctx)
        L = [0]
        PREP = 9

        with nc.Block() as block:
            @block.sync
            def _(sp):
                def load(dst, src, short=False):
                    L[0] += 16
                    sp.dma_start(dst, src, allow_slow_non_contiguous=short).then_inc(ld, 16)
                row = lambda ap: ap.rearrange("(a n) -> a n", a=1)
                col = lambda ap: ap.rearrange("(n a) -> n a", a=1)
                load(si[:, :], a["src"].rearrange("(p j) -> p j", p=P))
                load(di[:, :], a["dst"].rearrange("(p j) -> p j", p=P))
                load(ti[:, :], a["edge_type_8"].rearrange("(p j) -> p j", p=P))
                load(ea[:, :, :], a["edge_attr_16"].rearrange("(p j) d -> p j d", p=P))
                load(ea3[:, :, :], a["edge_attr_3"].rearrange("(p j) d -> p j d", p=P))
                load(lab_i[:, :], a["node_type_2"].rearrange("(p k) -> p k", p=P))
                w2d = a["L0_gnn_W"].rearrange("h f i -> (h f) i")
                for b in range(2):
                    load(wd[:, b, :], w2d)
                for h in range(H):
                    load(acol[h * HF:(h + 1) * HF, :], a["L0_gnn_a"][h, :].rearrange("(s f) -> f s", f=HF), True)
                load(we[:, :], a["L0_gnn_W_edge"].rearrange("h f i -> (h f) i"))
                for b, n in enumerate(("L0_gnn_ln_scale", "L0_gnn_ln_bias")):
                    load(g.lnw[:, b, :], row(a[n]).broadcast_to([P, D]))
                load(g.w1a[:, :], a["L1_gnn_We1"][0:2 * D, :])
                load(g.w1r[:, :], a["L1_gnn_We1"][2 * D:2 * D + 1, :].broadcast_to([P, D]))
                load(g.be1[:, :], col(a["L1_gnn_be1"]))
                load(g.w2[:, :], a["L1_gnn_We2"])
                load(g.be2[:, :], col(a["L1_gnn_be2"]))
                load(wacol[:, :], a["L1_gnn_Wa"])
                load(g.ba[:, :], row(a["L1_gnn_ba"]).broadcast_to([D, 1]))
                for b in range(2):
                    half = slice(b * D, (b + 1) * D)
                    load(wn1h[half, 0, :], a["L1_gnn_Wn1"][0:D, :])
                    load(wn1h[half, 1, :], a["L1_gnn_Wn1"][D:2 * D, :])
                    load(wn2h[half, :], a["L1_gnn_Wn2"])
                    load(g.bn1p[half, :], col(a["L1_gnn_bn1"]))
                load(bn2[:, :], row(a["L1_gnn_bn2"]).broadcast_to([3, D]))
                for b in range(2):
                    load(ws2[:, b, :], a["L2_gnn_W_self"])
                load(wg2[:, :, :], a["L2_gnn_W_groups"].rearrange("g o i -> o g i"))
                w3v = a["L3_gnn_W"].rearrange("r d f -> d r f")
                for b in range(2):
                    load(g.w3[b * D:(b + 1) * D, :].rearrange("p (r f) -> p r f", r=R), w3v)
                    load(ws3[b * D:(b + 1) * D, :], a["L3_gnn_W_self"])
                load(att3[0:D, :], a["L3_gnn_att_src"].rearrange("r f -> (r f)").rearrange("(a n) -> a n", a=1).broadcast_to([D, R * D]))
                load(att3[D:128, :], a["L3_gnn_att_dst"].rearrange("r f -> (r f)").rearrange("(a n) -> a n", a=1).broadcast_to([D, R * D]))
                load(brow[:, 0:D], row(a["L3_gnn_b_self"]).broadcast_to([3, D]))
                load(brow[:, D:], a["L3_gnn_bias"].rearrange("r f -> (r f)").rearrange("(a n) -> a n", a=1).broadcast_to([3, R * D]))

            @block.gpsimd
            def _(pool):
                pool_n.up(pool.memset(g.ones[:, :], 1.0))
                pool_n.up(pool.memset(g.ident[:, :], 0.0))
                pool_n.up(pool.memset(bd[:, :], 1.0))
                pool_n.up(pool.memset(shift[:, :], 0.0))
                pool_n.up(pool.iota(iot[:, :], pattern=[[1, LO]], base=0, channel_multiplier=0))
                pool_n.here(pool)
                pool_n.up(pool.affine_select(out=g.ident[:, :], in_=g.ident[:, :], compare_op=ALU.not_equal,
                                             fill=1.0, base=0, pattern=[[-1, 128]], channel_multiplier=1))
                pool_n.up(pool.affine_select(out=shift[:, :], in_=shift[:, :], compare_op=ALU.not_equal,
                                             fill=1.0, base=D, pattern=[[-1, 128]], channel_multiplier=1))
                pool_n.up(pool.affine_select(out=bd[:, :], in_=bd[:, :], compare_op=ALU.is_ge, fill=0.0, base=0,
                                             pattern=[[-HF, H]], channel_multiplier=1))
                pool_n.here(pool)
                pool_n.up(pool.affine_select(out=bd[:, :], in_=bd[:, :], compare_op=ALU.is_ge, fill=0.0,
                                             base=HF - 1, pattern=[[HF, H]], channel_multiplier=-1))

            steps = {}

            @block.vector
            def _(v):
                def up(ins):
                    v_n.up(ins)
                v.wait_ge(pc, PREP)
                v.wait_ge(ld, L[0])
                up(v.tensor_copy(g.identb[:, :], g.ident[:, :]))
                for k in range(3):
                    up(v.tensor_scalar(abd[:, k, :], bd[:, :], acol[:, k:k + 1], None, ALU.mult))
                v_n.here(v)
                up(v.tensor_tensor(wea[:, :, :], we[:, :].unsqueeze(1).broadcast_to([D, H, HF]),
                                   abd[:, 2, :].unsqueeze(2).broadcast_to([D, H, HF]), ALU.mult))
                up(v.tensor_copy(g.wa[:, :], wacol[:, 0:1].broadcast_to([D, D])))
                up(v.tensor_tensor(t3[:, :], g.w3[:, :], att3[:, :], ALU.mult))
                v_n.here(v)
                up(v.tensor_reduce(u3[:, 0:R], t3[:, :].rearrange("p (r f) -> p r f", r=R), AX.X, ALU.add))
                v_n.here(v)
                steps["small"] = v_n.n
                up(v.tensor_copy(g.rec[:, :, SRC], si[:, :]))
                up(v.tensor_copy(g.rec[:, :, DST], di[:, :]))
                up(v.tensor_copy(g.rec[:, :, TYPE], ti[:, :]))
                up(v.tensor_copy(g.label[:, :], lab_i[:, :]))
                up(v.tensor_tensor(ea3[:, :, :], ea3[:, :, :], ea3[:, :, :], ALU.mult))
                v_n.here(v)
                up(v.tensor_reduce(g.rec[:, :, RADIAL], ea3[:, :, :], AX.X, ALU.add))
                for s, idx in enumerate((di, si)):
                    up(v.tensor_scalar(hl[:, 2 * s, :], idx[:, :], 8, None, ALU.logical_shift_right))
                    up(v.tensor_scalar(hl[:, 2 * s + 1, :], idx[:, :], LO - 1, None, ALU.bitwise_and))
                up(v.memset(g.keys[:, :, EJ:], 0.0))
                up(v.tensor_copy(g.iota[:, :], iot[:, :]))
                up(v.tensor_copy(g.iotaf[:, :], iot[0:P, 0:R]))
                v_n.here(v)
                up(v.tensor_copy(g.keys[:, :, 0:EJ], hl[:, :, :]))
                v.wait_ge(tc, 3)
                up(v.tensor_copy(g.w0[0:D, 0:D], ps[0:D, 0:D]))
                up(v.tensor_scalar(g.w0[D:128, 0:D], ps[D:128, 0:D], -1.0, None, ALU.mult))
                up(v.tensor_copy(g.w0[0:D, D:D + H], ps2[0:D, 0:H]))
                up(v.tensor_copy(g.w0[D:128, D:D + H], ps2[D:128, H:2 * H]))
                up(v.memset(g.w0[0:D, D + H:], 0.0))
                up(v.tensor_copy(g.w0[D:128, D + H:], ps2[D:128, 0:H]))
                up(v.tensor_copy(wvb[:, :, :], ps3[0:P, 0:D].rearrange("p (h k) -> p h k", h=H)))
                up(v.memset(g.n1p[:, :], 0.0))
                v_n.here(v)
                up(v.tensor_copy(g.n1p[0:D, 0:D], ps[0:D, 0:D]))
                up(v.tensor_copy(g.n1p[D:128, D:], ps[D:128, 0:D]))
                v_n.here(v)
                up(v.tensor_tensor(g.w0[D:128, D + H:], g.w0[D:128, D + H:], g.w0[D:128, D:D + H], ALU.add))
                steps["ps_free"] = v_n.n
                for h in range(H):
                    up(v.tensor_tensor(tmp[:, :, :], ea[:, :, :],
                                       wvb[:, h, :].unsqueeze(1).broadcast_to([P, EJ, 16]), ALU.mult))
                    v_n.here(v)
                    up(v.tensor_reduce(g.rec[:, :, ATT + h], tmp[:, :, :], AX.X, ALU.add))
                    v_n.here(v)
                v.wait_ge(tc, 6)
                up(v.tensor_copy(g.wg[:, :], ps2[:, 0:D]))
                up(v.tensor_copy(half_w[:, 1, :], ps[:, 0:D]))
                up(v.tensor_copy(g.w3s[0:D, 0:R], u3[0:D, 0:R]))
                up(v.memset(g.w3s[0:D, R:], 0.0))
                up(v.tensor_copy(g.w3s[D:128, 0:R], u3[D:128, 0:R]))
                up(v.tensor_tensor(g.w3s[D:128, R:], ps3[D:128, 0:R], u3[D:128, 0:R], ALU.add))
                up(v.tensor_reduce(wsum[:, :], g.w3[:, :].rearrange("p (r f) -> p f r", r=R), AX.X, ALU.add))
                up(v.tensor_reduce(bsum[:, :], brow[:, :].rearrange("p (r f) -> p f r", r=R + 1), AX.X, ALU.add))
                up(v.tensor_copy(half_w[:, 0, :], wn2h[:, :]))
                v_n.here(v)
                up(v.tensor_tensor(half_w[:, 2, :], wsum[:, :], ws3[:, :], ALU.add))
                v_n.here(v)

                def centre(x, k, parts, count):
                    up(v.tensor_reduce(means[0:parts, k:k + count], x, AX.X, ALU.add))
                    v_n.here(v)
                    up(v.tensor_scalar(means[0:parts, k:k + count], means[0:parts, k:k + count], -1.0 / D, None, ALU.mult))
                    v_n.here(v)
                    up(v.tensor_tensor(x, x, means[0:parts, k:k + count].unsqueeze(2).broadcast_to([parts, count, D]),
                                       ALU.add))
                    v_n.here(v)

                centre(half_w[:, :, :], 0, 128, 3)
                centre(g.wg[:, :].unsqueeze(1), 3, 128, 1)
                centre(g.w3[:, :].rearrange("p (r f) -> p r f", r=R), 4, 128, R)
                centre(bsum[:, :].unsqueeze(1), 12, 3, 1)
                centre(bn2[:, :].unsqueeze(1), 13, 3, 1)
                up(v.tensor_scalar(g.w3[D:128, :], g.w3[D:128, :], -1.0, None, ALU.mult))
                for m in (g.wn1x, g.wn1g, g.wn2p, g.n3p, g.n4p):
                    up(v.memset(m[:, :], 0.0))
                v_n.here(v)
                for b in range(2):
                    half = slice(b * D, (b + 1) * D)
                    up(v.tensor_copy(g.wn1x[half, half], wn1h[half, 0, :]))
                    up(v.tensor_copy(g.wn1g[half, half], wn1h[half, 1, :]))
                    up(v.tensor_copy(g.wn2p[half, half], half_w[half, 0, :]))
                    up(v.tensor_tensor(g.n3p[half, half], half_w[half, 1, :], g.ident[half, half], ALU.add))
                    up(v.tensor_tensor(g.n4p[half, half], half_w[half, 2, :], g.ident[half, half], ALU.add))
                up(v.memset(g.onesb[:, :], 1.0))
                for m, x in ((g.b4c, bsum), (g.bn2c, bn2)):
                    up(v.memset(pieces[:, :], 0.0))
                    for k in range(3):
                        up(v.tensor_copy(piece[:, :], x[:, :]))
                        v_n.here(v)
                        up(v.scalar_tensor_tensor(pieces[:, :], piece[:, :], g.ident[0:3, k:k + 1], pieces[:, :],
                                                  ALU.mult, ALU.add))
                        up(v.tensor_tensor(x[:, :], x[:, :], piece[:, :], ALU.subtract))
                        v_n.here(v)
                    up(v.tensor_copy(m[:, :, :], pieces[:, :].unsqueeze(1).broadcast_to([3, NG, D])))
                    v_n.here(v)

            @block.tensor
            def _(t):
                t.wait_ge(pc, PREP)
                t.wait_ge(ld, L[0])
                t.wait_ge(vc, steps["small"])
                t_n.up(t.transpose(ps[:, 0:D], wd[:, :, :].rearrange("p b i -> p (b i)"), g.ident[0:D, 0:D]))
                t_n.up(t.matmul(ps2[:, 0:2 * H], wd[:, :, :].rearrange("p b i -> p (b i)"),
                                abd[:, 0:2, :].rearrange("p k h -> p (k h)"), start=True, stop=True))
                t_n.up(t.matmul(ps3[0:P, 0:D], g.ones[0:D, 0:P], wea[:, :, :].rearrange("p h k -> p (h k)"),
                                start=True, stop=True))
                t.wait_ge(vc, steps["ps_free"])
                t_n.up(t.transpose(ps2[:, 0:D], wg2[:, :, :].rearrange("p g i -> p (g i)"), g.ident[0:D, 0:D]))
                t_n.up(t.transpose(ps[:, 0:D], ws2[:, :, :].rearrange("p b i -> p (b i)"), g.ident[0:D, 0:D]))
                t_n.up(t.matmul(ps3[:, 0:R], shift[:, :], u3[0:D, 0:R], start=True, stop=True))


def histogram(g):
    sem = g.sem
    onehot, used, filled, zeroed = sem("hist_onehot"), sem("hist_used"), sem("hist_filled"), sem("hist_zeros")
    vc, tc = sem("base_vector"), sem("base_tensor")
    with ExitStack() as ctx:
        hi = [g.sb(f"h_hi{b}", [P, 2, 2 * HB], BF16, ctx) for b in range(2)]
        lo = [g.sb(f"h_lo{b}", [P, 2, LO], BF16, ctx) for b in range(2)]
        zero = g.sb("h_zero", [P, 512], BF16, ctx)
        incl = g.sb("incl", [HB, 2, 2, LO], F32, ctx)
        total = g.sb("row_total", [HB, 2, 2], F32, ctx)
        prev = g.sb("row_prev", [HB, 2, 2], F32, ctx)
        before = g.sb("before", [HB, HB], F32, ctx)
        cnt = [g.ps(f"count{s}", [HB, 512], F32, ctx) for s in range(2)]
        rows = g.ps("rows", [HB, 4], F32, ctx)
        with g.nc.Block() as block:
            @block.vector
            def _(v):
                v.memset(zero[:, :], 0.0).then_inc(zeroed, 1)
                v.sem_inc(used, 2)
                with v.Fori(0, EJ // 2) as i:
                    for b in range(2):
                        j = i * 2 + b
                        v.wait_ge(used, j + 1)
                        for s in range(2):
                            v.tensor_scalar(hi[b][:, s, :], g.iota[:, 0:2 * HB],
                                            g.keys[:, 2 * s, bass.ds(j, 1)], None, ALU.is_equal)
                            last = v.tensor_scalar(lo[b][:, s, :], g.iota[:, :],
                                                   g.keys[:, 2 * s + 1, bass.ds(j, 1)], None, ALU.is_equal)
                        last.then_inc(onehot, 1)
                n = Count(vc)
                n.up(v.memset(prev[:, :, :], 0.0))
                v.wait_ge(filled, 1)
                n.here(v)
                for s in range(2):
                    for h in range(2):
                        n.up(v.tensor_tensor_scan(incl[:, s, h, :], g.ones[0:HB, 0:1].broadcast_to([HB, LO]),
                                                  cnt[s][:, h * LO:(h + 1) * LO], 0.0, ALU.mult, ALU.add))
                n.here(v)
                n.up(v.tensor_copy(total[:, :, :], incl[:, :, :, LO - 1]))
                n.here(v)
                n.up(v.tensor_copy(prev[:, :, 1], total[:, :, 0]))
                v.wait_ge(tc, 1)
                for s in range(2):
                    n.up(v.tensor_tensor(g.base[:, s, :], incl[:, s, :, :].rearrange("p h l -> p (h l)"),
                                         cnt[s][:, :], ALU.subtract))
                n.here(v)
                for s in range(2):
                    for h in range(2):
                        k = 2 * s + h
                        n.up(v.tensor_scalar(g.base[:, s, h * LO:(h + 1) * LO],
                                             g.base[:, s, h * LO:(h + 1) * LO], rows[:, k:k + 1], None, ALU.add))

            @block.gpsimd
            def _(pool):
                n = Count(g.sem("before_mask"))
                n.up(pool.memset(before[:, :], 1.0))
                n.here(pool)
                n.up(pool.affine_select(out=before[:, :], in_=before[:, :], compare_op=ALU.is_gt, fill=0.0,
                                        base=0, pattern=[[1, HB]], channel_multiplier=-1))
                g.before_sem = n.sem
                n.up(pool.memset(g.strict[:, :], 1.0))
                n.here(pool)
                n.up(pool.affine_select(out=g.strict[:, :], in_=g.strict[:, :], compare_op=ALU.is_gt, fill=0.0,
                                        base=0, pattern=[[1, P]], channel_multiplier=-1))

            @block.tensor
            def _(t):
                t.wait_ge(zeroed, 1)
                for s in range(2):
                    t.matmul(cnt[s][:, :], zero[:, 0:HB], zero[:, :], start=True, stop=False,
                             skip_group_check=True)
                with t.Fori(0, EJ // 2) as i:
                    for b in range(2):
                        t.wait_ge(onehot, i * 2 + b + 1)
                        for s in range(2):
                            for h in range(2):
                                last = t.matmul(cnt[s][:, h * LO:(h + 1) * LO], hi[b][:, s, h * HB:(h + 1) * HB],
                                                lo[b][:, s, :], start=False, stop=False, skip_group_check=True)
                        last.then_inc(used, 1)
                for s in range(2):
                    last = t.matmul(cnt[s][:, :], zero[:, 0:HB], zero[:, :], start=False, stop=True,
                                    skip_group_check=True)
                last.then_inc(filled, 1)
                t.wait_ge(g.before_sem, 2)
                t.wait_ge(vc, 7)
                t.matmul(rows[:, :], before[:, :], total[:, :, :].rearrange("p s h -> p (s h)"),
                         start=True, stop=False)
                t.matmul(rows[:, :], g.ones[0:HB, 0:HB], prev[:, :, :].rearrange("p s h -> p (s h)"),
                         start=False, stop=True).then_inc(tc, 1)


def rank_and_scatter(g):
    sem = g.sem
    two = lambda n: [sem(f"{n}{s}") for s in range(2)]
    onehot, placed, summed = sem("rank_onehot"), sem("rank_placed"), sem("rank_summed")
    turned, turned_out, same, masked = sem("rank_turned"), sem("rank_turned_out"), sem("rank_same"), sem("rank_masked")
    table_up, table_out, looked = two("table_up"), two("table_out"), two("rank_looked")
    staged, sent = sem("rank_staged"), [g.once(f"rank_sent{b}") for b in range(2)]
    zeroed, cleared = sem("zero_rows_made"), sem("aggregates_cleared")
    RC = 4
    with ExitStack() as ctx:
        hi = [g.sb(f"r_hi{b}", [P, 2, 2 * HB], BF16, ctx) for b in range(2)]
        lo = [g.sb(f"r_lo{b}", [P, 2, LO], BF16, ctx) for b in range(2)]
        hit = [g.sb(f"hi_t{b}", [HB, 2, 2, P], F32, ctx) for b in range(2)]
        hitb = g.sb("hi_tb", [HB, 2, 2, P], BF16, ctx)
        tab = [[g.sb(f"tab_sb{s}{b}", [HB, 512], F32, ctx) for b in range(2)] for s in range(2)]
        eq = g.sb("eq", [P, 2, P], BF16, ctx)
        junk = g.sb("rank_junk", [P, LO], F32, ctx)
        one = g.sb("one_place", [P, 2, 2], F32, ctx)
        place = g.sb("place", [P, EJ, 2], F32, ctx)
        pidx = [g.sb(f"pidx{b}", [P, 2, RC], I32, ctx) for b in range(2)]
        stage = [g.sb(f"rstage{b}", [P, RC, REC], F32, ctx) for b in range(2)]
        zero = g.sb("zero_rows", [P, 512], F32, ctx)
        t_ps = g.ps("hit_ps", [HB, 2, 2, 128], BF16, ctx)
        e_ps = g.ps("eq_ps", [P, 2, P], F32, ctx)
        l_ps = [[g.ps(f"look_ps{s}{b}", [P, LO], F32, ctx) for b in range(2)] for s in range(2)]
        tab_ps = [g.ps(f"tab_ps{s}", [HB, 512], F32, ctx) for s in range(2)]
        with g.nc.Block() as block:
            @block.vector
            def _(v):
                n = Count(zeroed)
                n.up(v.memset(zero[:, :], 0.0))
                v.sem_inc(placed, 2)

                def onehots(b, j):
                    for s in range(2):
                        v.tensor_scalar(hi[b][:, s, :], g.iota[:, 0:2 * HB],
                                        g.keys[:, 2 * s, bass.ds(j, 1)], None, ALU.is_equal)
                        v.tensor_scalar(lo[b][:, s, :], g.iota[:, :],
                                        g.keys[:, 2 * s + 1, bass.ds(j, 1)], None, ALU.is_equal
                                        ).then_inc(onehot, 1)

                def mask():
                    v.tensor_tensor(eq[:, :, :], e_ps[:, :, :], g.strict[:, :].unsqueeze(1).broadcast_to([P, 2, P]),
                                    ALU.mult).then_inc(masked, 1)

                onehots(0, 0)
                v.wait_ge(same, 1)
                mask()
                with v.Fori(0, EJ // 2) as i:
                    for b in range(2):
                        j = i * 2 + b
                        for s in range(2):
                            v.wait_ge(looked[s], j + 1)
                        onehots(1 - b, j + 1)
                        for s in range(2):
                            v.wait_ge(looked[s], j + 2)
                            v.tensor_tensor_reduce(junk[:, :], l_ps[s][b][:, :], lo[b][:, s, :], 1.0, 0.0,
                                                   ALU.mult, ALU.add, one[:, b, s:s + 1]).then_inc(summed, 1)
                            v.wait_ge(summed, j * 2 + s + 1)
                        v.tensor_copy(place[:, bass.ds(j, 1), :], one[:, b, :].unsqueeze(1)).then_inc(placed, 1)
                        v.wait_ge(same, j + 2)
                        mask()

            @block.tensor
            def _(t):
                for s in range(2):
                    t.matmul(tab_ps[s][:, :], g.ident[0:HB, 0:HB], g.base[:, s, :], start=True, stop=False,
                             skip_group_check=True).then_inc(table_up[s], 1)
                    t.sem_inc(looked[s], 1)

                def turn(b):
                    for s in range(2):
                        for h in range(2):
                            last = t.transpose(t_ps[:, s, h, 0:P], hi[b][:, s, h * HB:(h + 1) * HB], g.identb[0:P, 0:P])
                    last.then_inc(turned, 1)

                def match():
                    for s in range(2):
                        for h in range(2):
                            last = t.matmul(e_ps[:, s, :], hitb[:, s, h, :], hitb[:, s, h, :], start=(h == 0), stop=(h == 1))
                    last.then_inc(same, 1)

                t.wait_ge(onehot, 2)
                turn(0)
                t.wait_ge(turned_out, 2)
                match()
                with t.Fori(0, EJ // 2) as i:
                    for b in range(2):
                        j = i * 2 + b
                        for s in range(2):
                            t.wait_ge(table_out[s], j + 1)
                            for h in range(2):
                                last = t.matmul(tab_ps[s][:, h * LO:(h + 1) * LO],
                                                hi[b][:, s, h * HB:(h + 1) * HB], lo[b][:, s, :],
                                                start=False, stop=False, skip_group_check=True)
                            last.then_inc(table_up[s], 1)
                        t.wait_ge(onehot, j * 2 + 4)
                        turn(1 - b)
                        t.wait_ge(placed, j + 1)
                        for s in range(2):
                            t.matmul(l_ps[s][b][:, :], hit[b][:, s, 0, :], tab[s][b][:, 0:LO], start=True, stop=False)
                            t.matmul(l_ps[s][b][:, :], hit[b][:, s, 1, :], tab[s][b][:, LO:], start=False, stop=False)
                            t.wait_ge(masked, j + 1)
                            t.matmul(l_ps[s][b][:, :], eq[:, s, :], lo[b][:, s, :], start=False, stop=True
                                     ).then_inc(looked[s], 1)
                        t.wait_ge(turned_out, j * 2 + 4)
                        match()

            @block.scalar
            def _(a):
                def copy_turned(b):
                    part = t_ps[:, :, :, 0:P]
                    a.activation(hit[b][:, :, :, :], part, ACT.Copy).then_inc(turned_out, 1)
                    a.activation(hitb[:, :, :, :], part, ACT.Copy).then_inc(turned_out, 1)

                def copy_table(s, b):
                    a.activation(tab[s][b][:, :], tab_ps[s][:, :], ACT.Copy).then_inc(table_out[s], 1)

                for s in range(2):
                    a.wait_ge(table_up[s], 1)
                    copy_table(s, 0)
                a.wait_ge(turned, 1)
                copy_turned(0)
                with a.Fori(0, EJ // 2) as i:
                    for b in range(2):
                        j = i * 2 + b
                        for s in range(2):
                            a.wait_ge(table_up[s], j + 2)
                            a.wait_ge(looked[s], j + 1)
                            copy_table(s, 1 - b)
                        a.wait_ge(turned, j + 2)
                        copy_turned(1 - b)

            @block.gpsimd
            def _(pool):
                n = LoopCount(staged, 6, g=g)
                with pool.Fori(0, EJ // (2 * RC)) as i:
                    for b in range(2):
                        c = i * 2 + b
                        pool.wait_ge(placed, c * RC + (RC + 2))
                        g.passed(pool)
                        pool.wait_ge(sent[b], i * (32 * RC))
                        g.passed(pool)
                        for s in range(2):
                            n.up(pool.tensor_copy(pidx[b][:, s, :], place[:, bass.ds(c * RC, RC), s]))
                        n.up(pool.tensor_copy(stage[b][:, :, :], g.rec[:, bass.ds(c * RC, RC), :]))
                        n.here(pool, i)
                        for s in range(2):
                            for k in range(RC):
                                pool.indirect_dma_start(
                                    out=g.sorted[s][:, :],
                                    out_offset=bass.IndirectOffsetOnAxis(ap=pidx[b][:, s, k:k + 1], axis=0),
                                    in_=stage[b][:, k, :], in_offset=None,
                                    bounds_check=E - 1, oob_is_err=False).then_inc(sent[b], 16)
                for b in range(2):
                    pool.wait_ge(sent[b], EJ * 16)

            @block.sync
            def _(sp):
                sp.wait_ge(zeroed, 1)
                for aggr in g.aggr:
                    sp.dma_start(aggr.rearrange("(p a k) d -> p a (k d)", p=P, k=512 // D),
                                 zero[:, :].unsqueeze(1).broadcast_to([P, NK * D // 512, 512])).then_inc(cleared, 16)
                sp.wait_ge(cleared, 16 * len(g.aggr))


def read_orders(g):
    ld, pc, vc = g.sem("orders_loaded"), g.sem("orders_pool"), g.sem("orders_vector")
    with ExitStack() as ctx:
        nxt = [g.sb(f"next{s}", [P, 1], F32, ctx) for s in range(2)]
        prv = [g.sb(f"prev{s}", [P, 1], F32, ctx) for s in range(2)]
        rec = [g.sb(f"sorted_rec{s}", [P, EJ, REC], F32, ctx) for s in range(2)]
        same = g.sb("same_next", [P, EJ], F32, ctx)
        rowf = g.sb("rowf", [P, EJ], F32, ctx)
        with g.nc.Block() as block:
            @block.gpsimd
            def _(pool):
                for s in range(2):
                    pool.memset(nxt[s][:, :], -1.0).then_inc(pc, 1)
                    pool.memset(prv[s][:, :], -1.0).then_inc(pc, 1)

            @block.sync
            def _(sp):
                sp.wait_ge(pc, 4)
                for s, f in ((0, DST), (1, SRC)):
                    flat = g.sorted[s].rearrange("(p j) r -> p j r", p=P)
                    sp.dma_start(rec[s][:, :, :], flat).then_inc(ld, 16)
                    sp.dma_start(prv[s][1:P, :], flat[0:P - 1, EJ - 1, f:f + 1],
                                 allow_slow_non_contiguous=True).then_inc(ld, 16)
                    sp.dma_start(nxt[s][0:P - 1, :], flat[1:P, 0, f:f + 1],
                                 allow_slow_non_contiguous=True).then_inc(ld, 16)

            @block.vector
            def _(v):
                n = Count(vc)
                v.wait_ge(ld, 96)
                for s, f in ((0, DST), (1, SRC)):
                    key = rec[s][:, :, f]
                    for k, e in ((0, SRC), (1, DST)):
                        n.up(v.tensor_copy(g.ends_of[s][:, k, :], rec[s][:, :, e]))
                    n.up(v.tensor_tensor(g.cont[s][:, 1:], key[:, 1:], key[:, 0:EJ - 1], ALU.is_equal))
                    n.up(v.tensor_tensor(g.cont[s][:, 0:1], key[:, 0:1], prv[s][:, :], ALU.is_equal))
                    n.here(v)
                    n.up(v.tensor_tensor(same[:, 0:EJ - 1], key[:, 0:EJ - 1], key[:, 1:], ALU.is_equal))
                    n.up(v.tensor_tensor(same[:, EJ - 1:], key[:, EJ - 1:], nxt[s][:, :], ALU.is_equal))
                    n.here(v)
                    n.up(v.scalar_tensor_tensor(rowf[:, :], same[:, :], SKIP, key, ALU.mult, ALU.add))
                    if s == 0:
                        n.up(v.tensor_copy(g.goes_on[:, :], same[:, :]))
                    n.here(v)
                    n.up(v.tensor_copy(g.out_row[s][:, :], rowf[:, :]))
                    n.up(v.tensor_tensor_scan(g.open[s][:, :], g.cont[s][:, :], g.ones[0:P, 0:1].broadcast_to([P, EJ]),
                                              1.0, ALU.mult, ALU.mult))
                    n.here(v)
                n.up(v.tensor_copy(g.etype[:, :], rec[0][:, :, TYPE]))
                n.up(v.tensor_copy(g.radial[:, :], rec[1][:, :, RADIAL]))
                n.up(v.tensor_copy(g.attn[:, :, :], rec[0][:, :, ATT:ATT + H].rearrange("p j h -> p h j")))
                n.here(v)


def gather(pool, g, rows, table, i, b, c, idx, dst, free, ready, n, sides, width=D):
    pool.wait_ge(free, c + 1)
    g.passed(pool)
    for k in range(sides):
        n.up(pool.tensor_copy(idx[:, k, :], rows[:, k, bass.ds(c * G, G)]))
    n.here(pool, i)
    for t in range(G):
        for k in range(sides):
            pool.indirect_dma_start(out=dst[:, t, k * width:(k + 1) * width], out_offset=None, in_=table,
                                    in_offset=bass.IndirectOffsetOnAxis(ap=idx[:, k, t:t + 1], axis=0),
                                    bounds_check=N - 1, oob_is_err=False).then_inc(ready[b], 16)


def edges(g, layer):
    sem = lambda n: g.sem(f"{n}_e")
    row_free, row_ready, copied = sem("rows_free"), [g.once(f"rows_ready{b}_e{layer}") for b in range(2)], sem("idx_copied")
    turned, turned_out, turned_free = sem("turned"), sem("turned_out"), sem("turned_free")
    made, made_free = sem("made"), sem("made_free")
    order = 1 if layer == 1 else 0
    sides = 1 if layer == 2 else 2
    with ExitStack() as ctx:
        sb = lambda n, s, d=F32: g.sb(f"{n}_e{layer}", s, d, ctx)
        ps = lambda n, s, d=F32: g.ps(f"{n}_e{layer}", s, d, ctx)
        idx = [sb(f"idx{b}", [P, 2, G], I32) for b in range(2)]
        rows = [sb(f"rows{b}", [P, G, 2 * D]) for b in range(2)]
        xt = [sb(f"xt{b}", [128, G * P]) for b in range(2)]
        tp = [ps(f"tp{b}", [128, G * P]) for b in range(2)]
        table = g.labelled if layer == 2 else g.feat[layer]
        if layer == 0:
            W = D + 2 * H
            out = [ps(f"out{b}", [P, G, W]) for b in range(2)]
        if layer == 1:
            out = [ps(f"out{b}", [P, G, D]) for b in range(2)]
            h_ps = [ps(f"h{k}", [D, G * P]) for k in range(3)]
            s_sb = [sb(f"s{k}", [D, G * P]) for k in range(3)]
            msg = sb("msg", [D, G * P])
            diag = [sb(f"diag{b}", [P, G, P]) for b in range(2)]
            hidden, hidden_out, diag_ready, msg_ready = sem("hidden"), sem("hidden_out"), sem("diag"), sem("msg")
        if layer == 2:
            lrow = [sb(f"lrow{b}", [P, G, g.LW]) for b in range(2)]
            pick = sb("pick", [P, 2, G])
            out = [ps(f"out{b}", [P, G, D]) for b in range(2)]
            masked, picked = sem("masked"), sem("picked")
        if layer == 3:
            hr = [ps(f"hr{b}", [P, R * D]) for b in range(2)]
            sc = [ps(f"sc{b}", [P, G, 2 * R]) for b in range(2)]
            prod = [sb(f"prod{b}", [P, R * D]) for b in range(2)]
            pick = [sb(f"pick{b}", [P, G, R]) for b in range(2)]
            psc = sb("psc", [P, 2, G, R])
            hr_ready, hr_free, step = sem("hr_ready"), sem("hr_free"), sem("select_steps")

        with g.nc.Block() as block:
            @block.gpsimd
            def _(pool):
                n = LoopCount(copied, 2 * sides, g=g)
                with pool.Fori(0, CH // 2) as i:
                    for b in range(2):
                        gather(pool, g, g.ends_of[order], table, i, b, i * 2 + b, idx[b], rows[b] if layer != 2 else lrow[b],
                               row_free, row_ready, n, sides, D if layer != 2 else g.LW)

            @block.tensor
            def _(t):
                if layer != 2:
                    t.sem_inc(row_free, 2)
                t.sem_inc(turned_free, 2)
                with t.Fori(0, CH // 2) as i:
                    for b in range(2):
                        c = i * 2 + b
                        if layer == 2:
                            t.wait_ge(masked, c + 1)
                        else:
                            t.wait_ge(row_ready[b], i * (32 * G) + 32 * G)
                        for k in range(G):
                            last = t.transpose(tp[b][:, k * P:(k + 1) * P], rows[b][:, k, :], g.ident[0:P, 0:P])
                        last.then_inc(turned, 1)
                        if layer != 2:
                            t.wait_ge(turned, c + 1)
                            t.sem_inc(row_free, 1)
                        t.wait_ge(turned_out, c + 1)
                        if layer == 0:
                            t.wait_ge(made_free, c + 1)
                            for k in range(G):
                                last = t.matmul(out[b][:, k, :], xt[b][:, k * P:(k + 1) * P], g.w0[:, :],
                                                start=True, stop=True)
                            last.then_inc(made, 1)
                            t.wait_ge(made, c + 1)
                            t.sem_inc(turned_free, 1)
                        if layer == 1:
                            t.wait_ge(diag_ready, c + 1)
                            t.matmul(h_ps[0][:, :], g.w1a[:, :], xt[b][:, :], start=True, stop=False)
                            t.matmul(h_ps[0][:, :], g.w1r[:, :], diag[b][:, :, :].rearrange("p k e -> p (k e)"),
                                     start=False, stop=True).then_inc(hidden, 1)
                            t.wait_ge(hidden, c * 3 + 1)
                            t.sem_inc(turned_free, 1)
                            for k, w in ((1, g.w2), (2, g.wa)):
                                t.wait_ge(hidden_out, c * 3 + k)
                                g.passed(t)
                                t.matmul(h_ps[k][:, :], w[:, :], s_sb[k - 1][:, :], start=True, stop=True
                                         ).then_inc(hidden, 1)
                            t.wait_ge(msg_ready, c + 1)
                            t.wait_ge(made_free, c + 1)
                            g.passed(t)
                            for k in range(G):
                                last = t.transpose(out[b][:, k, :], msg[:, k * P:(k + 1) * P], g.ident[0:D, 0:D])
                            last.then_inc(made, 1)
                        if layer == 2:
                            t.wait_ge(made_free, c + 1)
                            for k in range(G):
                                last = t.matmul(out[b][:, k, :], xt[b][:, k * P:(k + 1) * P], g.wg[:, :],
                                                start=True, stop=True)
                            last.then_inc(made, 1)
                            t.wait_ge(made, c + 1)
                            t.sem_inc(turned_free, 1)
                        if layer == 3:
                            t.wait_ge(made_free, c + 1)
                            for k in range(G):
                                last = t.matmul(sc[b][:, k, :], xt[b][:, k * P:(k + 1) * P], g.w3s[:, :],
                                                start=True, stop=True)
                            last.then_inc(made, 1)
                            for k in range(G):
                                t.wait_ge(hr_free, c * G + k + 1)
                                t.matmul(hr[k % 2][:, :], xt[b][:, k * P:(k + 1) * P], g.w3[:, :],
                                         start=True, stop=True).then_inc(hr_ready, 1)
                            t.wait_ge(hr_ready, c * G + G)
                            t.sem_inc(turned_free, 1)

            @block.scalar
            def _(a):
                with a.Fori(0, CH // 2) as i:
                    for b in range(2):
                        c = i * 2 + b
                        a.wait_ge(turned, c + 1)
                        a.wait_ge(turned_free, c + 1)
                        a.activation(xt[b][:, :], tp[b][:, :], ACT.Copy).then_inc(turned_out, 1)
                        if layer == 1:
                            for k, (bias, func) in enumerate(((g.be1, ACT.Silu), (g.be2, ACT.Silu), (g.ba, ACT.Sigmoid))):
                                a.wait_ge(hidden, c * 3 + k + 1)
                                if k > 0:
                                    a.wait_ge(msg_ready, c)
                                a.activation(s_sb[k][:, :], h_ps[k][:, :], func, bias=bias[:, 0:1]
                                             ).then_inc(hidden_out, 1)

            @block.vector
            def _(v):
                v.sem_inc(made_free, 2)
                if layer == 2:
                    v.sem_inc(row_free, 2)
                if layer == 3:
                    v.sem_inc(hr_free, 2)
                    n = LoopCount(step, 2 * (3 + 2 * G))
                if layer == 2:
                    n = LoopCount(picked, 4)
                with v.Fori(0, CH // 2) as i:
                    for b in range(2):
                        c = i * 2 + b
                        at = bass.ds(c * G, G)
                        if layer == 1:
                            v.tensor_tensor(diag[b][:, :, :], g.ident[0:P, 0:P].unsqueeze(1).broadcast_to([P, G, P]),
                                            g.radial[:, at].unsqueeze(2).broadcast_to([P, G, P]), ALU.mult
                                            ).then_inc(diag_ready, 1)
                            v.wait_ge(hidden_out, c * 3 + 3)
                            v.wait_ge(made, c)
                            v.tensor_tensor(msg[:, :], s_sb[1][:, :], s_sb[2][:, :], ALU.mult).then_inc(msg_ready, 1)
                        if layer == 2:
                            v.wait_ge(row_ready[b], i * (16 * G) + 16 * G)
                            v.wait_ge(turned, c)
                            for k in range(2):
                                n.up(v.tensor_scalar(pick[:, k, :], lrow[b][:, :, D], float(k), None, ALU.is_equal))
                            n.here(v, i)
                            for k in range(2):
                                last = v.tensor_tensor(rows[b][:, :, k * D:(k + 1) * D], lrow[b][:, :, 0:D],
                                                       pick[:, k, :].unsqueeze(2).broadcast_to([P, G, D]), ALU.mult)
                            last.then_inc(masked, 1)
                            v.wait_ge(masked, c + 1)
                            v.sem_inc(row_free, 1)
                        v.wait_ge(made, c + 1)
                        if layer == 0:
                            v.tensor_copy(g.val[:, at, :], out[b][:, :, 0:D])
                            v.tensor_copy(g.score[:, :, at], out[b][:, :, D:].rearrange("p j h -> p h j")
                                          ).then_inc(made_free, 1)
                        if layer in (1, 2):
                            v.tensor_copy(g.val[:, at, :], out[b][:, :, :]).then_inc(made_free, 1)
                        if layer == 3:
                            n.up(v.tensor_tensor(pick[b][:, :, :], g.iotaf[:, 0:R].unsqueeze(1).broadcast_to([P, G, R]),
                                                 g.etype[:, at].unsqueeze(2).broadcast_to([P, G, R]), ALU.is_equal))
                            n.here(v, i)
                            for k in range(2):
                                last = v.tensor_tensor(psc[:, k, :, :], sc[b][:, :, k * R:(k + 1) * R],
                                                       pick[b][:, :, :], ALU.mult)
                            n.up(last)
                            n.here(v, i)
                            v.sem_inc(made_free, 1)
                            n.up(v.tensor_reduce(g.score[:, 0:2, at], psc[:, :, :, :], AX.X, ALU.add))
                            for k in range(G):
                                v.wait_ge(hr_ready, c * G + k + 1)
                                n.up(v.tensor_tensor(prod[k % 2][:, :].rearrange("p (r f) -> p r f", r=R),
                                                     hr[k % 2][:, :].rearrange("p (r f) -> p r f", r=R),
                                                     pick[b][:, k, :].unsqueeze(2).broadcast_to([P, R, D]),
                                                     ALU.mult))
                                n.here(v, i)
                                v.sem_inc(hr_free, 1)
                                n.up(v.tensor_reduce(g.val[:, bass.ds(c * G + k, 1), :].rearrange("p a f -> p (a f)"),
                                                     prod[k % 2][:, :].rearrange("p (r f) -> p f r", r=R),
                                                     AX.X, ALU.add))
                                n.here(v, i)


def carry_on(eng, n, turned, g, k, A, B, C, out, a_sb, row, a_ps, b_ps, c_ps, op0, op1, init, back=False):
    n.here(eng)
    g.carries.append(n.n)
    eng.wait_ge(turned, 2 * k + 1)
    n.up(eng.tensor_copy(a_sb[0:C, :], a_ps[0:C, 0:P]))
    n.up(eng.memset(row[0:C, :], init))
    n.here(eng)
    if back:
        n.up(eng.tensor_tensor_scan(row[0:C, P - 1::-1], a_sb[0:C, P - 1::-1], b_ps[0:C, P - 1::-1],
                                    init, op0, op1))
    else:
        n.up(eng.tensor_tensor_scan(row[0:C, 1:P + 1], a_sb[0:C, :], b_ps[0:C, 0:P], init, op0, op1))
    g.carries.append(n.n)
    eng.wait_ge(turned, 2 * k + 2)
    n.up(eng.tensor_copy(out, c_ps[0:P, 0:C]))
    n.here(eng)


def turn_carries(t, g, vec, turned, sizes, A, B, row, a_ps, b_ps, c_ps):
    for k, (C, back) in enumerate(sizes):
        t.wait_ge(vec, g.carries[2 * k])
        t.transpose(a_ps[0:C, 0:P], A[:, 0:C], g.ident[0:P, 0:P])
        t.transpose(b_ps[0:C, 0:P], B[:, 0:C], g.ident[0:P, 0:P]).then_inc(turned, 1)
        t.wait_ge(vec, g.carries[2 * k + 1])
        off = 1 if back else 0
        t.transpose(c_ps[0:P, 0:C], row[0:C, off:off + P], g.ident[0:C, 0:C]).then_inc(turned, 1)


def segments(g, layer):
    order = 1 if layer == 1 else 0
    vec, sca, ten, scans = [g.sem(f"{n}_m") for n in ("vector", "scalar", "tensor", "scans")]
    g.carries = []
    BC = lambda ap, *s: ap.broadcast_to(list(s))
    with ExitStack() as ctx:
        sb = lambda n, s, d=F32: g.sb(f"{n}_m{layer}", s, d, ctx)
        A, B, a_sb, row = sb("A", [P, D]), sb("B", [P, D]), sb("a_sb", [D, P]), sb("row", [D, P + 1])
        a_ps, b_ps, c_ps = [g.ps(f"{n}_m{layer}", [128, 128], F32, ctx) for n in ("a_ps", "b_ps", "c_ps")]
        cont, opn = g.cont[order], g.open[order]
        if layer == 0:
            C = H
            lm, es, m, d = sb("lm", [P, C, EJ]), sb("es", [P, C, EJ]), sb("m", [P, C, EJ + 1]), sb("d", [P, C, EJ])
            w, wself, fac, z, cm = (sb("w", [P, C, EJ]), sb("ws", [P, C, EJ]), sb("fac", [P, C, EJ]),
                                    sb("z", [P, C, EJ]), sb("cm", [P, C]))
            drop, lowered, first = sb("drop", [P, EJ]), sb("lowered", [P, EJ]), sb("first", [P, EJ])
            sizes = [(H, False), (H, False), (D, False)]
        if layer == 3:
            C = R
            mask, neg, y = sb("mask", [P, R, EJ]), sb("neg", [P, R, EJ]), sb("y", [P, R, EJ])
            f = sb("f", [P, R, EJ])
            lm, es, sel = sb("lm", [P, EJ]), sb("es", [P, EJ]), sb("sel", [P, EJ])
            w, drop, lowered, cm = sb("w", [P, EJ]), sb("drop", [P, EJ]), sb("lowered", [P, EJ]), sb("cm", [P, R])
            ends, cback = sb("ends", [P, EJ]), sb("cback", [P, R])
            openb = sb("openb", [P, EJ])
            sizes = [(R, False), (R, True), (R, False), (R, True), (D, False)]
        if layer in (1, 2):
            sizes = [(D, False)]

        with g.nc.Block() as block:
            @block.vector
            def _(v):
                n = Count(vec)
                acts = [0]

                def scalar_done():
                    acts[0] += 1
                    v.wait_ge(sca, acts[0])

                def up(ins):
                    n.up(ins)
                    n.here(v)

                def carry(out, Cn, op0, op1, init, back=False):
                    k = len(g.carries) // 2
                    carry_on(v, n, ten, g, k, A, B, Cn, out, a_sb, row, a_ps, b_ps, c_ps, op0, op1, init, back)

                def leaky(out, ap, slope):
                    up(v.scalar_tensor_tensor(out, ap, slope, ap, ALU.mult, ALU.max))

                if layer == 0:
                    up(v.tensor_tensor(lm[:, :, :], g.score[:, 0:H, :], g.attn[:, :, :], ALU.add))
                    leaky(lm[:, :, :], lm[:, :, :], 0.01)
                    leaky(es[:, :, :], g.score[:, H:, :], 0.01)
                    up(v.tensor_tensor(d[:, :, :], lm[:, :, :], es[:, :, :], ALU.max))
                    up(v.tensor_scalar(drop[:, :], cont[:, :], 1.0, BIG, ALU.subtract, ALU.mult))
                    up(v.tensor_scalar(lowered[:, :], opn[:, :], 1.0, BIG, ALU.subtract, ALU.mult))
                    up(v.tensor_scalar(first[:, :], cont[:, :], -1.0, 1.0, ALU.mult, ALU.add))
                    for h in range(H):
                        up(v.tensor_tensor_scan(m[:, h, 1:], drop[:, :], d[:, h, :], -BIG, ALU.add, ALU.max))
                    up(v.tensor_copy(A[:, 0:H], BC(lowered[:, EJ - 1:], P, H)))
                    up(v.tensor_copy(B[:, 0:H], m[:, :, EJ]))
                    carry(cm[:, :], H, ALU.add, ALU.max, -BIG)
                    for h in range(H):
                        up(v.scalar_tensor_tensor(m[:, h, 1:], lowered[:, :], cm[:, h:h + 1], m[:, h, 1:],
                                                  ALU.add, ALU.max))
                    up(v.tensor_copy(m[:, :, 0], cm[:, :]))
                    up(v.tensor_tensor(fac[:, :, :], m[:, :, 0:EJ], m[:, :, 1:], ALU.subtract))
                    up(v.tensor_scalar(fac[:, :, :], fac[:, :, :], 0.0, None, ALU.min))
                    up(v.tensor_tensor(w[:, :, :], lm[:, :, :], m[:, :, 1:], ALU.subtract))
                    up(v.tensor_tensor(wself[:, :, :], es[:, :, :], m[:, :, 1:], ALU.subtract))
                    g.exp_in = n.n
                    scalar_done()
                    up(v.tensor_tensor(fac[:, :, :], fac[:, :, :], BC(cont[:, :].unsqueeze(1), P, H, EJ), ALU.mult))
                    up(v.tensor_tensor(d[:, :, :], wself[:, :, :], BC(first[:, :].unsqueeze(1), P, H, EJ), ALU.mult))
                    up(v.tensor_tensor(d[:, :, :], d[:, :, :], w[:, :, :], ALU.add))
                    for h in range(H):
                        up(v.tensor_tensor_scan(z[:, h, :], fac[:, h, :], d[:, h, :], 0.0, ALU.mult, ALU.add))
                        up(v.tensor_tensor_scan(g.reach[:, h, :], fac[:, h, :], BC(g.ones[0:P, 0:1], P, EJ),
                                                1.0, ALU.mult, ALU.mult))
                    up(v.tensor_copy(A[:, 0:H], g.reach[:, :, EJ - 1]))
                    up(v.tensor_copy(B[:, 0:H], z[:, :, EJ - 1]))
                    carry(cm[:, :], H, ALU.mult, ALU.add, 0.0)
                    for h in range(H):
                        up(v.scalar_tensor_tensor(z[:, h, :], g.reach[:, h, :], cm[:, h:h + 1], z[:, h, :],
                                                  ALU.mult, ALU.add))
                    up(v.reciprocal(g.rz[:, :, :], z[:, :, :]))
                    for h in range(H):
                        part = g.val[:, :, h * HF:(h + 1) * HF]
                        up(v.tensor_tensor(part, part, BC(w[:, h, :].unsqueeze(2), P, EJ, HF), ALU.mult))
                if layer == 3:
                    leaky(lm[:, :], g.score[:, 0, :], 0.2)
                    leaky(es[:, :], g.score[:, 1, :], 0.2)
                    up(v.tensor_tensor(sel[:, :], lm[:, :], es[:, :], ALU.max))
                    up(v.tensor_tensor(mask[:, :, :], BC(g.iotaf[:, 0:R].unsqueeze(2), P, R, EJ),
                                       BC(g.etype[:, :].unsqueeze(1), P, R, EJ), ALU.is_equal))
                    up(v.tensor_scalar(neg[:, :, :], mask[:, :, :], 1.0, BIG, ALU.subtract, ALU.mult))
                    up(v.tensor_tensor(y[:, :, :], mask[:, :, :], BC(sel[:, :].unsqueeze(1), P, R, EJ), ALU.mult))
                    up(v.tensor_tensor(y[:, :, :], y[:, :, :], neg[:, :, :], ALU.add))
                    up(v.tensor_scalar(drop[:, :], cont[:, :], 1.0, BIG, ALU.subtract, ALU.mult))
                    up(v.tensor_scalar(lowered[:, :], opn[:, :], 1.0, BIG, ALU.subtract, ALU.mult))
                    up(v.tensor_scalar(ends[:, :], g.goes_on[:, :], -1.0, 1.0, ALU.mult, ALU.add))
                    up(v.tensor_tensor_scan(openb[:, ::-1], g.goes_on[:, ::-1], BC(g.ones[0:P, 0:1], P, EJ),
                                            1.0, ALU.mult, ALU.mult))

                    def to_all_edges():
                        up(v.tensor_tensor(f[:, :, :], f[:, :, :], BC(ends[:, :].unsqueeze(1), P, R, EJ), ALU.mult))
                        for r in range(R):
                            up(v.tensor_tensor_scan(y[:, r, ::-1], g.goes_on[:, ::-1], f[:, r, ::-1], 0.0,
                                                    ALU.mult, ALU.add))
                        up(v.tensor_copy(A[:, 0:R], BC(openb[:, 0:1], P, R)))
                        up(v.tensor_copy(B[:, 0:R], y[:, :, 0]))
                        carry(cback[:, :], R, ALU.mult, ALU.add, 0.0, back=True)
                        for r in range(R):
                            up(v.scalar_tensor_tensor(y[:, r, :], openb[:, :], cback[:, r:r + 1], y[:, r, :],
                                                      ALU.mult, ALU.add))
                        up(v.tensor_tensor(y[:, :, :], y[:, :, :], mask[:, :, :], ALU.mult))
                        up(v.tensor_reduce(sel[:, :], y[:, :, :].rearrange("p r j -> p j r"), AX.X, ALU.add))

                    for r in range(R):
                        up(v.tensor_tensor_scan(f[:, r, :], drop[:, :], y[:, r, :], -BIG, ALU.add, ALU.max))
                    up(v.tensor_copy(A[:, 0:R], BC(lowered[:, EJ - 1:], P, R)))
                    up(v.tensor_copy(B[:, 0:R], f[:, :, EJ - 1]))
                    carry(cm[:, :], R, ALU.add, ALU.max, -BIG)
                    for r in range(R):
                        up(v.scalar_tensor_tensor(f[:, r, :], lowered[:, :], cm[:, r:r + 1], f[:, r, :],
                                                  ALU.add, ALU.max))
                    to_all_edges()
                    up(v.tensor_tensor(w[:, :], lm[:, :], sel[:, :], ALU.subtract))
                    up(v.tensor_tensor(es[:, :], es[:, :], sel[:, :], ALU.subtract))
                    g.exp_in = n.n
                    scalar_done()
                    up(v.tensor_tensor(y[:, :, :], mask[:, :, :], BC(w[:, :].unsqueeze(1), P, R, EJ), ALU.mult))
                    for r in range(R):
                        up(v.tensor_tensor_scan(f[:, r, :], cont[:, :], y[:, r, :], 0.0, ALU.mult, ALU.add))
                    up(v.tensor_copy(A[:, 0:R], BC(opn[:, EJ - 1:], P, R)))
                    up(v.tensor_copy(B[:, 0:R], f[:, :, EJ - 1]))
                    carry(cm[:, :], R, ALU.mult, ALU.add, 0.0)
                    for r in range(R):
                        up(v.scalar_tensor_tensor(f[:, r, :], opn[:, :], cm[:, r:r + 1], f[:, r, :],
                                                  ALU.mult, ALU.add))
                    to_all_edges()
                    up(v.tensor_tensor(sel[:, :], sel[:, :], es[:, :], ALU.add))
                    up(v.reciprocal(sel[:, :], sel[:, :]))
                    up(v.tensor_tensor(w[:, :], w[:, :], sel[:, :], ALU.mult))
                    up(v.tensor_tensor(g.val[:, :, :], g.val[:, :, :], BC(w[:, :].unsqueeze(2), P, EJ, D), ALU.mult))

                flat = g.val[:, :, :].rearrange("p j f -> p f j")
                if layer == 0:
                    for h in range(H):
                        with v.Fori(0, HF) as k:
                            col = flat[:, bass.ds(k + h * HF, 1), :].rearrange("p a j -> p (a j)")
                            v.tensor_tensor_scan(col, fac[:, h, :], col, 0.0, ALU.mult, ALU.add).then_inc(scans, 1)
                else:
                    with v.Fori(0, D) as k:
                        col = flat[:, bass.ds(k, 1), :].rearrange("p a j -> p (a j)")
                        v.tensor_tensor_scan(col, cont[:, :], col, 0.0, ALU.mult, ALU.add).then_inc(scans, 1)
                v.wait_ge(scans, D)
                if layer == 0:
                    up(v.tensor_copy(A[:, :].rearrange("p (h f) -> p h f", h=H),
                                     BC(g.reach[:, :, EJ - 1:], P, H, HF)))
                else:
                    up(v.tensor_copy(A[:, :], BC(opn[:, EJ - 1:], P, D)))
                up(v.tensor_copy(B[:, :], g.val[:, EJ - 1, :]))
                carry(g.carry[:, :], D, ALU.mult, ALU.add, 0.0)

            @block.scalar
            def _(a):
                if layer == 0:
                    a.wait_ge(vec, g.exp_in)
                    for x in (fac, w, wself):
                        last = a.activation(x[:, :, :], x[:, :, :], ACT.Exp)
                    last.then_inc(sca, 1)
                if layer == 3:
                    a.wait_ge(vec, g.exp_in)
                    for x in (w, es):
                        last = a.activation(x[:, :], x[:, :], ACT.Exp)
                    last.then_inc(sca, 1)

            @block.tensor
            def _(t):
                turn_carries(t, g, vec, ten, sizes, A, B, row, a_ps, b_ps, c_ps)


def scatter(g, layer):
    order = 1 if layer == 1 else 0
    step, staged, sent = g.sem("step_s"), g.sem("staged_s"), [g.once(f"sent{b}_s{layer}") for b in range(2)]
    copied = g.sem("idx_s")
    opn = g.open[order]
    with ExitStack() as ctx:
        stage = [g.sb(f"stage{b}_s{layer}", [P, G, D], F32, ctx) for b in range(2)]
        idx = [g.sb(f"idx{b}_s{layer}", [P, G], I32, ctx) for b in range(2)]
        with g.nc.Block() as block:
            @block.vector
            def _(v):
                n = LoopCount(step, 2 * (3 if layer == 0 else 2))
                with v.Fori(0, CH // 2) as i:
                    for b in range(2):
                        c = i * 2 + b
                        at = bass.ds(c * G, G)
                        v.wait_ge(sent[b], i * (16 * G))
                        if layer == 0:
                            for h in range(H):
                                f = slice(h * HF, (h + 1) * HF)
                                last = v.tensor_tensor(stage[b][:, :, f],
                                                       g.carry[:, f].unsqueeze(1).broadcast_to([P, G, HF]),
                                                       g.reach[:, h, at].unsqueeze(2).broadcast_to([P, G, HF]), ALU.mult)
                            n.up(last)
                        else:
                            n.up(v.tensor_tensor(stage[b][:, :, :], g.carry[:, :].unsqueeze(1).broadcast_to([P, G, D]),
                                                 opn[:, at].unsqueeze(2).broadcast_to([P, G, D]), ALU.mult))
                        n.here(v, i)
                        n.up(v.tensor_tensor(stage[b][:, :, :], stage[b][:, :, :], g.val[:, at, :], ALU.add))
                        n.here(v, i)
                        if layer == 0:
                            for h in range(H):
                                f = slice(h * HF, (h + 1) * HF)
                                last = v.tensor_tensor(stage[b][:, :, f], stage[b][:, :, f],
                                                       g.rz[:, h, at].unsqueeze(2).broadcast_to([P, G, HF]), ALU.mult)
                            n.up(last)
                            n.here(v, i)
                        v.sem_inc(staged, 1)

            @block.gpsimd
            def _(pool):
                n = LoopCount(copied, 2, g=g)
                with pool.Fori(0, CH // 2) as i:
                    for b in range(2):
                        c = i * 2 + b
                        pool.wait_ge(sent[b], i * (16 * G))
                        g.passed(pool)
                        n.up(pool.tensor_copy(idx[b][:, :], g.out_row[order][:, bass.ds(c * G, G)]))
                        n.here(pool, i)
                        pool.wait_ge(staged, c + 1)
                        g.passed(pool)
                        for k in range(G):
                            pool.indirect_dma_start(out=g.aggr[layer],
                                                    out_offset=bass.IndirectOffsetOnAxis(ap=idx[b][:, k:k + 1], axis=0),
                                                    in_=stage[b][:, k, :], in_offset=None,
                                                    bounds_check=N - 1, oob_is_err=False).then_inc(sent[b], 16)
                for b in range(2):
                    pool.wait_ge(sent[b], EJ * 8)


def nodes(g, layer):
    if layer == 0:
        return first_nodes(g)
    sem = lambda n: g.sem(f"{n}_n")
    row_in, row_free, turned, turned_out = [sem(f"in{b}") for b in range(2)], sem("free"), sem("turned"), sem("turned_out")
    made, summed, squared, reduced, rooted = sem("made"), sem("summed"), sem("squared"), sem("reduced"), sem("rooted")
    inverse, y_done, sent = sem("inverse"), sem("y_done"), [sem(f"sent{b}") for b in range(2)]
    zeroed = sem("zeroed")
    PAIRS = NG // 2
    with ExitStack() as ctx:
        sb = lambda n, s, d=F32: g.sb(f"{n}_n{layer}", s, d, ctx)
        ps = lambda n, s, d=F32: g.ps(f"{n}_n{layer}", s, d, ctx)
        two = lambda n, s: [sb(f"{n}{b}", s) for b in range(2)]
        rows, arow, y, v_sb = [two(n, [P, NG, D]) for n in ("rows", "arow", "y", "v")]
        xt = two("xt", [128, PAIRS * P])
        sq, q, sd, rs = two("sq", [P, NG, D]), two("q", [P, NG]), two("sd", [P, NG]), two("rs", [P, NG])
        eps = sb("eps", [P, 1])
        out = [ps(f"out{b}", [P, NG, D]) for b in range(2)]
        tp = [ps(f"tp{b}", [128, PAIRS * P]) for b in range(2)]
        if layer == 1:
            at = two("at", [128, PAIRS * P])
            tpa = [ps(f"tpa{b}", [128, PAIRS * P]) for b in range(2)]
            h_ps = [ps(f"h{b}", [128, PAIRS * P]) for b in range(2)]
            h_sb = two("h_sb", [128, PAIRS * P])
            lab = two("lab", [P, NG, g.LW])
            hidden, hidden_out = sem("hidden"), sem("hidden_out")
            padded = sem("lab_padded")
            lab_done, lab_sent = sem("lab_done"), [sem(f"lab_sent{b}") for b in range(2)]
        dense = {1: g.wn2p, 2: g.n3p, 3: g.n4p}[layer]
        bias = {1: g.bn2c, 3: g.b4c}.get(layer)
        by_part = lambda table: table.rearrange("(p k) d -> p k d", p=P)
        src, asrc, labelled = by_part(g.feat[layer]), by_part(g.aggr[layer]), by_part(g.labelled)
        dst = by_part(g.feat[layer + 1] if layer < 3 else g.out)

        with g.nc.Block() as block:
            @block.sync
            def _(sp):
                def load(c, b):
                    sp.dma_start(rows[b][:, :, :], src[:, bass.ds(c * NG, NG), :]).then_inc(row_in[b], 16)
                    sp.dma_start(arow[b][:, :, :], asrc[:, bass.ds(c * NG, NG), :]).then_inc(row_in[b], 16)

                def store(c, b):
                    sp.dma_start(dst[:, bass.ds(c * NG, NG), :], y[b][:, :, :]).then_inc(sent[b], 16)
                    if layer == 1:
                        sp.wait_ge(lab_done, c * 2 + 6)
                        g.passed(sp)
                        sp.dma_start(labelled[:, bass.ds(c * NG, NG), :], lab[b][:, :, :]).then_inc(lab_sent[b], 16)

                for b in range(2):
                    load(b, b)
                with sp.Fori(0, NCH // 2 - 1) as i:
                    for b in range(2):
                        sp.wait_ge(row_free, i * 2 + b + 1)
                        g.passed(sp)
                        load(i * 2 + (2 + b), b)
                    for b in range(2):
                        sp.wait_ge(y_done, i * 2 + b + 1)
                        g.passed(sp)
                        store(i * 2 + b, b)
                for b in range(2):
                    sp.wait_ge(y_done, NCH - 1 + b)
                    store(NCH - 2 + b, b)
                for b in range(2):
                    sp.wait_ge(sent[b], NCH * 8)
                    if layer == 1:
                        sp.wait_ge(lab_sent[b], NCH * 8)

            @block.tensor
            def _(t):
                with t.Fori(0, NCH // 2) as i:
                    for b in range(2):
                        c = i * 2 + b
                        t.wait_ge(row_in[b], i * 32 + 32)
                        for side, to in ((rows, tp), (arow, tpa)) if layer == 1 else ((rows, tp),):
                            for k in range(PAIRS):
                                last = t.transpose(to[b][:, k * P:(k + 1) * P],
                                                   side[b][:, 2 * k:2 * k + 2, :].rearrange("p k d -> p (k d)"),
                                                   g.ident[0:P, 0:P])
                            last.then_inc(turned, 1)
                    if layer == 1:
                        for b in range(2):
                            c = i * 2 + b
                            t.wait_ge(turned_out, c * 2 + 2)
                            t.matmul(h_ps[b][:, :], g.wn1x[:, :], xt[b][:, :], start=True, stop=False)
                            t.matmul(h_ps[b][:, :], g.wn1g[:, :], at[b][:, :], start=False, stop=True).then_inc(hidden, 1)
                    for b in range(2):
                        c = i * 2 + b
                        if layer == 1:
                            t.wait_ge(hidden_out, c + 1)
                        else:
                            t.wait_ge(turned_out, c + 1)
                        t.wait_ge(summed, c + 1)
                        flat = out[b][:, :, :].rearrange("p k d -> p (k d)")
                        if bias is not None:
                            t.matmul(flat, g.onesb[:, :], bias[:, :, :].rearrange("p k d -> p (k d)"), start=True, stop=False, skip_group_check=True)
                        lhs = h_sb[b] if layer == 1 else xt[b]
                        for k in range(PAIRS):
                            last = t.matmul(flat[:, 2 * D * k:2 * D * (k + 1)], lhs[:, k * P:(k + 1) * P], dense[:, :],
                                            start=bias is None, stop=True, skip_group_check=True)
                        last.then_inc(made, 1)

            @block.scalar
            def _(a):
                a.activation(eps[:, :], g.ones[0:P, 0:1], ACT.Copy, scale=1e-5).then_inc(zeroed, 1)
                a.wait_ge(zeroed, 1)
                with a.Fori(0, NCH // 2) as i:
                    for b in range(2):
                        c = i * 2 + b
                        a.wait_ge(made, c + 1)
                        if layer == 1:
                            a.wait_ge(turned, c * 2 + 1)
                            a.activation(xt[b][:, :], tp[b][:, :], ACT.Copy).then_inc(turned_out, 1)
                            a.wait_ge(turned, c * 2 + 2)
                            a.activation(at[b][:, :], tpa[b][:, :], ACT.Copy).then_inc(turned_out, 1)
                        else:
                            a.wait_ge(turned, c + 1)
                            a.activation(xt[b][:, :], tp[b][:, :], ACT.Copy).then_inc(turned_out, 1)
                    if layer == 1:
                        for b in range(2):
                            a.wait_ge(hidden, i * 2 + b + 1)
                            a.activation(h_sb[b][:, :], h_ps[b][:, :], ACT.Silu, bias=g.bn1p[:, 0:1]).then_inc(hidden_out, 1)
                    for b in range(2):
                        a.wait_ge(summed, i * 2 + b + 3)
                        a.activation(sq[b][:, :, :], v_sb[b][:, :, :], ACT.Square).then_inc(squared, 1)
                    for b in range(2):
                        a.wait_ge(reduced, i * 2 + b + 1)
                        a.activation(sd[b][:, :], q[b][:, :], ACT.Sqrt, scale=1.0 / D, bias=eps[:, 0:1]).then_inc(rooted, 1)

            @block.vector
            def _(v):
                v.sem_inc(summed, 2)
                if layer == 1:
                    v.sem_inc(lab_done, 4)
                v.sem_inc(made, 2)
                with v.Fori(0, NCH // 2) as i:
                    for b in range(2):
                        c = i * 2 + b
                        v.wait_ge(made, c + 3)
                        v.tensor_tensor(v_sb[b][:, :, :], out[b][:, :, :], (rows if layer == 1 else arow)[b][:, :, :],
                                        ALU.add).then_inc(summed, 1)
                        v.wait_ge(summed, c + 3)
                        v.sem_inc(row_free, 1)
                    for b in range(2):
                        v.wait_ge(squared, i * 2 + b + 1)
                        v.tensor_reduce(q[b][:, :], sq[b][:, :, :], AX.X, ALU.add).then_inc(reduced, 1)
                    for b in range(2):
                        c = i * 2 + b
                        v.wait_ge(rooted, c + 1)
                        v.reciprocal(rs[b][:, :], sd[b][:, :]).then_inc(inverse, 1)
                        v.wait_ge(inverse, c + 1)
                        v.wait_ge(sent[b], i * 16)
                        if layer == 1:
                            v.wait_ge(lab_done, i * 4 + (2 * b + 1))
                        scale = rs[b][:, :].unsqueeze(2).broadcast_to([P, NG, D])
                        v.tensor_tensor(y[b][:, :, :], v_sb[b][:, :, :], scale, ALU.mult).then_inc(y_done, 1)

            @block.gpsimd
            def _(pool):
                if layer == 1:
                    for b in range(2):
                        pool.memset(lab[b][:, :, D:], 0.0).then_inc(padded, 1)
                    pool.wait_ge(padded, 2)
                    with pool.Fori(0, NCH // 2) as i:
                        for b in range(2):
                            c = i * 2 + b
                            pool.wait_ge(lab_sent[b], i * 16)
                            pool.wait_ge(y_done, c + 1)
                            g.passed(pool)
                            pool.tensor_copy(lab[b][:, :, 0:D], y[b][:, :, :]).then_inc(lab_done, 1)
                            pool.tensor_copy(lab[b][:, :, D:D + 1], g.label[:, bass.ds(c * NG, NG)].unsqueeze(2)
                                             ).then_inc(lab_done, 1)


def first_nodes(g):
    sem = lambda n: g.sem(f"{n}_n")
    row_in, turned, turned_out = [sem(f"in{b}") for b in range(2)], sem("turned"), sem("turned_out")
    made, relu_done, exp_done, sq_done, rooted = sem("made"), sem("summed"), sem("squared"), sem("reduced"), sem("rooted")
    step, centred, shifted, y_done = sem("inverse"), sem("centred"), sem("shifted"), sem("y_done")
    sent, zeroed = [sem(f"sent{b}") for b in range(2)], sem("zeroed")
    PAIRS = NG // 2
    STEPS = ["elu", "sum1", "mean1", "q1", "rs1", "scale", "sum", "sum2", "mean2", "q2", "rs2", "y"]
    per = 2 * len(STEPS)
    num = {(n, b): 2 * k + b + 1 for k, n in enumerate(STEPS) for b in range(2)}
    with ExitStack() as ctx:
        sb = lambda n, s, d=F32: g.sb(f"{n}_n0", s, d, ctx)
        ps = lambda n, s, d=F32: g.ps(f"{n}_n0", s, d, ctx)
        two = lambda n, s: [sb(f"{n}{b}", s) for b in range(2)]
        rows, arow, y = [two(n, [P, NG, D]) for n in ("rows", "arow", "y")]
        xt = two("xt", [128, PAIRS * P])
        e, u, cd, sq, xb, ce = [two(n, [P, NG, D]) for n in ("e", "u", "cd", "sq", "xb", "ce")]
        st, q, sd, rs = [two(n, [P, 2, NG]) for n in ("st", "q", "sd", "rs")]
        eps = sb("eps", [P, 2])
        tp = [ps(f"tp{b}", [128, PAIRS * P]) for b in range(2)]
        out = [ps(f"out{b}", [P, NG, D]) for b in range(2)]
        src, asrc, dst = [table.rearrange("(p k) d -> p k d", p=P) for table in (g.feat[0], g.aggr[0], g.feat[1])]
        B3 = [P, NG, D]
        with g.nc.Block() as block:
            @block.sync
            def _(sp):
                def load(c, b):
                    sp.dma_start(rows[b][:, :, :], src[:, bass.ds(c * NG, NG), :]).then_inc(row_in[b], 16)
                    sp.dma_start(arow[b][:, :, :], asrc[:, bass.ds(c * NG, NG), :]).then_inc(row_in[b], 16)

                def store(c, b):
                    sp.dma_start(dst[:, bass.ds(c * NG, NG), :], y[b][:, :, :]).then_inc(sent[b], 16)

                for b in range(2):
                    load(b, b)
                with sp.Fori(0, NCH // 2 - 1) as i:
                    for b in range(2):
                        sp.wait_ge(made, i * 2 + b + 3)
                        g.passed(sp)
                        sp.wait_ge(shifted, i * 2 + b + 1)
                        g.passed(sp)
                        load(i * 2 + (2 + b), b)
                    for b in range(2):
                        sp.wait_ge(step, i * per + (num["y", b] + per))
                        g.passed(sp)
                        store(i * 2 + b, b)
                for b in range(2):
                    sp.wait_ge(step, (NCH // 2) * per + num["y", b])
                    store(NCH - 2 + b, b)
                for b in range(2):
                    sp.wait_ge(sent[b], NCH * 8)

            @block.tensor
            def _(t):
                with t.Fori(0, NCH // 2) as i:
                    for b in range(2):
                        t.wait_ge(row_in[b], i * 32 + 32)
                        for k in range(PAIRS):
                            last = t.transpose(tp[b][:, k * P:(k + 1) * P],
                                               rows[b][:, 2 * k:2 * k + 2, :].rearrange("p k d -> p (k d)"), g.ident[0:P, 0:P])
                        last.then_inc(turned, 1)
                    for b in range(2):
                        t.wait_ge(step, i * per + num["elu", b])
                        flat = out[b][:, :, :].rearrange("p k d -> p (k d)")
                        t.matmul(flat, g.ident[0:P, 0:P], arow[b][:, :, :].rearrange("p k d -> p (k d)"),
                                 start=True, stop=False, skip_group_check=True)
                        t.wait_ge(turned_out, i * 2 + b + 1)
                        for k in range(PAIRS):
                            last = t.matmul(flat[:, 2 * D * k:2 * D * (k + 1)], xt[b][:, k * P:(k + 1) * P], g.n1p[:, :],
                                            start=False, stop=True, skip_group_check=True)
                        last.then_inc(made, 1)

            @block.scalar
            def _(a):
                a.activation(eps[:, 0:1], g.ones[0:P, 0:1], ACT.Copy, scale=1e-6).then_inc(zeroed, 1)
                a.activation(eps[:, 1:2], g.ones[0:P, 0:1], ACT.Copy, scale=1e-5).then_inc(zeroed, 1)
                a.wait_ge(zeroed, 2)
                with a.Fori(0, NCH // 2) as i:
                    for b in range(2):
                        a.wait_ge(turned, i * 2 + b + 1)
                        a.wait_ge(made, i * 2 + b + 1)
                        a.activation(xt[b][:, :], tp[b][:, :], ACT.Copy).then_inc(turned_out, 1)
                    for b in range(2):
                        a.wait_ge(made, i * 2 + b + 3)
                        a.activation(e[b][:, :, :], out[b][:, :, :], ACT.Relu, scale=-1.0).then_inc(relu_done, 1)
                    for b in range(2):
                        a.wait_ge(relu_done, i * 2 + b + 1)
                        a.activation(e[b][:, :, :], e[b][:, :, :], ACT.Exp, scale=-1.0).then_inc(exp_done, 1)
                    for b in range(2):
                        a.wait_ge(centred, i * 4 + b + 1)
                        a.activation(sq[b][:, :, :], cd[b][:, :, :], ACT.Square).then_inc(sq_done, 1)
                    for b in range(2):
                        a.wait_ge(step, i * per + (num["q1", b] + per))
                        a.activation(sd[b][:, 0, :], q[b][:, 0, :], ACT.Sqrt, scale=1.0 / D, bias=eps[:, 0:1]).then_inc(rooted, 1)
                    for b in range(2):
                        a.wait_ge(centred, i * 4 + b + 3)
                        a.activation(sq[b][:, :, :], ce[b][:, :, :], ACT.Square).then_inc(sq_done, 1)
                    for b in range(2):
                        a.wait_ge(step, i * per + (num["q2", b] + per))
                        a.activation(sd[b][:, 1, :], q[b][:, 1, :], ACT.Sqrt, scale=1.0 / D, bias=eps[:, 1:2]).then_inc(rooted, 1)

            @block.vector
            def _(v):
                v.sem_inc(step, per)
                v.sem_inc(made, 2)

                def after(i, name, b):
                    v.wait_ge(step, i * per + (num[name, b] + per))

                with v.Fori(0, NCH // 2) as i:
                    for b in range(2):
                        v.wait_ge(exp_done, i * 2 + b + 1)
                        v.scalar_tensor_tensor(u[b][:, :, :], e[b][:, :, :], -1.0, out[b][:, :, :], ALU.add, ALU.max
                                               ).then_inc(step, 1)
                    for b in range(2):
                        after(i, "elu", b)
                        v.tensor_reduce(st[b][:, 0, :], u[b][:, :, :], AX.X, ALU.add).then_inc(step, 1)
                    for b in range(2):
                        after(i, "sum1", b)
                        v.tensor_scalar(st[b][:, 0, :], st[b][:, 0, :], -1.0 / D, None, ALU.mult).then_inc(step, 1)
                    for b in range(2):
                        v.wait_ge(sq_done, i * 4 + b + 1)
                        v.tensor_reduce(q[b][:, 0, :], sq[b][:, :, :], AX.X, ALU.add).then_inc(step, 1)
                    for b in range(2):
                        v.wait_ge(rooted, i * 4 + b + 1)
                        v.reciprocal(rs[b][:, 0, :], sd[b][:, 0, :]).then_inc(step, 1)
                    for b in range(2):
                        after(i, "rs1", b)
                        for k in range(NG):
                            last = v.scalar_tensor_tensor(u[b][:, k, :], cd[b][:, k, :], rs[b][:, 0, k:k + 1],
                                                          g.lnw[:, 0, :], ALU.mult, ALU.mult)
                        last.then_inc(step, 1)
                    for b in range(2):
                        after(i, "scale", b)
                        v.wait_ge(shifted, i * 2 + b + 1)
                        v.tensor_tensor(u[b][:, :, :], u[b][:, :, :], xb[b][:, :, :], ALU.add).then_inc(step, 1)
                    for b in range(2):
                        after(i, "sum", b)
                        v.tensor_reduce(st[b][:, 1, :], u[b][:, :, :], AX.X, ALU.add).then_inc(step, 1)
                    for b in range(2):
                        after(i, "sum2", b)
                        v.tensor_scalar(st[b][:, 1, :], st[b][:, 1, :], -1.0 / D, None, ALU.mult).then_inc(step, 1)
                    for b in range(2):
                        v.wait_ge(sq_done, i * 4 + b + 3)
                        v.tensor_reduce(q[b][:, 1, :], sq[b][:, :, :], AX.X, ALU.add).then_inc(step, 1)
                    for b in range(2):
                        v.wait_ge(rooted, i * 4 + b + 3)
                        v.reciprocal(rs[b][:, 1, :], sd[b][:, 1, :]).then_inc(step, 1)
                    for b in range(2):
                        after(i, "rs2", b)
                        v.wait_ge(sent[b], i * 16)
                        v.tensor_tensor(y[b][:, :, :], ce[b][:, :, :], rs[b][:, 1, :].unsqueeze(2).broadcast_to(B3),
                                        ALU.mult).then_inc(step, 1)

            @block.gpsimd
            def _(pool):
                with pool.Fori(0, NCH // 2) as i:
                    for b in range(2):
                        pool.wait_ge(row_in[b], i * 32 + 32)
                        g.passed(pool)
                        pool.wait_ge(step, i * per + num["sum", b])
                        g.passed(pool)
                        pool.tensor_tensor(xb[b][:, :, :], rows[b][:, :, :], g.lnw[:, 1, :].unsqueeze(1).broadcast_to(B3),
                                           ALU.add).then_inc(shifted, 1)
                    for name, to, k in (("mean1", cd, 0), ("mean2", ce, 1)):
                        for b in range(2):
                            pool.wait_ge(step, i * per + (num[name, b] + per))
                            g.passed(pool)
                            pool.tensor_tensor(to[b][:, :, :], u[b][:, :, :], st[b][:, k, :].unsqueeze(2).broadcast_to(B3),
                                               ALU.add).then_inc(centred, 1)


def build(nc, args, out, features, aggregates, labelled, sorted_, layers=4):
    with ExitStack() as ctx:
        g = Graph(nc, args, ctx)
        g.feat, g.aggr, g.out, g.labelled, g.sorted = [args["x"]] + features, aggregates, out, labelled, sorted_
        g.LW = labelled.shape[1]
        g.ends_of = [g.sb(f"ends_of{s}", [P, 2, EJ], I32) for s in range(2)]
        g.out_row = [g.sb(f"out_row{s}", [P, EJ], I32) for s in range(2)]
        g.cont = [g.sb(f"cont{s}", [P, EJ]) for s in range(2)]
        g.open = [g.sb(f"open{s}", [P, EJ]) for s in range(2)]
        g.goes_on = g.sb("goes_on", [P, EJ])
        g.etype, g.radial, g.attn = g.sb("etype", [P, EJ]), g.sb("radial", [P, EJ]), g.sb("attn", [P, H, EJ])
        g.iotaf = g.sb("iotaf", [P, R])
        weights(g)
        with ExitStack() as sorting:
            g.rec = g.sb("rec", [P, EJ, REC], F32, sorting)
            g.keys = g.sb("keys", [P, 4, EJ + 1], F32, sorting)
            g.iota = g.sb("iota", [P, LO], BF16, sorting)
            g.base = g.sb("base", [HB, 2, 2 * LO], F32, sorting)
            g.strict = g.sb("strict", [P, P], F32, sorting)
            load_and_constants(g)
            histogram(g)
            rank_and_scatter(g)
        read_orders(g)
        g.clear()
        g.val = g.sb("val", [P, EJ, D])
        g.score = g.sb("score", [P, 2 * H, EJ])
        g.reach, g.rz, g.carry = g.sb("reach", [P, H, EJ]), g.sb("rz", [P, H, EJ]), g.sb("carry", [P, D])
        for layer in range(layers):
            for phase in (edges, segments, scatter, nodes):
                phase(g, layer)
                g.clear()


def kernel(**inputs):
    import numpy as _np
    import concourse.bacc as _bacc
    from concourse import mybir as _mybir
    from concourse.bass_utils import run_bass_kernel_spmd as _run

    nc = _bacc.Bacc("TRN2", target_bir_lowering=False, num_devices=1)
    arrays, args = {}, {}
    for name, value in inputs.items():
        arr = _np.ascontiguousarray(value)
        arrays[f"in_{name}"] = arr
        args[name] = nc.dram_tensor(f"in_{name}", arr.shape, _mybir.dt.from_np(arr.dtype), kind="ExternalInput").ap()
    out = nc.dram_tensor("out_0", (N, D), F32, kind="ExternalOutput").ap()
    features = [nc.dram_tensor(f"features{k + 1}", (N, D), F32, kind="Internal").ap() for k in range(3)]
    aggregates = [nc.dram_tensor(f"aggregates{k}", (N, D), F32, kind="Internal").ap() for k in range(4)]
    labelled = nc.dram_tensor("labelled", (N, 72), F32, kind="Internal").ap()
    sorted_ = [nc.dram_tensor(f"sorted{k}", (E, REC), F32, kind="Internal").ap() for k in range(2)]
    build(nc, args, out, features, aggregates, labelled, sorted_)
    r = _run(nc, [arrays], core_ids=[0])
    return r.results[0]["out_0"]
```

```python
from contextlib import ExitStack

import concourse.bass as bass
from concourse import mybir

F32 = mybir.dt.float32
BF16 = mybir.dt.bfloat16
I32 = mybir.dt.int32
ALU = mybir.AluOpType
ACT = mybir.ActivationFunctionType
AX = mybir.AxisListType

N = 50000
E = 25000
D = 64
P = 125
EJ = E // P
NK = N // P
G = 4
CH = EJ // G
RING = 4
NG = 8
NCH = NK // NG
R = 8
H = 4
HF = 16
HB = 128
LO = -(-N // (2 * HB))
REC = 8
SRC, DST, TYPE, RADIAL, ATT = 0, 1, 2, 3, 4
BIG = 1.0e30
SKIP = 1.0e6
assert P * EJ == E and P * NK == N and CH % 2 == 0 and EJ % RING == 0
assert 2 * HB * LO >= N and LO <= 2 * HB <= 256


class Count:

    def __init__(self, sem):
        self.sem, self.n = sem, 0

    def up(self, ins):
        self.n += 1
        return ins.then_inc(self.sem, 1)

    def here(self, eng):
        eng.wait_ge(self.sem, self.n)


class LoopCount:

    def __init__(self, sem, per, base=0, g=None):
        self.sem, self.per, self.base, self.n, self.g = sem, per, base, 0, g

    def up(self, ins):
        self.n += 1
        assert self.n <= self.per
        return ins.then_inc(self.sem, 1)

    def here(self, eng, i):
        eng.wait_ge(self.sem, i * self.per + (self.base + self.n))
        if self.g:
            self.g.passed(eng)

    def at(self, i, n):
        return i * self.per + (self.base + n)


def turns(eng, total, ahead, turn, first, last, ring=2):
    for c in range(first, ahead):
        turn(c, c % ring, lambda k, c=c: 0 <= c + k < total)
    assert (total - 2 * ahead) % ring == 0
    with eng.Fori(0, (total - 2 * ahead) // ring) as i:
        for b in range(ring):
            turn(i * ring + (b + ahead), (b + ahead) % ring, lambda k: True)
    for c in range(total - ahead, last + 1):
        turn(c, c % ring, lambda k, c=c: 0 <= c + k < total)


class Graph:

    def __init__(self, nc, args, ctx):
        self.nc, self.ctx, self.a = nc, ctx, args
        self.sems, self.raised = {"waits_passed": ctx.enter_context(nc.semaphore("waits_passed"))}, []

    def sem(self, name):
        if name not in self.sems:
            self.sems[name] = self.ctx.enter_context(self.nc.semaphore(name))
        self.raised.append(self.sems[name])
        return self.sems[name]

    def once(self, name):
        return self.ctx.enter_context(self.nc.semaphore(name))

    def passed(self, eng):
        eng.sem_inc(self.sems["waits_passed"], 1)

    def clear(self):
        with self.nc.Block() as block:
            @block.sync
            def _(sp):
                for s in self.raised:
                    sp.sem_clear(s)
                sp.sem_clear(self.sems["waits_passed"])
        self.raised = []

    def sb(self, name, shape, dt=F32, ctx=None):
        t = (ctx or self.ctx).enter_context(self.nc.sbuf_tensor(name, shape, dt))
        return t

    def ps(self, name, shape, dt=F32, ctx=None):
        return ctx.enter_context(self.nc.psum_tensor(name, shape, dt))


def weights(g):
    g.ident = g.sb("ident", [128, 128])
    g.identb = g.sb("identb", [128, 128], BF16)
    g.ones = g.sb("ones", [128, 128])
    g.w0 = g.sb("w0", [128, D + 2 * H])
    g.n1p, g.wn1x, g.wn1g, g.wn2p, g.n3p, g.n4p = [g.sb(n, [128, 128]) for n in
                                                   ("n1p", "wn1x", "wn1g", "wn2p", "n3p", "n4p")]
    g.bn1p = g.sb("bn1p", [128, 1])
    g.onesb = g.sb("onesb", [3, P], BF16)
    g.bn2c = g.sb("bn2c", [3, NG, D], BF16)
    g.b4c = g.sb("b4c", [3, NG, D], BF16)
    g.w1a = g.sb("w1a", [128, D])
    g.w1r = g.sb("w1r", [P, D])
    g.be1 = g.sb("be1", [D, 1])
    g.w2 = g.sb("w2", [D, D])
    g.be2 = g.sb("be2", [D, 1])
    g.wa = g.sb("wa", [D, D])
    g.ba = g.sb("ba", [D, 1])
    g.wg = g.sb("wg", [128, D])
    g.w3 = g.sb("w3", [128, R * D])
    g.w3s = g.sb("w3s", [128, 2 * R])
    g.lnw = g.sb("lnw", [P, 2, D])
    g.label = g.sb("label", [P, NK])


def load_and_constants(g):
    nc, a = g.nc, g.a
    ld = g.sem("inputs_loaded")
    pc, vc, tc = g.sem("prep_pool"), g.sem("prep_vector"), g.sem("prep_tensor")
    pool_n, v_n, t_n = Count(pc), Count(vc), Count(tc)

    with ExitStack() as ctx:
        sb = lambda n, s, d=F32: g.sb(n, s, d, ctx)
        wd = sb("wd", [D, 2, D]); acol = sb("acol", [D, 3]); bd = sb("bd", [D, H])
        abd = sb("abd", [D, 3, H]); we = sb("we", [D, HF]); wea = sb("wea", [D, H, HF])
        wvb = sb("wvb", [P, H, HF]); wacol = sb("wacol", [D, 1])
        ws2 = sb("ws2", [D, 2, D]); wg2 = sb("wg2", [D, 2, D])
        att3 = sb("att3", [128, R * D]); t3 = sb("t3", [128, R * D]); u3 = sb("u3", [128, 2 * R])
        ws3 = sb("ws3", [128, D]); wsum = sb("wsum", [128, D])
        brow = sb("brow", [3, (R + 1) * D]); bsum = sb("bsum", [3, D])
        piece, pieces = sb("piece", [3, D], BF16), sb("pieces", [3, D])
        wn1h, wn2h, bn2 = sb("wn1h", [128, 2, D]), sb("wn2h", [128, D]), sb("bn2", [3, D])
        half_w, means = sb("half_w", [128, 3, D]), sb("means", [128, 16])
        lab_i = sb("lab_i", [P, NK], I32)
        ea = sb("ea", [P, EJ, 16]); ea3 = sb("ea3", [P, EJ, 3]); tmp = sb("tmp", [P, EJ, 16])
        si = sb("si", [P, EJ], I32); di = sb("di", [P, EJ], I32); ti = sb("ti", [P, EJ], I32)
        high_i = sb("high_i", [P, 2, EJ], I32); iot = sb("iot", [P, 2 * HB], I32)
        hf, lf, off = [sb(n, [P, 2, EJ]) for n in ("high", "low", "off")]
        shift = sb("shift", [D, 128])
        ps = g.ps("prep_ps", [128, 512], F32, ctx)
        ps2 = g.ps("prep_ps2", [128, 512], F32, ctx)
        ps3 = g.ps("prep_ps3", [128, 512], F32, ctx)
        L = [0]
        PREP = 9

        with nc.Block() as block:
            @block.sync
            def _(sp):
                def load(dst, src, short=False):
                    L[0] += 16
                    sp.dma_start(dst, src, allow_slow_non_contiguous=short).then_inc(ld, 16)
                row = lambda ap: ap.rearrange("(a n) -> a n", a=1)
                col = lambda ap: ap.rearrange("(n a) -> n a", a=1)
                load(si[:, :], a["src"].rearrange("(p j) -> p j", p=P))
                load(di[:, :], a["dst"].rearrange("(p j) -> p j", p=P))
                load(ti[:, :], a["edge_type_8"].rearrange("(p j) -> p j", p=P))
                load(ea[:, :, :], a["edge_attr_16"].rearrange("(p j) d -> p j d", p=P))
                load(ea3[:, :, :], a["edge_attr_3"].rearrange("(p j) d -> p j d", p=P))
                load(lab_i[:, :], a["node_type_2"].rearrange("(p k) -> p k", p=P))
                w2d = a["L0_gnn_W"].rearrange("h f i -> (h f) i")
                for b in range(2):
                    load(wd[:, b, :], w2d)
                for h in range(H):
                    load(acol[h * HF:(h + 1) * HF, :], a["L0_gnn_a"][h, :].rearrange("(s f) -> f s", f=HF), True)
                load(we[:, :], a["L0_gnn_W_edge"].rearrange("h f i -> (h f) i"))
                for b, n in enumerate(("L0_gnn_ln_scale", "L0_gnn_ln_bias")):
                    load(g.lnw[:, b, :], row(a[n]).broadcast_to([P, D]))
                load(g.w1a[:, :], a["L1_gnn_We1"][0:2 * D, :])
                load(g.w1r[:, :], a["L1_gnn_We1"][2 * D:2 * D + 1, :].broadcast_to([P, D]))
                load(g.be1[:, :], col(a["L1_gnn_be1"]))
                load(g.w2[:, :], a["L1_gnn_We2"])
                load(g.be2[:, :], col(a["L1_gnn_be2"]))
                load(wacol[:, :], a["L1_gnn_Wa"])
                load(g.ba[:, :], row(a["L1_gnn_ba"]).broadcast_to([D, 1]))
                for b in range(2):
                    half = slice(b * D, (b + 1) * D)
                    load(wn1h[half, 0, :], a["L1_gnn_Wn1"][0:D, :])
                    load(wn1h[half, 1, :], a["L1_gnn_Wn1"][D:2 * D, :])
                    load(wn2h[half, :], a["L1_gnn_Wn2"])
                    load(g.bn1p[half, :], col(a["L1_gnn_bn1"]))
                load(bn2[:, :], row(a["L1_gnn_bn2"]).broadcast_to([3, D]))
                for b in range(2):
                    load(ws2[:, b, :], a["L2_gnn_W_self"])
                load(wg2[:, :, :], a["L2_gnn_W_groups"].rearrange("g o i -> o g i"))
                w3v = a["L3_gnn_W"].rearrange("r d f -> d r f")
                for b in range(2):
                    load(g.w3[b * D:(b + 1) * D, :].rearrange("p (r f) -> p r f", r=R), w3v)
                    load(ws3[b * D:(b + 1) * D, :], a["L3_gnn_W_self"])
                load(att3[0:D, :], a["L3_gnn_att_src"].rearrange("r f -> (r f)").rearrange("(a n) -> a n", a=1).broadcast_to([D, R * D]))
                load(att3[D:128, :], a["L3_gnn_att_dst"].rearrange("r f -> (r f)").rearrange("(a n) -> a n", a=1).broadcast_to([D, R * D]))
                load(brow[:, 0:D], row(a["L3_gnn_b_self"]).broadcast_to([3, D]))
                load(brow[:, D:], a["L3_gnn_bias"].rearrange("r f -> (r f)").rearrange("(a n) -> a n", a=1).broadcast_to([3, R * D]))

            @block.gpsimd
            def _(pool):
                pool_n.up(pool.memset(g.ones[:, :], 1.0))
                pool_n.up(pool.memset(g.ident[:, :], 0.0))
                pool_n.up(pool.memset(bd[:, :], 1.0))
                pool_n.up(pool.memset(shift[:, :], 0.0))
                pool_n.up(pool.iota(iot[:, :], pattern=[[1, 2 * HB]], base=0, channel_multiplier=0))
                pool_n.here(pool)
                pool_n.up(pool.affine_select(out=g.ident[:, :], in_=g.ident[:, :], compare_op=ALU.not_equal,
                                             fill=1.0, base=0, pattern=[[-1, 128]], channel_multiplier=1))
                pool_n.up(pool.affine_select(out=shift[:, :], in_=shift[:, :], compare_op=ALU.not_equal,
                                             fill=1.0, base=D, pattern=[[-1, 128]], channel_multiplier=1))
                pool_n.up(pool.affine_select(out=bd[:, :], in_=bd[:, :], compare_op=ALU.is_ge, fill=0.0, base=0,
                                             pattern=[[-HF, H]], channel_multiplier=1))
                pool_n.here(pool)
                pool_n.up(pool.affine_select(out=bd[:, :], in_=bd[:, :], compare_op=ALU.is_ge, fill=0.0,
                                             base=HF - 1, pattern=[[HF, H]], channel_multiplier=-1))

            steps = {}

            @block.vector
            def _(v):
                def up(ins):
                    v_n.up(ins)
                v.wait_ge(pc, PREP)
                v.wait_ge(ld, L[0])
                up(v.tensor_copy(g.identb[:, :], g.ident[:, :]))
                for k in range(3):
                    up(v.tensor_scalar(abd[:, k, :], bd[:, :], acol[:, k:k + 1], None, ALU.mult))
                v_n.here(v)
                up(v.tensor_tensor(wea[:, :, :], we[:, :].unsqueeze(1).broadcast_to([D, H, HF]),
                                   abd[:, 2, :].unsqueeze(2).broadcast_to([D, H, HF]), ALU.mult))
                up(v.tensor_copy(g.wa[:, :], wacol[:, 0:1].broadcast_to([D, D])))
                up(v.tensor_tensor(t3[:, :], g.w3[:, :], att3[:, :], ALU.mult))
                v_n.here(v)
                up(v.tensor_reduce(u3[:, 0:R], t3[:, :].rearrange("p (r f) -> p r f", r=R), AX.X, ALU.add))
                v_n.here(v)
                steps["small"] = v_n.n
                up(v.tensor_copy(g.rec[:, :, SRC], si[:, :]))
                up(v.tensor_copy(g.rec[:, :, DST], di[:, :]))
                up(v.tensor_copy(g.rec[:, :, TYPE], ti[:, :]))
                up(v.tensor_copy(g.label[:, :], lab_i[:, :]))
                up(v.tensor_tensor(ea3[:, :, :], ea3[:, :, :], ea3[:, :, :], ALU.mult))
                v_n.here(v)
                up(v.tensor_reduce(g.rec[:, :, RADIAL], ea3[:, :, :], AX.X, ALU.add))
                for side, e in enumerate((DST, SRC)):
                    up(v.tensor_scalar(hf[:, side, :], g.rec[:, :, e], 1.0 / LO, None, ALU.mult))
                v_n.here(v)
                up(v.tensor_copy(high_i[:, :, :], hf[:, :, :]))
                v_n.here(v)
                up(v.tensor_copy(hf[:, :, :], high_i[:, :, :]))
                v_n.here(v)
                for side, e in enumerate((DST, SRC)):
                    up(v.scalar_tensor_tensor(lf[:, side, :], hf[:, side, :], -float(LO), g.rec[:, :, e], ALU.mult, ALU.add))
                v_n.here(v)
                for compare, bound, high_by, low_by in ((ALU.is_lt, 0.0, -1.0, float(LO)), (ALU.is_ge, float(LO), 1.0, -float(LO))):
                    up(v.tensor_scalar(off[:, :, :], lf[:, :, :], bound, None, compare))
                    v_n.here(v)
                    up(v.scalar_tensor_tensor(hf[:, :, :], off[:, :, :], high_by, hf[:, :, :], ALU.mult, ALU.add))
                    up(v.scalar_tensor_tensor(lf[:, :, :], off[:, :, :], low_by, lf[:, :, :], ALU.mult, ALU.add))
                    v_n.here(v)
                up(v.memset(g.keys[:, :, EJ:], 0.0))
                up(v.tensor_copy(g.iota[:, :], iot[:, :]))
                up(v.tensor_copy(g.iotaf[:, :], iot[0:P, 0:R]))
                v_n.here(v)
                for side in range(2):
                    up(v.tensor_copy(g.keys[:, 2 * side, 0:EJ], hf[:, side, :]))
                    up(v.tensor_copy(g.keys[:, 2 * side + 1, 0:EJ], lf[:, side, :]))
                v.wait_ge(tc, 3)
                up(v.tensor_copy(g.w0[0:D, 0:D], ps[0:D, 0:D]))
                up(v.tensor_scalar(g.w0[D:128, 0:D], ps[D:128, 0:D], -1.0, None, ALU.mult))
                up(v.tensor_copy(g.w0[0:D, D:D + H], ps2[0:D, 0:H]))
                up(v.tensor_copy(g.w0[D:128, D:D + H], ps2[D:128, H:2 * H]))
                up(v.memset(g.w0[0:D, D + H:], 0.0))
                up(v.tensor_copy(g.w0[D:128, D + H:], ps2[D:128, 0:H]))
                up(v.tensor_copy(wvb[:, :, :], ps3[0:P, 0:D].rearrange("p (h k) -> p h k", h=H)))
                up(v.memset(g.n1p[:, :], 0.0))
                v_n.here(v)
                up(v.tensor_copy(g.n1p[0:D, 0:D], ps[0:D, 0:D]))
                up(v.tensor_copy(g.n1p[D:128, D:], ps[D:128, 0:D]))
                v_n.here(v)
                up(v.tensor_tensor(g.w0[D:128, D + H:], g.w0[D:128, D + H:], g.w0[D:128, D:D + H], ALU.add))
                steps["ps_free"] = v_n.n
                for h in range(H):
                    up(v.tensor_tensor(tmp[:, :, :], ea[:, :, :],
                                       wvb[:, h, :].unsqueeze(1).broadcast_to([P, EJ, 16]), ALU.mult))
                    v_n.here(v)
                    up(v.tensor_reduce(g.rec[:, :, ATT + h], tmp[:, :, :], AX.X, ALU.add))
                    v_n.here(v)
                v.wait_ge(tc, 6)
                up(v.tensor_copy(g.wg[:, :], ps2[:, 0:D]))
                up(v.tensor_copy(half_w[:, 1, :], ps[:, 0:D]))
                up(v.tensor_copy(g.w3s[0:D, 0:R], u3[0:D, 0:R]))
                up(v.memset(g.w3s[0:D, R:], 0.0))
                up(v.tensor_copy(g.w3s[D:128, 0:R], u3[D:128, 0:R]))
                up(v.tensor_tensor(g.w3s[D:128, R:], ps3[D:128, 0:R], u3[D:128, 0:R], ALU.add))
                up(v.tensor_reduce(wsum[:, :], g.w3[:, :].rearrange("p (r f) -> p f r", r=R), AX.X, ALU.add))
                up(v.tensor_reduce(bsum[:, :], brow[:, :].rearrange("p (r f) -> p f r", r=R + 1), AX.X, ALU.add))
                up(v.tensor_copy(half_w[:, 0, :], wn2h[:, :]))
                v_n.here(v)
                up(v.tensor_tensor(half_w[:, 2, :], wsum[:, :], ws3[:, :], ALU.add))
                v_n.here(v)

                def centre(x, k, parts, count):
                    up(v.tensor_reduce(means[0:parts, k:k + count], x, AX.X, ALU.add))
                    v_n.here(v)
                    up(v.tensor_scalar(means[0:parts, k:k + count], means[0:parts, k:k + count], -1.0 / D, None, ALU.mult))
                    v_n.here(v)
                    up(v.tensor_tensor(x, x, means[0:parts, k:k + count].unsqueeze(2).broadcast_to([parts, count, D]),
                                       ALU.add))
                    v_n.here(v)

                centre(half_w[:, :, :], 0, 128, 3)
                centre(g.wg[:, :].unsqueeze(1), 3, 128, 1)
                centre(g.w3[:, :].rearrange("p (r f) -> p r f", r=R), 4, 128, R)
                centre(bsum[:, :].unsqueeze(1), 12, 3, 1)
                centre(bn2[:, :].unsqueeze(1), 13, 3, 1)
                up(v.tensor_scalar(g.w3[D:128, :], g.w3[D:128, :], -1.0, None, ALU.mult))
                for m in (g.wn1x, g.wn1g, g.wn2p, g.n3p, g.n4p):
                    up(v.memset(m[:, :], 0.0))
                v_n.here(v)
                for b in range(2):
                    half = slice(b * D, (b + 1) * D)
                    up(v.tensor_copy(g.wn1x[half, half], wn1h[half, 0, :]))
                    up(v.tensor_copy(g.wn1g[half, half], wn1h[half, 1, :]))
                    up(v.tensor_copy(g.wn2p[half, half], half_w[half, 0, :]))
                    up(v.tensor_tensor(g.n3p[half, half], half_w[half, 1, :], g.ident[half, half], ALU.add))
                    up(v.tensor_tensor(g.n4p[half, half], half_w[half, 2, :], g.ident[half, half], ALU.add))
                up(v.memset(g.onesb[:, :], 1.0))
                for m, x in ((g.b4c, bsum), (g.bn2c, bn2)):
                    up(v.memset(pieces[:, :], 0.0))
                    for k in range(3):
                        up(v.tensor_copy(piece[:, :], x[:, :]))
                        v_n.here(v)
                        up(v.scalar_tensor_tensor(pieces[:, :], piece[:, :], g.ident[0:3, k:k + 1], pieces[:, :],
                                                  ALU.mult, ALU.add))
                        up(v.tensor_tensor(x[:, :], x[:, :], piece[:, :], ALU.subtract))
                        v_n.here(v)
                    up(v.tensor_copy(m[:, :, :], pieces[:, :].unsqueeze(1).broadcast_to([3, NG, D])))
                    v_n.here(v)

            @block.tensor
            def _(t):
                t.wait_ge(pc, PREP)
                t.wait_ge(ld, L[0])
                t.wait_ge(vc, steps["small"])
                t_n.up(t.transpose(ps[:, 0:D], wd[:, :, :].rearrange("p b i -> p (b i)"), g.ident[0:D, 0:D]))
                t_n.up(t.matmul(ps2[:, 0:2 * H], wd[:, :, :].rearrange("p b i -> p (b i)"),
                                abd[:, 0:2, :].rearrange("p k h -> p (k h)"), start=True, stop=True))
                t_n.up(t.matmul(ps3[0:P, 0:D], g.ones[0:D, 0:P], wea[:, :, :].rearrange("p h k -> p (h k)"),
                                start=True, stop=True))
                t.wait_ge(vc, steps["ps_free"])
                t_n.up(t.transpose(ps2[:, 0:D], wg2[:, :, :].rearrange("p g i -> p (g i)"), g.ident[0:D, 0:D]))
                t_n.up(t.transpose(ps[:, 0:D], ws2[:, :, :].rearrange("p b i -> p (b i)"), g.ident[0:D, 0:D]))
                t_n.up(t.matmul(ps3[:, 0:R], shift[:, :], u3[0:D, 0:R], start=True, stop=True))


def histogram(g):
    sem = g.sem
    onehot, used, filled, zeroed = sem("hist_onehot"), sem("hist_used"), sem("hist_filled"), sem("hist_zeros")
    rows_zeroed, cleared = sem("zero_rows_made"), sem("aggregates_cleared")
    vc, tc = sem("base_vector"), sem("base_tensor")
    with ExitStack() as ctx:
        hi = [g.sb(f"h_hi{b}", [P, 2, 2 * HB], BF16, ctx) for b in range(RING)]
        lo = [g.sb(f"h_lo{b}", [P, 2, LO], BF16, ctx) for b in range(RING)]
        zero = g.sb("h_zero", [P, 2 * LO], BF16, ctx)
        incl = g.sb("incl", [HB, 2, 2, LO], F32, ctx)
        total = g.sb("row_total", [HB, 2, 2], F32, ctx)
        prev = g.sb("row_prev", [HB, 2, 2], F32, ctx)
        before = g.sb("before", [HB, HB], F32, ctx)
        cnt = [g.ps(f"count{s}", [HB, 2 * LO], F32, ctx) for s in range(2)]
        rows = g.ps("rows", [HB, 4], F32, ctx)
        zero_rows = g.sb("zero_rows", [P, 512], F32, ctx)
        with g.nc.Block() as block:
            @block.sync
            def _(sp):
                sp.wait_ge(rows_zeroed, 1)
                for aggr in g.aggr:
                    sp.dma_start(aggr.rearrange("(p a k) d -> p a (k d)", p=P, k=512 // D),
                                 zero_rows[:, :].unsqueeze(1).broadcast_to([P, NK * D // 512, 512])).then_inc(cleared, 16)
                sp.wait_ge(cleared, 16 * len(g.aggr))

            @block.vector
            def _(v):
                v.memset(zero_rows[:, :], 0.0).then_inc(rows_zeroed, 1)
                v.memset(zero[:, :], 0.0).then_inc(zeroed, 1)
                v.sem_inc(used, RING)
                with v.Fori(0, EJ // RING) as i:
                    for b in range(RING):
                        j = i * RING + b
                        v.wait_ge(used, j + 1)
                        for s in range(2):
                            v.tensor_scalar(hi[b][:, s, :], g.iota[:, 0:2 * HB],
                                            g.keys[:, 2 * s, bass.ds(j, 1)], None, ALU.is_equal)
                            last = v.tensor_scalar(lo[b][:, s, :], g.iota[:, 0:LO],
                                                   g.keys[:, 2 * s + 1, bass.ds(j, 1)], None, ALU.is_equal)
                        last.then_inc(onehot, 1)
                n = Count(vc)
                n.up(v.memset(prev[:, :, :], 0.0))
                v.wait_ge(filled, 1)
                n.here(v)
                for s in range(2):
                    for h in range(2):
                        n.up(v.tensor_tensor_scan(incl[:, s, h, :], g.ones[0:HB, 0:1].broadcast_to([HB, LO]),
                                                  cnt[s][:, h * LO:(h + 1) * LO], 0.0, ALU.mult, ALU.add))
                n.here(v)
                n.up(v.tensor_copy(total[:, :, :], incl[:, :, :, LO - 1]))
                n.here(v)
                n.up(v.tensor_copy(prev[:, :, 1], total[:, :, 0]))
                v.wait_ge(tc, 1)
                for s in range(2):
                    n.up(v.tensor_tensor(g.base[:, s, :], incl[:, s, :, :].rearrange("p h l -> p (h l)"),
                                         cnt[s][:, :], ALU.subtract))
                n.here(v)
                for s in range(2):
                    for h in range(2):
                        k = 2 * s + h
                        n.up(v.tensor_scalar(g.base[:, s, h * LO:(h + 1) * LO],
                                             g.base[:, s, h * LO:(h + 1) * LO], rows[:, k:k + 1], None, ALU.add))

            @block.gpsimd
            def _(pool):
                n = Count(g.sem("before_mask"))
                n.up(pool.memset(before[:, :], 1.0))
                n.here(pool)
                n.up(pool.affine_select(out=before[:, :], in_=before[:, :], compare_op=ALU.is_gt, fill=0.0,
                                        base=0, pattern=[[1, HB]], channel_multiplier=-1))
                g.before_sem = n.sem
                n.up(pool.memset(g.strict[:, :], 1.0))
                n.here(pool)
                n.up(pool.affine_select(out=g.strict[:, :], in_=g.strict[:, :], compare_op=ALU.is_gt, fill=0.0,
                                        base=0, pattern=[[1, P]], channel_multiplier=-1))

            @block.tensor
            def _(t):
                t.wait_ge(zeroed, 1)
                for s in range(2):
                    t.matmul(cnt[s][:, :], zero[:, 0:HB], zero[:, :], start=True, stop=False,
                             skip_group_check=True)
                with t.Fori(0, EJ // RING) as i:
                    for b in range(RING):
                        t.wait_ge(onehot, i * RING + b + 1)
                        for s in range(2):
                            for h in range(2):
                                last = t.matmul(cnt[s][:, h * LO:(h + 1) * LO], hi[b][:, s, h * HB:(h + 1) * HB],
                                                lo[b][:, s, :], start=False, stop=False, skip_group_check=True)
                        last.then_inc(used, 1)
                for s in range(2):
                    last = t.matmul(cnt[s][:, :], zero[:, 0:HB], zero[:, :], start=False, stop=True,
                                    skip_group_check=True)
                last.then_inc(filled, 1)
                t.wait_ge(g.before_sem, 2)
                t.wait_ge(vc, 7)
                t.matmul(rows[:, :], before[:, :], total[:, :, :].rearrange("p s h -> p (s h)"),
                         start=True, stop=False)
                t.matmul(rows[:, :], g.ones[0:HB, 0:HB], prev[:, :, :].rearrange("p s h -> p (s h)"),
                         start=False, stop=True).then_inc(tc, 1)


def rank_and_scatter(g):
    sem = g.sem
    two = lambda n: [sem(f"{n}{s}") for s in range(2)]
    onehot, placed, summed, looked = sem("rank_onehot"), sem("rank_placed"), sem("rank_summed"), sem("rank_looked")
    turned, turned_out, same, masked = sem("rank_turned"), sem("rank_turned_out"), sem("rank_same"), sem("rank_masked")
    table_up, table_out = two("table_up"), two("table_out")
    staged, sent = sem("rank_staged"), [g.once(f"rank_sent{b}") for b in range(2)]
    RC = 4
    with ExitStack() as ctx:
        hi = [g.sb(f"r_hi{b}", [P, 2, 2 * HB], BF16, ctx) for b in range(RING)]
        lo = [g.sb(f"r_lo{b}", [P, 2, LO], BF16, ctx) for b in range(RING)]
        hit = [g.sb(f"hi_t{b}", [HB, 2, 2, P], F32, ctx) for b in range(2)]
        hitb = [g.sb(f"hi_tb{b}", [HB, 2, 2, P], BF16, ctx) for b in range(2)]
        tab = [[g.sb(f"tab_sb{s}{b}", [HB, 2 * LO], F32, ctx) for b in range(2)] for s in range(2)]
        eq = [g.sb(f"eq{b}", [P, 2, P], BF16, ctx) for b in range(2)]
        junk = g.sb("rank_junk", [P, LO], F32, ctx)
        one = g.sb("one_place", [P, 2, 2], F32, ctx)
        place = g.sb("place", [P, EJ, 2], F32, ctx)
        pidx = [g.sb(f"pidx{b}", [P, 2, RC], I32, ctx) for b in range(2)]
        stage = [g.sb(f"rstage{b}", [P, RC, REC], F32, ctx) for b in range(2)]
        t_ps = [g.ps(f"hit_ps{b}", [HB, 2, 2, 128], BF16, ctx) for b in range(2)]
        e_ps = [g.ps(f"eq_ps{b}", [P, 2, P], F32, ctx) for b in range(2)]
        l_ps = [g.ps(f"look_ps{b}", [P, 2, LO], F32, ctx) for b in range(2)]
        tab_ps = [g.ps(f"tab_ps{s}", [HB, 2 * LO], F32, ctx) for s in range(2)]
        with g.nc.Block() as block:
            @block.vector
            def _(v):
                v.sem_inc(placed, 2)

                def onehots(q, j):
                    for s in range(2):
                        v.tensor_scalar(hi[q][:, s, :], g.iota[:, 0:2 * HB],
                                        g.keys[:, 2 * s, bass.ds(j, 1)], None, ALU.is_equal)
                        v.tensor_scalar(lo[q][:, s, :], g.iota[:, 0:LO],
                                        g.keys[:, 2 * s + 1, bass.ds(j, 1)], None, ALU.is_equal
                                        ).then_inc(onehot, 1)

                def mask(b):
                    v.tensor_tensor(eq[b][:, :, :], e_ps[b][:, :, :], g.strict[:, :].unsqueeze(1).broadcast_to([P, 2, P]),
                                    ALU.mult).then_inc(masked, 1)

                for q in range(2):
                    onehots(q, q)
                v.wait_ge(same, 1)
                mask(0)
                with v.Fori(0, EJ // RING) as i:
                    for q in range(RING):
                        j, b = i * RING + q, q % 2
                        v.wait_ge(looked, j + 1)
                        onehots((q + 2) % RING, j + 2)
                        v.wait_ge(same, j + 2)
                        mask(1 - b)
                        v.wait_ge(looked, j + 2)
                        for s in range(2):
                            v.tensor_tensor_reduce(junk[:, :], l_ps[b][:, s, :], lo[q][:, s, :], 1.0, 0.0,
                                                   ALU.mult, ALU.add, one[:, b, s:s + 1]).then_inc(summed, 1)
                            v.wait_ge(summed, j * 2 + s + 1)
                        v.tensor_copy(place[:, bass.ds(j, 1), :], one[:, b, :].unsqueeze(1)).then_inc(placed, 1)

            @block.tensor
            def _(t):
                for s in range(2):
                    t.matmul(tab_ps[s][:, :], g.ident[0:HB, 0:HB], g.base[:, s, :], start=True, stop=False,
                             skip_group_check=True).then_inc(table_up[s], 1)
                t.sem_inc(looked, 1)

                def turn(q, b):
                    for s in range(2):
                        for h in range(2):
                            last = t.transpose(t_ps[b][:, s, h, 0:P], hi[q][:, s, h * HB:(h + 1) * HB], g.identb[0:P, 0:P])
                    last.then_inc(turned, 1)

                def match(b):
                    for s in range(2):
                        for h in range(2):
                            last = t.matmul(e_ps[b][:, s, :], hitb[b][:, s, h, :], hitb[b][:, s, h, :],
                                            start=(h == 0), stop=(h == 1))
                    last.then_inc(same, 1)

                t.wait_ge(onehot, 2)
                turn(0, 0)
                t.wait_ge(turned_out, 2)
                match(0)
                with t.Fori(0, EJ // RING) as i:
                    for q in range(RING):
                        j, b = i * RING + q, q % 2
                        t.wait_ge(onehot, j * 2 + 4)
                        turn((q + 1) % RING, 1 - b)
                        t.wait_ge(turned_out, j * 2 + 2)
                        for s in range(2):
                            t.wait_ge(table_out[s], j + 1)
                            for h in range(2):
                                last = t.matmul(tab_ps[s][:, h * LO:(h + 1) * LO],
                                                hi[q][:, s, h * HB:(h + 1) * HB], lo[q][:, s, :],
                                                start=False, stop=False, skip_group_check=True)
                            last.then_inc(table_up[s], 1)
                        t.wait_ge(placed, j + 1)
                        for s in range(2):
                            if s == 1:
                                t.wait_ge(turned_out, j * 2 + 3)
                                match(1 - b)
                            for h in range(2):
                                t.matmul(l_ps[b][:, s, :], hit[b][:, s, h, :], tab[s][b][:, h * LO:(h + 1) * LO],
                                         start=(h == 0), stop=False)
                            t.wait_ge(masked, j + 1)
                            last = t.matmul(l_ps[b][:, s, :], eq[b][:, s, :], lo[q][:, s, :], start=False, stop=True)
                        last.then_inc(looked, 1)

            @block.scalar
            def _(a):
                def copy_turned(b):
                    part = t_ps[b][:, :, :, 0:P]
                    a.activation(hitb[b][:, :, :, :], part, ACT.Copy).then_inc(turned_out, 1)
                    a.activation(hit[b][:, :, :, :], part, ACT.Copy).then_inc(turned_out, 1)

                def copy_table(s, b):
                    a.activation(tab[s][b][:, :], tab_ps[s][:, :], ACT.Copy).then_inc(table_out[s], 1)

                for s in range(2):
                    a.wait_ge(table_up[s], 1)
                    copy_table(s, 0)
                a.wait_ge(turned, 1)
                copy_turned(0)
                with a.Fori(0, EJ // RING) as i:
                    for q in range(RING):
                        j, b = i * RING + q, q % 2
                        a.wait_ge(looked, j + 1)
                        a.wait_ge(turned, j + 2)
                        copy_turned(1 - b)
                        for s in range(2):
                            a.wait_ge(table_up[s], j + 2)
                            copy_table(s, 1 - b)

            @block.gpsimd
            def _(pool):
                def turn(c, b, has):
                    n = LoopCount(staged, 3, g=g)
                    pool.wait_ge(placed, c * RC + (RC + 2))
                    g.passed(pool)
                    if has(-2):
                        pool.wait_ge(sent[b], (c - b) * (16 * RC))
                        g.passed(pool)
                    for s in range(2):
                        n.up(pool.tensor_copy(pidx[b][:, s, :], place[:, bass.ds(c * RC, RC), s]))
                    n.up(pool.tensor_copy(stage[b][:, :, :], g.rec[:, bass.ds(c * RC, RC), :]))
                    n.here(pool, c)
                    for s in range(2):
                        for k in range(RC):
                            pool.indirect_dma_start(
                                out=g.sorted[s][:, :],
                                out_offset=bass.IndirectOffsetOnAxis(ap=pidx[b][:, s, k:k + 1], axis=0),
                                in_=stage[b][:, k, :], in_offset=None,
                                bounds_check=E - 1, oob_is_err=False).then_inc(sent[b], 16)

                turns(pool, EJ // RC, 2, turn, 0, EJ // RC - 1)
                for b in range(2):
                    pool.wait_ge(sent[b], EJ * 16)


def read_orders(g):
    ld, pc, vc = g.sem("orders_loaded"), g.sem("orders_pool"), g.sem("orders_vector")
    with ExitStack() as ctx:
        nxt = [g.sb(f"next{s}", [P, 1], F32, ctx) for s in range(2)]
        prv = [g.sb(f"prev{s}", [P, 1], F32, ctx) for s in range(2)]
        rec = [g.sb(f"sorted_rec{s}", [P, EJ, REC], F32, ctx) for s in range(2)]
        same = g.sb("same_next", [P, EJ], F32, ctx)
        rowf = g.sb("rowf", [P, EJ], F32, ctx)
        with g.nc.Block() as block:
            @block.gpsimd
            def _(pool):
                for s in range(2):
                    pool.memset(nxt[s][:, :], -1.0).then_inc(pc, 1)
                    pool.memset(prv[s][:, :], -1.0).then_inc(pc, 1)

            @block.sync
            def _(sp):
                sp.wait_ge(pc, 4)
                for s, f in ((0, DST), (1, SRC)):
                    flat = g.sorted[s].rearrange("(p j) r -> p j r", p=P)
                    sp.dma_start(rec[s][:, :, :], flat).then_inc(ld, 16)
                    sp.dma_start(prv[s][1:P, :], flat[0:P - 1, EJ - 1, f:f + 1],
                                 allow_slow_non_contiguous=True).then_inc(ld, 16)
                    sp.dma_start(nxt[s][0:P - 1, :], flat[1:P, 0, f:f + 1],
                                 allow_slow_non_contiguous=True).then_inc(ld, 16)

            @block.vector
            def _(v):
                n = Count(vc)
                v.wait_ge(ld, 96)
                for s, f in ((0, DST), (1, SRC)):
                    key = rec[s][:, :, f]
                    for k, e in ((0, SRC), (1, DST)):
                        n.up(v.tensor_copy(g.ends_of[s][:, k, :], rec[s][:, :, e]))
                    n.up(v.tensor_tensor(g.cont[s][:, 1:], key[:, 1:], key[:, 0:EJ - 1], ALU.is_equal))
                    n.up(v.tensor_tensor(g.cont[s][:, 0:1], key[:, 0:1], prv[s][:, :], ALU.is_equal))
                    n.here(v)
                    n.up(v.tensor_tensor(same[:, 0:EJ - 1], key[:, 0:EJ - 1], key[:, 1:], ALU.is_equal))
                    n.up(v.tensor_tensor(same[:, EJ - 1:], key[:, EJ - 1:], nxt[s][:, :], ALU.is_equal))
                    n.here(v)
                    n.up(v.scalar_tensor_tensor(rowf[:, :], same[:, :], SKIP, key, ALU.mult, ALU.add))
                    if s == 0:
                        n.up(v.tensor_copy(g.goes_on[:, :], same[:, :]))
                    n.here(v)
                    n.up(v.tensor_copy(g.out_row[s][:, :], rowf[:, :]))
                    n.up(v.tensor_tensor_scan(g.open[s][:, :], g.cont[s][:, :], g.ones[0:P, 0:1].broadcast_to([P, EJ]),
                                              1.0, ALU.mult, ALU.mult))
                    n.here(v)
                n.up(v.tensor_copy(g.etype[:, :], rec[0][:, :, TYPE]))
                n.up(v.tensor_copy(g.radial[:, :], rec[1][:, :, RADIAL]))
                n.up(v.tensor_copy(g.attn[:, :, :], rec[0][:, :, ATT:ATT + H].rearrange("p j h -> p h j")))
                n.here(v)


def gather(pool, g, rows, table, i, b, c, idx, dst, free, ready, n):
    pool.wait_ge(free, c + 1)
    g.passed(pool)
    for k in range(2):
        n.up(pool.tensor_copy(idx[:, k, :], rows[:, k, bass.ds(c * G, G)]))
    n.here(pool, i)
    for t in range(G):
        for k in range(2):
            pool.indirect_dma_start(out=dst[:, t, k * D:(k + 1) * D], out_offset=None, in_=table,
                                    in_offset=bass.IndirectOffsetOnAxis(ap=idx[:, k, t:t + 1], axis=0),
                                    bounds_check=N - 1, oob_is_err=False).then_inc(ready[b], 16)


def message_edges(g):
    sem = lambda n: g.sem(f"{n}_e")
    row_ready, copied = [g.once(f"rows_ready{b}_e1") for b in range(2)], sem("idx_copied")
    turned, turned_out, made, made_free = sem("turned"), sem("turned_out"), sem("made"), sem("made_free")
    hidden, hidden_out = [sem(f"hidden{k}") for k in range(3)], [sem(f"hidden_out{k}") for k in range(3)]
    diag_ready, msg_ready = sem("diag"), sem("msg")
    with ExitStack() as ctx:
        sb = lambda n, s, d=F32: g.sb(f"{n}_e1", s, d, ctx)
        ps = lambda n, s, d=F32: g.ps(f"{n}_e1", s, d, ctx)
        idx = [sb(f"idx{b}", [P, 2, G], I32) for b in range(2)]
        rows = [sb(f"rows{b}", [P, G, 2 * D]) for b in range(2)]
        xt = [sb(f"xt{b}", [128, G * P]) for b in range(2)]
        first, gate, msg = sb("first", [D, G * P]), sb("gate", [D, G * P]), sb("msg", [D, G * P])
        second = [sb(f"second{b}", [D, G * P]) for b in range(2)]
        diag = [sb(f"diag{b}", [P, G, P]) for b in range(2)]
        tp = [ps(f"tp{b}", [128, G * P]) for b in range(2)]
        h_ps = [ps(f"h{k}", [D, G * P]) for k in range(3)]
        out = [ps(f"out{b}", [P, G, D]) for b in range(2)]
        with g.nc.Block() as block:
            @block.gpsimd
            def _(pool):
                n = LoopCount(copied, 4, g=g)
                with pool.Fori(0, CH // 2) as i:
                    for b in range(2):
                        gather(pool, g, g.ends_of[1], g.feat[1], i, b, i * 2 + b, idx[b], rows[b], turned, row_ready, n)

            @block.tensor
            def _(t):
                t.sem_inc(turned, 2)

                def turn(c, b, has):
                    o = 1 - b
                    if has(0):
                        t.wait_ge(row_ready[b], (c - b) * (16 * G) + 32 * G)
                        for k in range(G):
                            last = t.transpose(tp[b][:, k * P:(k + 1) * P], rows[b][:, k, :], g.ident[0:P, 0:P])
                        last.then_inc(turned, 1)
                    if has(-3):
                        t.wait_ge(msg_ready, c - 2)
                        g.passed(t)
                        if has(-5):
                            t.wait_ge(made_free, c - 4)
                            g.passed(t)
                        for k in range(G):
                            last = t.transpose(out[o][:, k, :], msg[:, k * P:(k + 1) * P], g.ident[0:D, 0:D])
                        last.then_inc(made, 1)
                    if has(-1):
                        t.wait_ge(hidden_out[0], c)
                        g.passed(t)
                        t.matmul(h_ps[1][:, :], g.w2[:, :], first[:, :], start=True, stop=True).then_inc(hidden[1], 1)
                    if has(-2):
                        t.wait_ge(hidden_out[1], c - 1)
                        g.passed(t)
                        t.matmul(h_ps[2][:, :], g.wa[:, :], second[b][:, :], start=True, stop=True).then_inc(hidden[2], 1)
                    if has(0):
                        t.wait_ge(turned_out, c + 1)
                        t.matmul(h_ps[0][:, :], g.w1a[:, :], xt[b][:, :], start=True, stop=False)
                        t.wait_ge(diag_ready, c + 1)
                        t.matmul(h_ps[0][:, :], g.w1r[:, :], diag[b][:, :, :].rearrange("p k e -> p (k e)"),
                                 start=False, stop=True).then_inc(hidden[0], 1)

                turns(t, CH, 6, turn, 0, CH + 2)

            @block.scalar
            def _(a):
                def turn(c, b, has):
                    o = 1 - b
                    if has(0):
                        a.wait_ge(turned, c + 3)
                        if has(-2):
                            a.wait_ge(hidden[0], c - 1)
                        a.activation(xt[b][:, :], tp[b][:, :], ACT.Copy).then_inc(turned_out, 1)
                    if has(-1):
                        a.wait_ge(hidden[1], c)
                        if has(-3):
                            a.wait_ge(msg_ready, c - 2)
                        a.activation(second[o][:, :], h_ps[1][:, :], ACT.Silu, bias=g.be2[:, 0:1]).then_inc(hidden_out[1], 1)
                    if has(-2):
                        a.wait_ge(hidden[2], c - 1)
                        a.activation(gate[:, :], h_ps[2][:, :], ACT.Sigmoid, bias=g.ba[:, 0:1]).then_inc(hidden_out[2], 1)
                    if has(0):
                        a.wait_ge(hidden[0], c + 1)
                        a.activation(first[:, :], h_ps[0][:, :], ACT.Silu, bias=g.be1[:, 0:1]).then_inc(hidden_out[0], 1)

                turns(a, CH, 6, turn, 0, CH + 1)

            @block.vector
            def _(v):
                def turn(c, b, has):
                    o = 1 - b
                    if has(1):
                        if has(-1):
                            v.wait_ge(hidden[0], c)
                        v.tensor_tensor(diag[o][:, :, :], g.ident[0:P, 0:P].unsqueeze(1).broadcast_to([P, G, P]),
                                        g.radial[:, bass.ds((c + 1) * G, G)].unsqueeze(2).broadcast_to([P, G, P]), ALU.mult
                                        ).then_inc(diag_ready, 1)
                    if has(-3):
                        v.wait_ge(made, c - 2)
                        v.tensor_copy(g.val[:, bass.ds((c - 3) * G, G), :], out[o][:, :, :]).then_inc(made_free, 1)
                    if has(-2):
                        v.wait_ge(hidden_out[2], c - 1)
                        v.tensor_tensor(msg[:, :], second[b][:, :], gate[:, :], ALU.mult).then_inc(msg_ready, 1)

                turns(v, CH, 6, turn, -1, CH + 2)


def group_edges(g):
    sem = lambda n: g.sem(f"{n}_e")
    row_ready, copied = [g.once(f"rows_ready{q}_e2") for q in range(4)], sem("idx_copied")
    turned, turned_out, made, made_free = sem("turned"), sem("turned_out"), sem("made"), sem("made_free")
    picked, masked = sem("picked"), sem("masked")
    with ExitStack() as ctx:
        sb = lambda n, s, d=F32: g.sb(f"{n}_e2", s, d, ctx)
        idx = [sb(f"idx{q}", [P, G], I32) for q in range(4)]
        lrow = [sb(f"lrow{q}", [P, G, g.LW]) for q in range(4)]
        rows = [sb(f"rows{b}", [P, G, 2 * D]) for b in range(2)]
        pick = [sb(f"pick{b}", [P, 2, G]) for b in range(2)]
        xt = [sb(f"xt{b}", [128, G * P]) for b in range(2)]
        tp = [g.ps(f"tp{b}_e2", [128, G * P], F32, ctx) for b in range(2)]
        out = [g.ps(f"out{b}_e2", [P, G, D], F32, ctx) for b in range(2)]
        all_turns = lambda eng, turn, first, last: turns(eng, CH, 5, turn, first, last, ring=4)
        with g.nc.Block() as block:
            @block.gpsimd
            def _(pool):
                def turn(c, q, has):
                    if has(-4):
                        pool.wait_ge(masked, c - 3)
                        g.passed(pool)
                    pool.tensor_copy(idx[q][:, :], g.ends_of[0][:, 0, bass.ds(c * G, G)]).then_inc(copied, 1)
                    pool.wait_ge(copied, c + 1)
                    g.passed(pool)
                    for t in range(G):
                        pool.indirect_dma_start(out=lrow[q][:, t, :], out_offset=None, in_=g.labelled,
                                                in_offset=bass.IndirectOffsetOnAxis(ap=idx[q][:, t:t + 1], axis=0),
                                                bounds_check=N - 1, oob_is_err=False).then_inc(row_ready[q], 16)

                all_turns(pool, turn, 0, CH - 1)

            @block.tensor
            def _(t):
                def turn(c, q, has):
                    b, o = q % 2, (q + 1) % 2
                    if has(0):
                        t.wait_ge(masked, c + 1)
                        for k in range(G):
                            last = t.transpose(tp[b][:, k * P:(k + 1) * P], rows[b][:, k, :], g.ident[0:P, 0:P])
                        last.then_inc(turned, 1)
                    if has(-1):
                        t.wait_ge(turned_out, c)
                        if has(-3):
                            t.wait_ge(made_free, c - 2)
                        for k in range(G):
                            last = t.matmul(out[o][:, k, :], xt[o][:, k * P:(k + 1) * P], g.wg[:, :],
                                            start=True, stop=True)
                        last.then_inc(made, 1)

                all_turns(t, turn, 0, CH)

            @block.scalar
            def _(a):
                def turn(c, q, has):
                    b = q % 2
                    a.wait_ge(turned, c + 1)
                    if has(-2):
                        a.wait_ge(made, c - 1)
                    a.activation(xt[b][:, :], tp[b][:, :], ACT.Copy).then_inc(turned_out, 1)

                all_turns(a, turn, 0, CH - 1)

            @block.vector
            def _(v):
                def turn(c, q, has):
                    b, o = q % 2, (q + 1) % 2
                    if has(0):
                        v.wait_ge(row_ready[q], (c - q) * (4 * G) + 16 * G)
                        if has(-2):
                            v.wait_ge(turned, c - 1)
                        for k in range(2):
                            v.tensor_scalar(pick[b][:, k, :], lrow[q][:, :, D], float(k), None, ALU.is_equal
                                            ).then_inc(picked, 1)
                        v.wait_ge(picked, c * 2 + 2)
                        for k in range(2):
                            last = v.tensor_tensor(rows[b][:, :, k * D:(k + 1) * D], lrow[q][:, :, 0:D],
                                                   pick[b][:, k, :].unsqueeze(2).broadcast_to([P, G, D]), ALU.mult)
                        last.then_inc(masked, 1)
                    if has(-1):
                        v.wait_ge(made, c)
                        v.tensor_copy(g.val[:, bass.ds((c - 1) * G, G), :], out[o][:, :, :]).then_inc(made_free, 1)

                all_turns(v, turn, 0, CH)


def edges(g, layer):
    if layer == 1:
        return message_edges(g)
    if layer == 2:
        return group_edges(g)
    sem = lambda n: g.sem(f"{n}_e")
    row_free, row_ready, copied = sem("rows_free"), [g.once(f"rows_ready{b}_e{layer}") for b in range(2)], sem("idx_copied")
    turned, turned_out, turned_free = sem("turned"), sem("turned_out"), sem("turned_free")
    made, made_free = sem("made"), sem("made_free")
    with ExitStack() as ctx:
        sb = lambda n, s, d=F32: g.sb(f"{n}_e{layer}", s, d, ctx)
        ps = lambda n, s, d=F32: g.ps(f"{n}_e{layer}", s, d, ctx)
        idx = [sb(f"idx{b}", [P, 2, G], I32) for b in range(2)]
        rows = [sb(f"rows{b}", [P, G, 2 * D]) for b in range(2)]
        xt = [sb(f"xt{b}", [128, G * P]) for b in range(2)]
        tp = [ps(f"tp{b}", [128, G * P]) for b in range(2)]
        if layer == 0:
            W = D + 2 * H
            out = [ps(f"out{b}", [P, G, W]) for b in range(2)]
        if layer == 3:
            hr = [ps(f"hr{b}", [P, R * D]) for b in range(2)]
            sc = [ps(f"sc{b}", [P, G, 2 * R]) for b in range(2)]
            prod = [sb(f"prod{b}", [P, R * D]) for b in range(2)]
            pick = [sb(f"pick{b}", [P, G, R]) for b in range(2)]
            psc = sb("psc", [P, 2, G, R])
            hr_ready, hr_free, step = sem("hr_ready"), sem("hr_free"), sem("select_steps")

        with g.nc.Block() as block:
            @block.gpsimd
            def _(pool):
                n = LoopCount(copied, 4, g=g)
                with pool.Fori(0, CH // 2) as i:
                    for b in range(2):
                        gather(pool, g, g.ends_of[0], g.feat[layer], i, b, i * 2 + b, idx[b], rows[b], row_free,
                               row_ready, n)

            @block.tensor
            def _(t):
                t.sem_inc(row_free, 2)
                t.sem_inc(turned_free, 2)
                with t.Fori(0, CH // 2) as i:
                    for b in range(2):
                        c = i * 2 + b
                        t.wait_ge(row_ready[b], i * (32 * G) + 32 * G)
                        for k in range(G):
                            last = t.transpose(tp[b][:, k * P:(k + 1) * P], rows[b][:, k, :], g.ident[0:P, 0:P])
                        last.then_inc(turned, 1)
                        t.wait_ge(turned, c + 1)
                        t.sem_inc(row_free, 1)
                        t.wait_ge(turned_out, c + 1)
                        if layer == 0:
                            t.wait_ge(made_free, c + 1)
                            for k in range(G):
                                last = t.matmul(out[b][:, k, :], xt[b][:, k * P:(k + 1) * P], g.w0[:, :],
                                                start=True, stop=True)
                            last.then_inc(made, 1)
                            t.wait_ge(made, c + 1)
                            t.sem_inc(turned_free, 1)
                        if layer == 3:
                            t.wait_ge(made_free, c + 1)
                            for k in range(G):
                                last = t.matmul(sc[b][:, k, :], xt[b][:, k * P:(k + 1) * P], g.w3s[:, :],
                                                start=True, stop=True)
                            last.then_inc(made, 1)
                            for k in range(G):
                                t.wait_ge(hr_free, c * G + k + 1)
                                t.matmul(hr[k % 2][:, :], xt[b][:, k * P:(k + 1) * P], g.w3[:, :],
                                         start=True, stop=True).then_inc(hr_ready, 1)
                            t.wait_ge(hr_ready, c * G + G)
                            t.sem_inc(turned_free, 1)

            @block.scalar
            def _(a):
                with a.Fori(0, CH // 2) as i:
                    for b in range(2):
                        c = i * 2 + b
                        a.wait_ge(turned, c + 1)
                        a.wait_ge(turned_free, c + 1)
                        a.activation(xt[b][:, :], tp[b][:, :], ACT.Copy).then_inc(turned_out, 1)

            @block.vector
            def _(v):
                v.sem_inc(made_free, 2)
                if layer == 3:
                    v.sem_inc(hr_free, 2)
                    n = LoopCount(step, 2 * (3 + 2 * G))
                with v.Fori(0, CH // 2) as i:
                    for b in range(2):
                        c = i * 2 + b
                        at = bass.ds(c * G, G)
                        v.wait_ge(made, c + 1)
                        if layer == 0:
                            v.tensor_copy(g.val[:, at, :], out[b][:, :, 0:D])
                            v.tensor_copy(g.score[:, :, at], out[b][:, :, D:].rearrange("p j h -> p h j")
                                          ).then_inc(made_free, 1)
                        if layer == 3:
                            n.up(v.tensor_tensor(pick[b][:, :, :], g.iotaf[:, 0:R].unsqueeze(1).broadcast_to([P, G, R]),
                                                 g.etype[:, at].unsqueeze(2).broadcast_to([P, G, R]), ALU.is_equal))
                            n.here(v, i)
                            for k in range(2):
                                last = v.tensor_tensor(psc[:, k, :, :], sc[b][:, :, k * R:(k + 1) * R],
                                                       pick[b][:, :, :], ALU.mult)
                            n.up(last)
                            n.here(v, i)
                            v.sem_inc(made_free, 1)
                            n.up(v.tensor_reduce(g.score[:, 0:2, at], psc[:, :, :, :], AX.X, ALU.add))
                            for k in range(G):
                                v.wait_ge(hr_ready, c * G + k + 1)
                                n.up(v.tensor_tensor(prod[k % 2][:, :].rearrange("p (r f) -> p r f", r=R),
                                                     hr[k % 2][:, :].rearrange("p (r f) -> p r f", r=R),
                                                     pick[b][:, k, :].unsqueeze(2).broadcast_to([P, R, D]),
                                                     ALU.mult))
                                n.here(v, i)
                                v.sem_inc(hr_free, 1)
                                n.up(v.tensor_reduce(g.val[:, bass.ds(c * G + k, 1), :].rearrange("p a f -> p (a f)"),
                                                     prod[k % 2][:, :].rearrange("p (r f) -> p f r", r=R),
                                                     AX.X, ALU.add))
                                n.here(v, i)


def carry_on(eng, n, turned, g, k, A, B, C, out, a_sb, row, a_ps, b_ps, c_ps, op0, op1, init, back=False):
    n.here(eng)
    g.carries.append(n.n)
    eng.wait_ge(turned, 2 * k + 1)
    n.up(eng.tensor_copy(a_sb[0:C, :], a_ps[0:C, 0:P]))
    n.up(eng.memset(row[0:C, :], init))
    n.here(eng)
    if back:
        n.up(eng.tensor_tensor_scan(row[0:C, P - 1::-1], a_sb[0:C, P - 1::-1], b_ps[0:C, P - 1::-1],
                                    init, op0, op1))
    else:
        n.up(eng.tensor_tensor_scan(row[0:C, 1:P + 1], a_sb[0:C, :], b_ps[0:C, 0:P], init, op0, op1))
    g.carries.append(n.n)
    eng.wait_ge(turned, 2 * k + 2)
    n.up(eng.tensor_copy(out, c_ps[0:P, 0:C]))
    n.here(eng)


def turn_carries(t, g, vec, turned, sizes, A, B, row, a_ps, b_ps, c_ps):
    for k, (C, back) in enumerate(sizes):
        t.wait_ge(vec, g.carries[2 * k])
        t.transpose(a_ps[0:C, 0:P], A[:, 0:C], g.ident[0:P, 0:P])
        t.transpose(b_ps[0:C, 0:P], B[:, 0:C], g.ident[0:P, 0:P]).then_inc(turned, 1)
        t.wait_ge(vec, g.carries[2 * k + 1])
        off = 1 if back else 0
        t.transpose(c_ps[0:P, 0:C], row[0:C, off:off + P], g.ident[0:C, 0:C]).then_inc(turned, 1)


def segments(g, layer):
    order = 1 if layer == 1 else 0
    vec, sca, ten, scans = [g.sem(f"{n}_m") for n in ("vector", "scalar", "tensor", "scans")]
    g.carries = []
    BC = lambda ap, *s: ap.broadcast_to(list(s))
    with ExitStack() as ctx:
        sb = lambda n, s, d=F32: g.sb(f"{n}_m{layer}", s, d, ctx)
        A, B, a_sb, row = sb("A", [P, D]), sb("B", [P, D]), sb("a_sb", [D, P]), sb("row", [D, P + 1])
        a_ps, b_ps, c_ps = [g.ps(f"{n}_m{layer}", [128, 128], F32, ctx) for n in ("a_ps", "b_ps", "c_ps")]
        cont, opn = g.cont[order], g.open[order]
        if layer == 0:
            C = H
            lm, es, m, d = sb("lm", [P, C, EJ]), sb("es", [P, C, EJ]), sb("m", [P, C, EJ + 1]), sb("d", [P, C, EJ])
            w, wself, fac, z, cm = (sb("w", [P, C, EJ]), sb("ws", [P, C, EJ]), sb("fac", [P, C, EJ]),
                                    sb("z", [P, C, EJ]), sb("cm", [P, C]))
            drop, lowered, first = sb("drop", [P, EJ]), sb("lowered", [P, EJ]), sb("first", [P, EJ])
            sizes = [(H, False), (H, False), (D, False)]
        if layer == 3:
            C = R
            mask, neg, y = sb("mask", [P, R, EJ]), sb("neg", [P, R, EJ]), sb("y", [P, R, EJ])
            f = sb("f", [P, R, EJ])
            lm, es, sel = sb("lm", [P, EJ]), sb("es", [P, EJ]), sb("sel", [P, EJ])
            w, drop, lowered, cm = sb("w", [P, EJ]), sb("drop", [P, EJ]), sb("lowered", [P, EJ]), sb("cm", [P, R])
            ends, cback = sb("ends", [P, EJ]), sb("cback", [P, R])
            openb = sb("openb", [P, EJ])
            sizes = [(R, False), (R, True), (R, False), (R, True), (D, False)]
        if layer in (1, 2):
            sizes = [(D, False)]

        with g.nc.Block() as block:
            @block.vector
            def _(v):
                n = Count(vec)
                acts = [0]

                def scalar_done():
                    acts[0] += 1
                    v.wait_ge(sca, acts[0])

                def up(ins):
                    n.up(ins)
                    n.here(v)

                def carry(out, Cn, op0, op1, init, back=False):
                    k = len(g.carries) // 2
                    carry_on(v, n, ten, g, k, A, B, Cn, out, a_sb, row, a_ps, b_ps, c_ps, op0, op1, init, back)

                def leaky(out, ap, slope):
                    up(v.scalar_tensor_tensor(out, ap, slope, ap, ALU.mult, ALU.max))

                if layer == 0:
                    up(v.tensor_tensor(lm[:, :, :], g.score[:, 0:H, :], g.attn[:, :, :], ALU.add))
                    leaky(lm[:, :, :], lm[:, :, :], 0.01)
                    leaky(es[:, :, :], g.score[:, H:, :], 0.01)
                    up(v.tensor_tensor(d[:, :, :], lm[:, :, :], es[:, :, :], ALU.max))
                    up(v.tensor_scalar(drop[:, :], cont[:, :], 1.0, BIG, ALU.subtract, ALU.mult))
                    up(v.tensor_scalar(lowered[:, :], opn[:, :], 1.0, BIG, ALU.subtract, ALU.mult))
                    up(v.tensor_scalar(first[:, :], cont[:, :], -1.0, 1.0, ALU.mult, ALU.add))
                    for h in range(H):
                        up(v.tensor_tensor_scan(m[:, h, 1:], drop[:, :], d[:, h, :], -BIG, ALU.add, ALU.max))
                    up(v.tensor_copy(A[:, 0:H], BC(lowered[:, EJ - 1:], P, H)))
                    up(v.tensor_copy(B[:, 0:H], m[:, :, EJ]))
                    carry(cm[:, :], H, ALU.add, ALU.max, -BIG)
                    for h in range(H):
                        up(v.scalar_tensor_tensor(m[:, h, 1:], lowered[:, :], cm[:, h:h + 1], m[:, h, 1:],
                                                  ALU.add, ALU.max))
                    up(v.tensor_copy(m[:, :, 0], cm[:, :]))
                    up(v.tensor_tensor(fac[:, :, :], m[:, :, 0:EJ], m[:, :, 1:], ALU.subtract))
                    up(v.tensor_scalar(fac[:, :, :], fac[:, :, :], 0.0, None, ALU.min))
                    up(v.tensor_tensor(w[:, :, :], lm[:, :, :], m[:, :, 1:], ALU.subtract))
                    up(v.tensor_tensor(wself[:, :, :], es[:, :, :], m[:, :, 1:], ALU.subtract))
                    g.exp_in = n.n
                    scalar_done()
                    up(v.tensor_tensor(fac[:, :, :], fac[:, :, :], BC(cont[:, :].unsqueeze(1), P, H, EJ), ALU.mult))
                    up(v.tensor_tensor(d[:, :, :], wself[:, :, :], BC(first[:, :].unsqueeze(1), P, H, EJ), ALU.mult))
                    up(v.tensor_tensor(d[:, :, :], d[:, :, :], w[:, :, :], ALU.add))
                    for h in range(H):
                        up(v.tensor_tensor_scan(z[:, h, :], fac[:, h, :], d[:, h, :], 0.0, ALU.mult, ALU.add))
                        up(v.tensor_tensor_scan(g.reach[:, h, :], fac[:, h, :], BC(g.ones[0:P, 0:1], P, EJ),
                                                1.0, ALU.mult, ALU.mult))
                    up(v.tensor_copy(A[:, 0:H], g.reach[:, :, EJ - 1]))
                    up(v.tensor_copy(B[:, 0:H], z[:, :, EJ - 1]))
                    carry(cm[:, :], H, ALU.mult, ALU.add, 0.0)
                    for h in range(H):
                        up(v.scalar_tensor_tensor(z[:, h, :], g.reach[:, h, :], cm[:, h:h + 1], z[:, h, :],
                                                  ALU.mult, ALU.add))
                    up(v.reciprocal(g.rz[:, :, :], z[:, :, :]))
                    for h in range(H):
                        part = g.val[:, :, h * HF:(h + 1) * HF]
                        up(v.tensor_tensor(part, part, BC(w[:, h, :].unsqueeze(2), P, EJ, HF), ALU.mult))
                if layer == 3:
                    leaky(lm[:, :], g.score[:, 0, :], 0.2)
                    leaky(es[:, :], g.score[:, 1, :], 0.2)
                    up(v.tensor_tensor(sel[:, :], lm[:, :], es[:, :], ALU.max))
                    up(v.tensor_tensor(mask[:, :, :], BC(g.iotaf[:, 0:R].unsqueeze(2), P, R, EJ),
                                       BC(g.etype[:, :].unsqueeze(1), P, R, EJ), ALU.is_equal))
                    up(v.tensor_scalar(neg[:, :, :], mask[:, :, :], 1.0, BIG, ALU.subtract, ALU.mult))
                    up(v.tensor_tensor(y[:, :, :], mask[:, :, :], BC(sel[:, :].unsqueeze(1), P, R, EJ), ALU.mult))
                    up(v.tensor_tensor(y[:, :, :], y[:, :, :], neg[:, :, :], ALU.add))
                    up(v.tensor_scalar(drop[:, :], cont[:, :], 1.0, BIG, ALU.subtract, ALU.mult))
                    up(v.tensor_scalar(lowered[:, :], opn[:, :], 1.0, BIG, ALU.subtract, ALU.mult))
                    up(v.tensor_scalar(ends[:, :], g.goes_on[:, :], -1.0, 1.0, ALU.mult, ALU.add))
                    up(v.tensor_tensor_scan(openb[:, ::-1], g.goes_on[:, ::-1], BC(g.ones[0:P, 0:1], P, EJ),
                                            1.0, ALU.mult, ALU.mult))

                    def to_all_edges():
                        up(v.tensor_tensor(f[:, :, :], f[:, :, :], BC(ends[:, :].unsqueeze(1), P, R, EJ), ALU.mult))
                        for r in range(R):
                            up(v.tensor_tensor_scan(y[:, r, ::-1], g.goes_on[:, ::-1], f[:, r, ::-1], 0.0,
                                                    ALU.mult, ALU.add))
                        up(v.tensor_copy(A[:, 0:R], BC(openb[:, 0:1], P, R)))
                        up(v.tensor_copy(B[:, 0:R], y[:, :, 0]))
                        carry(cback[:, :], R, ALU.mult, ALU.add, 0.0, back=True)
                        for r in range(R):
                            up(v.scalar_tensor_tensor(y[:, r, :], openb[:, :], cback[:, r:r + 1], y[:, r, :],
                                                      ALU.mult, ALU.add))
                        up(v.tensor_tensor(y[:, :, :], y[:, :, :], mask[:, :, :], ALU.mult))
                        up(v.tensor_reduce(sel[:, :], y[:, :, :].rearrange("p r j -> p j r"), AX.X, ALU.add))

                    for r in range(R):
                        up(v.tensor_tensor_scan(f[:, r, :], drop[:, :], y[:, r, :], -BIG, ALU.add, ALU.max))
                    up(v.tensor_copy(A[:, 0:R], BC(lowered[:, EJ - 1:], P, R)))
                    up(v.tensor_copy(B[:, 0:R], f[:, :, EJ - 1]))
                    carry(cm[:, :], R, ALU.add, ALU.max, -BIG)
                    for r in range(R):
                        up(v.scalar_tensor_tensor(f[:, r, :], lowered[:, :], cm[:, r:r + 1], f[:, r, :],
                                                  ALU.add, ALU.max))
                    to_all_edges()
                    up(v.tensor_tensor(w[:, :], lm[:, :], sel[:, :], ALU.subtract))
                    up(v.tensor_tensor(es[:, :], es[:, :], sel[:, :], ALU.subtract))
                    g.exp_in = n.n
                    scalar_done()
                    up(v.tensor_tensor(y[:, :, :], mask[:, :, :], BC(w[:, :].unsqueeze(1), P, R, EJ), ALU.mult))
                    for r in range(R):
                        up(v.tensor_tensor_scan(f[:, r, :], cont[:, :], y[:, r, :], 0.0, ALU.mult, ALU.add))
                    up(v.tensor_copy(A[:, 0:R], BC(opn[:, EJ - 1:], P, R)))
                    up(v.tensor_copy(B[:, 0:R], f[:, :, EJ - 1]))
                    carry(cm[:, :], R, ALU.mult, ALU.add, 0.0)
                    for r in range(R):
                        up(v.scalar_tensor_tensor(f[:, r, :], opn[:, :], cm[:, r:r + 1], f[:, r, :],
                                                  ALU.mult, ALU.add))
                    to_all_edges()
                    up(v.tensor_tensor(sel[:, :], sel[:, :], es[:, :], ALU.add))
                    up(v.reciprocal(sel[:, :], sel[:, :]))
                    up(v.tensor_tensor(w[:, :], w[:, :], sel[:, :], ALU.mult))
                    up(v.tensor_tensor(g.val[:, :, :], g.val[:, :, :], BC(w[:, :].unsqueeze(2), P, EJ, D), ALU.mult))

                flat = g.val[:, :, :].rearrange("p j f -> p f j")
                if layer == 0:
                    for h in range(H):
                        with v.Fori(0, HF // 8) as k:
                            for q in range(8):
                                col = flat[:, bass.ds(k * 8 + (h * HF + q), 1), :].rearrange("p a j -> p (a j)")
                                v.tensor_tensor_scan(col, fac[:, h, :], col, 0.0, ALU.mult, ALU.add).then_inc(scans, 1)
                else:
                    with v.Fori(0, D // 8) as k:
                        for q in range(8):
                            col = flat[:, bass.ds(k * 8 + q, 1), :].rearrange("p a j -> p (a j)")
                            v.tensor_tensor_scan(col, cont[:, :], col, 0.0, ALU.mult, ALU.add).then_inc(scans, 1)
                v.wait_ge(scans, D)
                if layer == 0:
                    up(v.tensor_copy(A[:, :].rearrange("p (h f) -> p h f", h=H),
                                     BC(g.reach[:, :, EJ - 1:], P, H, HF)))
                else:
                    up(v.tensor_copy(A[:, :], BC(opn[:, EJ - 1:], P, D)))
                up(v.tensor_copy(B[:, :], g.val[:, EJ - 1, :]))
                carry(g.carry[:, :], D, ALU.mult, ALU.add, 0.0)

            @block.scalar
            def _(a):
                if layer == 0:
                    a.wait_ge(vec, g.exp_in)
                    for x in (fac, w, wself):
                        last = a.activation(x[:, :, :], x[:, :, :], ACT.Exp)
                    last.then_inc(sca, 1)
                if layer == 3:
                    a.wait_ge(vec, g.exp_in)
                    for x in (w, es):
                        last = a.activation(x[:, :], x[:, :], ACT.Exp)
                    last.then_inc(sca, 1)

            @block.tensor
            def _(t):
                turn_carries(t, g, vec, ten, sizes, A, B, row, a_ps, b_ps, c_ps)


def scatter(g, layer):
    order = 1 if layer == 1 else 0
    step, staged, sent = g.sem("step_s"), g.sem("staged_s"), [g.once(f"sent{b}_s{layer}") for b in range(2)]
    copied = g.sem("idx_s")
    opn = g.open[order]
    with ExitStack() as ctx:
        stage = [g.sb(f"stage{b}_s{layer}", [P, G, D], F32, ctx) for b in range(2)]
        idx = [g.sb(f"idx{b}_s{layer}", [P, G], I32, ctx) for b in range(2)]
        with g.nc.Block() as block:
            @block.vector
            def _(v):
                def turn(c, b, has):
                    n = LoopCount(step, 3 if layer == 0 else 2)
                    at = bass.ds(c * G, G)
                    if has(-2):
                        v.wait_ge(sent[b], (c - b) * (8 * G))
                    if layer == 0:
                        for h in range(H):
                            f = slice(h * HF, (h + 1) * HF)
                            last = v.tensor_tensor(stage[b][:, :, f],
                                                   g.carry[:, f].unsqueeze(1).broadcast_to([P, G, HF]),
                                                   g.reach[:, h, at].unsqueeze(2).broadcast_to([P, G, HF]), ALU.mult)
                        n.up(last)
                    else:
                        n.up(v.tensor_tensor(stage[b][:, :, :], g.carry[:, :].unsqueeze(1).broadcast_to([P, G, D]),
                                             opn[:, at].unsqueeze(2).broadcast_to([P, G, D]), ALU.mult))
                    n.here(v, c)
                    last = v.tensor_tensor(stage[b][:, :, :], stage[b][:, :, :], g.val[:, at, :], ALU.add)
                    if layer == 0:
                        n.up(last)
                        n.here(v, c)
                        for h in range(H):
                            f = slice(h * HF, (h + 1) * HF)
                            last = v.tensor_tensor(stage[b][:, :, f], stage[b][:, :, f],
                                                   g.rz[:, h, at].unsqueeze(2).broadcast_to([P, G, HF]), ALU.mult)
                    n.up(last)
                    n.here(v, c)
                    v.sem_inc(staged, 1)

                turns(v, CH, 2, turn, 0, CH - 1)

            @block.gpsimd
            def _(pool):
                def turn(c, b, has):
                    if has(-2):
                        pool.wait_ge(sent[b], (c - b) * (8 * G))
                        g.passed(pool)
                    pool.tensor_copy(idx[b][:, :], g.out_row[order][:, bass.ds(c * G, G)]).then_inc(copied, 1)
                    pool.wait_ge(copied, c + 1)
                    g.passed(pool)
                    pool.wait_ge(staged, c + 1)
                    g.passed(pool)
                    for k in range(G):
                        pool.indirect_dma_start(out=g.aggr[layer],
                                                out_offset=bass.IndirectOffsetOnAxis(ap=idx[b][:, k:k + 1], axis=0),
                                                in_=stage[b][:, k, :], in_offset=None,
                                                bounds_check=N - 1, oob_is_err=False).then_inc(sent[b], 16)

                turns(pool, CH, 2, turn, 0, CH - 1)
                for b in range(2):
                    pool.wait_ge(sent[b], EJ * 8)


def nodes(g, layer):
    if layer == 0:
        return first_nodes(g)
    sem = lambda n: g.sem(f"{n}_n")
    lag = 2 if layer == 1 else 1
    row_in, turned, turned_out = [sem(f"in{q}") for q in range(4)], sem("turned"), sem("turned_out")
    made, summed, squared, reduced, rooted = sem("made"), sem("summed"), sem("squared"), sem("reduced"), sem("rooted")
    inverse, y_done, sent = sem("inverse"), sem("y_done"), [sem(f"sent{b}") for b in range(2)]
    zeroed = sem("zeroed")
    PAIRS = NG // 2
    with ExitStack() as ctx:
        sb = lambda n, s, d=F32: g.sb(f"{n}_n{layer}", s, d, ctx)
        ps = lambda n, s, d=F32: g.ps(f"{n}_n{layer}", s, d, ctx)
        two = lambda n, s: [sb(f"{n}{b}", s) for b in range(2)]
        rows, arow = [[sb(f"{n}{q}", [P, NG, D]) for q in range(4)] for n in ("rows", "arow")]
        y, v_sb = [two(n, [P, NG, D]) for n in ("y", "v")]
        xt = two("xt", [128, PAIRS * P])
        sq, q_sb, sd, rs = two("sq", [P, NG, D]), two("q", [P, NG]), two("sd", [P, NG]), two("rs", [P, NG])
        eps = sb("eps", [P, 1])
        out = [ps(f"out{b}", [P, NG, D]) for b in range(2)]
        tp = [ps(f"tp{b}", [128, PAIRS * P]) for b in range(2)]
        if layer == 1:
            at = two("at", [128, PAIRS * P])
            tpa = [ps(f"tpa{b}", [128, PAIRS * P]) for b in range(2)]
            h_ps = [ps(f"h{b}", [128, PAIRS * P]) for b in range(2)]
            h_sb = two("h_sb", [128, PAIRS * P])
            lab = two("lab", [P, NG, g.LW])
            hidden, hidden_out, aturned_out = sem("hidden"), sem("hidden_out"), sem("aturned_out")
            padded = sem("lab_padded")
            lab_done, lab_sent = sem("lab_done"), [sem(f"lab_sent{b}") for b in range(2)]
        dense = {1: g.wn2p, 2: g.n3p, 3: g.n4p}[layer]
        bias = {1: g.bn2c, 3: g.b4c}.get(layer)
        by_part = lambda table: table.rearrange("(p k) d -> p k d", p=P)
        src, asrc, labelled = by_part(g.feat[layer]), by_part(g.aggr[layer]), by_part(g.labelled)
        dst = by_part(g.feat[layer + 1] if layer < 3 else g.out)

        all_turns = lambda eng, turn, first, last: turns(eng, NCH, 5, turn, first, last, ring=4)
        with g.nc.Block() as block:
            @block.sync
            def _(sp):
                def turn(c, q, has):
                    if has(2):
                        at, into = bass.ds((c + 2) * NG, NG), (q + 2) % 4
                        if has(-2):
                            sp.wait_ge(summed, c - 1)
                            g.passed(sp)
                        sp.dma_start(rows[into][:, :, :], src[:, at, :]).then_inc(row_in[into], 16)
                        sp.dma_start(arow[into][:, :, :], asrc[:, at, :]).then_inc(row_in[into], 16)
                    if has(-lag - 2):
                        j, b = c - (lag + 2), (q - lag) % 2
                        at = bass.ds(j * NG, NG)
                        sp.wait_ge(y_done, j + 1)
                        g.passed(sp)
                        sp.dma_start(dst[:, at, :], y[b][:, :, :]).then_inc(sent[b], 16)
                        if layer == 1:
                            sp.wait_ge(lab_done, j * 2 + 2)
                            g.passed(sp)
                            sp.dma_start(labelled[:, at, :], lab[b][:, :, :]).then_inc(lab_sent[b], 16)

                all_turns(sp, turn, -2, NCH + lag + 1)
                for b in range(2):
                    sp.wait_ge(sent[b], NCH * 8)
                    if layer == 1:
                        sp.wait_ge(lab_sent[b], NCH * 8)

            @block.tensor
            def _(t):
                def turn(c, q, has):
                    b, o = q % 2, (q + 1) % 2
                    if has(0):
                        t.wait_ge(row_in[q], (c - q) * 8 + 32)
                        for side, to in ((rows, tp), (arow, tpa)) if layer == 1 else ((rows, tp),):
                            for k in range(PAIRS):
                                last = t.transpose(to[b][:, k * P:(k + 1) * P],
                                                   side[q][:, 2 * k:2 * k + 2, :].rearrange("p k d -> p (k d)"),
                                                   g.ident[0:P, 0:P])
                            last.then_inc(turned, 1)
                    if layer == 1 and has(-1):
                        t.wait_ge(turned_out, c)
                        t.matmul(h_ps[o][:, :], g.wn1x[:, :], xt[o][:, :], start=True, stop=False)
                        t.wait_ge(aturned_out, c)
                        t.matmul(h_ps[o][:, :], g.wn1g[:, :], at[o][:, :], start=False, stop=True).then_inc(hidden, 1)
                    if has(-lag):
                        kb = (q - lag) % 2
                        t.wait_ge(hidden_out if layer == 1 else turned_out, c - (lag - 1))
                        if has(-lag - 2):
                            t.wait_ge(summed, c - (lag + 1))
                        flat = out[kb][:, :, :].rearrange("p k d -> p (k d)")
                        if bias is not None:
                            t.matmul(flat, g.onesb[:, :], bias[:, :, :].rearrange("p k d -> p (k d)"), start=True,
                                     stop=False, skip_group_check=True)
                        lhs = h_sb[kb] if layer == 1 else xt[kb]
                        for k in range(PAIRS):
                            last = t.matmul(flat[:, 2 * D * k:2 * D * (k + 1)], lhs[:, k * P:(k + 1) * P], dense[:, :],
                                            start=bias is None, stop=True, skip_group_check=True)
                        last.then_inc(made, 1)

                all_turns(t, turn, 0, NCH - 1 + lag)

            @block.scalar
            def _(a):
                a.activation(eps[:, :], g.ones[0:P, 0:1], ACT.Copy, scale=1e-5).then_inc(zeroed, 1)
                a.wait_ge(zeroed, 1)

                def turn(c, q, has):
                    b, o, jb = q % 2, (q + 1) % 2, (q - lag - 1) % 2
                    if has(0):
                        if has(-2):
                            a.wait_ge(hidden if layer == 1 else made, c - 1)
                        a.wait_ge(turned, c * lag + 1)
                        a.activation(xt[b][:, :], tp[b][:, :], ACT.Copy).then_inc(turned_out, 1)
                    if has(-lag - 1):
                        a.wait_ge(summed, c - lag)
                        a.activation(sq[jb][:, :, :], v_sb[jb][:, :, :], ACT.Square).then_inc(squared, 1)
                        a.wait_ge(reduced, c - lag)
                        a.activation(sd[jb][:, :], q_sb[jb][:, :], ACT.Sqrt, scale=1.0 / D, bias=eps[:, 0:1]).then_inc(rooted, 1)
                    if layer == 1 and has(-1):
                        a.wait_ge(hidden, c)
                        if has(-3):
                            a.wait_ge(made, c - 2)
                        a.activation(h_sb[o][:, :], h_ps[o][:, :], ACT.Silu, bias=g.bn1p[:, 0:1]).then_inc(hidden_out, 1)

                all_turns(a, turn, 0, NCH + lag)

            @block.vector
            def _(v):
                def turn(c, q, has):
                    kq, kb, jb = (q - lag) % 4, (q - lag) % 2, (q - lag - 1) % 2
                    if layer == 1 and has(0):
                        v.wait_ge(turned, c * 2 + 2)
                        if has(-2):
                            v.wait_ge(hidden, c - 1)
                        v.tensor_copy(at[q % 2][:, :], tpa[q % 2][:, :]).then_inc(aturned_out, 1)
                    if has(-lag - 1):
                        v.wait_ge(squared, c - lag)
                        v.tensor_reduce(q_sb[jb][:, :], sq[jb][:, :, :], AX.X, ALU.add).then_inc(reduced, 1)
                    if has(-lag):
                        v.wait_ge(made, c - (lag - 1))
                        if has(-lag - 2):
                            v.wait_ge(y_done, c - (lag + 1))
                        v.tensor_tensor(v_sb[kb][:, :, :], out[kb][:, :, :], (rows if layer == 1 else arow)[kq][:, :, :],
                                        ALU.add).then_inc(summed, 1)
                    if has(-lag - 1):
                        v.wait_ge(rooted, c - lag)
                        v.reciprocal(rs[jb][:, :], sd[jb][:, :]).then_inc(inverse, 1)
                        v.wait_ge(inverse, c - lag)
                        if has(-lag - 3):
                            v.wait_ge(sent[jb], (c - (lag + 1 + jb)) * 8)
                            if layer == 1:
                                v.wait_ge(lab_done, (c - (lag + 2)) * 2 - 1)
                        v.tensor_tensor(y[jb][:, :, :], v_sb[jb][:, :, :],
                                        rs[jb][:, :].unsqueeze(2).broadcast_to([P, NG, D]), ALU.mult).then_inc(y_done, 1)

                all_turns(v, turn, 0, NCH + lag)

            if layer == 1:
                @block.gpsimd
                def _(pool):
                    for b in range(2):
                        pool.memset(lab[b][:, :, D:], 0.0).then_inc(padded, 1)
                    pool.wait_ge(padded, 2)

                    def turn(j, q, has):
                        b = q % 2
                        if has(-2):
                            pool.wait_ge(lab_sent[b], (j - b) * 8)
                            g.passed(pool)
                        pool.wait_ge(y_done, j + 1)
                        g.passed(pool)
                        pool.tensor_copy(lab[b][:, :, 0:D], y[b][:, :, :]).then_inc(lab_done, 1)
                        pool.tensor_copy(lab[b][:, :, D:D + 1], g.label[:, bass.ds(j * NG, NG)].unsqueeze(2)
                                         ).then_inc(lab_done, 1)

                    all_turns(pool, turn, 0, NCH - 1)


def first_nodes(g):
    sem = lambda n: g.sem(f"{n}_n")
    row_in, turned, turned_out = [sem(f"in{q}") for q in range(4)], sem("turned"), sem("turned_out")
    made, relu_done, exp_done, rooted1, rooted2 = sem("made"), sem("summed"), sem("squared"), sem("rooted"), sem("rooted2")
    squared1, squared2, centred1, centred2 = sem("squared1"), sem("squared2"), sem("centred1"), sem("centred2")
    scaled, shifted, sent, zeroed = sem("scaled"), sem("shifted"), [sem(f"sent{b}") for b in range(2)], sem("zeroed")
    elu_steps, norm1_steps, norm2_steps = sem("elu_steps"), sem("norm1_steps"), sem("norm2_steps")
    ELU, SUM1, MEAN1, PER_ELU = 1, 2, 3, 3
    Q1, INV1, SCALE1, ADDED, SUM2, MEAN2, PER_NORM1 = 1, 2, 3, 4, 5, 6, 6
    Q2, INV2, Y, PER_NORM2 = 1, 2, 3, 3
    PAIRS = NG // 2
    with ExitStack() as ctx:
        sb = lambda n, s, d=F32: g.sb(f"{n}_n0", s, d, ctx)
        ps = lambda n, s, d=F32: g.ps(f"{n}_n0", s, d, ctx)
        two = lambda n, s: [sb(f"{n}{b}", s) for b in range(2)]
        rows, arow = [[sb(f"{n}{q}", [P, NG, D]) for q in range(4)] for n in ("rows", "arow")]
        y, e, u, cd, cs, sq1, sq2, xb, w, ce = [two(n, [P, NG, D]) for n in (
            "y", "e", "u", "cd", "cs", "sq1", "sq2", "xb", "w", "ce")]
        xt = two("xt", [128, PAIRS * P])
        mean1, mean2, q1, q2, sd1, sd2, rs1, rs2 = [two(n, [P, NG]) for n in (
            "mean1", "mean2", "q1", "q2", "sd1", "sd2", "rs1", "rs2")]
        eps = sb("eps", [P, 2])
        tp = [ps(f"tp{b}", [128, PAIRS * P]) for b in range(2)]
        out = [ps(f"out{b}", [P, NG, D]) for b in range(2)]
        src, asrc, dst = [table.rearrange("(p k) d -> p k d", p=P) for table in (g.feat[0], g.aggr[0], g.feat[1])]
        wide = lambda x: x[:, :].unsqueeze(2).broadcast_to([P, NG, D])
        flat = lambda x: x[:, :, :].rearrange("p k d -> p (k d)")
        ln_row = lambda k: g.lnw[:, k, :].unsqueeze(1).broadcast_to([P, NG, D])
        all_turns = lambda eng, turn, first, last: turns(eng, NCH, 5, turn, first, last, ring=4)
        with g.nc.Block() as block:
            @block.sync
            def _(sp):
                def turn(c, q, has):
                    b = q % 2
                    if has(2):
                        at, into = bass.ds((c + 2) * NG, NG), (q + 2) % 4
                        if has(-2):
                            sp.wait_ge(made, c - 1)
                            g.passed(sp)
                            sp.wait_ge(shifted, c - 1)
                            g.passed(sp)
                        sp.dma_start(rows[into][:, :, :], src[:, at, :]).then_inc(row_in[into], 16)
                        sp.dma_start(arow[into][:, :, :], asrc[:, at, :]).then_inc(row_in[into], 16)
                    if has(-2):
                        sp.wait_ge(norm2_steps, (c - 2) * PER_NORM2 + Y)
                        g.passed(sp)
                        sp.dma_start(dst[:, bass.ds((c - 2) * NG, NG), :], y[b][:, :, :]).then_inc(sent[b], 16)

                all_turns(sp, turn, -2, NCH + 1)
                for b in range(2):
                    sp.wait_ge(sent[b], NCH * 8)

            @block.tensor
            def _(t):
                def turn(c, q, has):
                    b = q % 2
                    t.wait_ge(row_in[q], (c - q) * 8 + 32)
                    for k in range(PAIRS):
                        last = t.transpose(tp[b][:, k * P:(k + 1) * P],
                                           rows[q][:, 2 * k:2 * k + 2, :].rearrange("p k d -> p (k d)"), g.ident[0:P, 0:P])
                    last.then_inc(turned, 1)
                    if has(-2):
                        t.wait_ge(elu_steps, (c - 2) * PER_ELU + ELU)
                    t.matmul(flat(out[b]), g.ident[0:P, 0:P], flat(arow[q]), start=True, stop=False, skip_group_check=True)
                    t.wait_ge(turned_out, c + 1)
                    for k in range(PAIRS):
                        last = t.matmul(flat(out[b])[:, 2 * D * k:2 * D * (k + 1)], xt[b][:, k * P:(k + 1) * P], g.n1p[:, :],
                                        start=False, stop=True, skip_group_check=True)
                    last.then_inc(made, 1)

                all_turns(t, turn, 0, NCH - 1)

            @block.scalar
            def _(a):
                a.activation(eps[:, 0:1], g.ones[0:P, 0:1], ACT.Copy, scale=1e-6).then_inc(zeroed, 1)
                a.activation(eps[:, 1:2], g.ones[0:P, 0:1], ACT.Copy, scale=1e-5).then_inc(zeroed, 1)
                a.wait_ge(zeroed, 2)

                def turn(c, q, has):
                    b, o = q % 2, (q + 1) % 2
                    if has(-1):
                        a.wait_ge(centred1, c)
                        a.activation(sq1[o][:, :, :], cd[o][:, :, :], ACT.Square).then_inc(squared1, 1)
                    if has(1):
                        a.wait_ge(turned, c + 2)
                        a.activation(xt[o][:, :], tp[o][:, :], ACT.Copy).then_inc(turned_out, 1)
                    if has(-2):
                        a.wait_ge(centred2, c - 1)
                        a.activation(sq2[b][:, :, :], ce[b][:, :, :], ACT.Square).then_inc(squared2, 1)
                    if has(-1):
                        a.wait_ge(norm1_steps, (c - 1) * PER_NORM1 + Q1)
                        a.activation(sd1[o][:, :], q1[o][:, :], ACT.Sqrt, scale=1.0 / D, bias=eps[:, 0:1]).then_inc(rooted1, 1)
                    if has(-2):
                        a.wait_ge(norm2_steps, (c - 2) * PER_NORM2 + Q2)
                        a.activation(sd2[b][:, :], q2[b][:, :], ACT.Sqrt, scale=1.0 / D, bias=eps[:, 1:2]).then_inc(rooted2, 1)
                    if has(1):
                        a.wait_ge(made, c + 2)
                        a.activation(e[o][:, :, :], out[o][:, :, :], ACT.Relu, scale=-1.0).then_inc(relu_done, 1)
                        a.wait_ge(relu_done, c + 2)
                        a.activation(e[o][:, :, :], e[o][:, :, :], ACT.Exp, scale=-1.0).then_inc(exp_done, 1)

                all_turns(a, turn, -1, NCH + 1)

            @block.vector
            def _(v):
                def turn(c, q, has):
                    b, o = q % 2, (q + 1) % 2
                    if has(-1):
                        v.wait_ge(squared1, c)
                        v.tensor_reduce(q1[o][:, :], sq1[o][:, :, :], AX.X, ALU.add).then_inc(norm1_steps, 1)
                    if has(0):
                        v.wait_ge(exp_done, c + 1)
                        v.scalar_tensor_tensor(u[b][:, :, :], e[b][:, :, :], -1.0, out[b][:, :, :], ALU.add, ALU.max
                                               ).then_inc(elu_steps, 1)
                        v.wait_ge(elu_steps, c * PER_ELU + ELU)
                        v.tensor_reduce(mean1[b][:, :], u[b][:, :, :], AX.X, ALU.add).then_inc(elu_steps, 1)
                    if has(-2):
                        v.wait_ge(squared2, c - 1)
                        v.tensor_reduce(q2[b][:, :], sq2[b][:, :, :], AX.X, ALU.add).then_inc(norm2_steps, 1)
                    if has(0):
                        v.wait_ge(elu_steps, c * PER_ELU + SUM1)
                        v.tensor_scalar(mean1[b][:, :], mean1[b][:, :], -1.0 / D, None, ALU.mult).then_inc(elu_steps, 1)
                    if has(-1):
                        done = lambda k: v.wait_ge(norm1_steps, (c - 1) * PER_NORM1 + k)
                        v.wait_ge(rooted1, c)
                        v.reciprocal(rs1[o][:, :], sd1[o][:, :]).then_inc(norm1_steps, 1)
                        done(INV1)
                        v.wait_ge(scaled, c)
                        v.tensor_tensor(w[o][:, :, :], cs[o][:, :, :], wide(rs1[o]), ALU.mult).then_inc(norm1_steps, 1)
                        done(SCALE1)
                        v.wait_ge(shifted, c)
                        v.tensor_tensor(w[o][:, :, :], w[o][:, :, :], xb[o][:, :, :], ALU.add).then_inc(norm1_steps, 1)
                        done(ADDED)
                        v.tensor_reduce(mean2[o][:, :], w[o][:, :, :], AX.X, ALU.add).then_inc(norm1_steps, 1)
                        done(SUM2)
                        v.tensor_scalar(mean2[o][:, :], mean2[o][:, :], -1.0 / D, None, ALU.mult).then_inc(norm1_steps, 1)
                    if has(-2):
                        v.wait_ge(rooted2, c - 1)
                        v.reciprocal(rs2[b][:, :], sd2[b][:, :]).then_inc(norm2_steps, 1)
                        v.wait_ge(norm2_steps, (c - 2) * PER_NORM2 + INV2)
                        if has(-4):
                            v.wait_ge(sent[b], (c - b) * 8 - 16)
                        v.tensor_tensor(y[b][:, :, :], ce[b][:, :, :], wide(rs2[b]), ALU.mult).then_inc(norm2_steps, 1)

                all_turns(v, turn, 0, NCH + 1)

            @block.gpsimd
            def _(pool):
                def turn(c, q, has):
                    b, o = q % 2, (q + 1) % 2
                    if has(0):
                        pool.wait_ge(elu_steps, c * PER_ELU + MEAN1)
                        g.passed(pool)
                        pool.tensor_tensor(cd[b][:, :, :], u[b][:, :, :], wide(mean1[b]), ALU.add).then_inc(centred1, 1)
                        pool.wait_ge(centred1, c + 1)
                        g.passed(pool)
                        pool.tensor_tensor(cs[b][:, :, :], cd[b][:, :, :], ln_row(0), ALU.mult).then_inc(scaled, 1)
                    if has(-1):
                        pool.wait_ge(norm1_steps, (c - 1) * PER_NORM1 + MEAN2)
                        g.passed(pool)
                        pool.tensor_tensor(ce[o][:, :, :], w[o][:, :, :], wide(mean2[o]), ALU.add).then_inc(centred2, 1)
                    if has(1):
                        nq = (q + 1) % 4
                        pool.wait_ge(row_in[nq], (c + 1 - nq) * 8 + 32)
                        g.passed(pool)
                        pool.tensor_tensor(xb[o][:, :, :], rows[nq][:, :, :], ln_row(1), ALU.add).then_inc(shifted, 1)

                all_turns(pool, turn, -1, NCH)


def build(nc, args, out, features, aggregates, labelled, sorted_, layers=4):
    with ExitStack() as ctx:
        g = Graph(nc, args, ctx)
        g.feat, g.aggr, g.out, g.labelled, g.sorted = [args["x"]] + features, aggregates, out, labelled, sorted_
        g.LW = labelled.shape[1]
        g.ends_of = [g.sb(f"ends_of{s}", [P, 2, EJ], I32) for s in range(2)]
        g.out_row = [g.sb(f"out_row{s}", [P, EJ], I32) for s in range(2)]
        g.cont = [g.sb(f"cont{s}", [P, EJ]) for s in range(2)]
        g.open = [g.sb(f"open{s}", [P, EJ]) for s in range(2)]
        g.goes_on = g.sb("goes_on", [P, EJ])
        g.etype, g.radial, g.attn = g.sb("etype", [P, EJ]), g.sb("radial", [P, EJ]), g.sb("attn", [P, H, EJ])
        g.iotaf = g.sb("iotaf", [P, R])
        weights(g)
        with ExitStack() as sorting:
            g.rec = g.sb("rec", [P, EJ, REC], F32, sorting)
            g.keys = g.sb("keys", [P, 4, EJ + 2], F32, sorting)
            g.iota = g.sb("iota", [P, 2 * HB], BF16, sorting)
            g.base = g.sb("base", [HB, 2, 2 * LO], F32, sorting)
            g.strict = g.sb("strict", [P, P], F32, sorting)
            load_and_constants(g)
            histogram(g)
            rank_and_scatter(g)
        read_orders(g)
        g.clear()
        g.val = g.sb("val", [P, EJ, D])
        g.score = g.sb("score", [P, 2 * H, EJ])
        g.reach, g.rz, g.carry = g.sb("reach", [P, H, EJ]), g.sb("rz", [P, H, EJ]), g.sb("carry", [P, D])
        for layer in range(layers):
            for phase in (edges, segments, scatter, nodes):
                phase(g, layer)
                g.clear()


def kernel(**inputs):
    import numpy as _np
    import concourse.bacc as _bacc
    from concourse import mybir as _mybir
    from concourse.bass_utils import run_bass_kernel_spmd as _run

    nc = _bacc.Bacc("TRN2", target_bir_lowering=False, num_devices=1)
    arrays, args = {}, {}
    for name, value in inputs.items():
        arr = _np.ascontiguousarray(value)
        arrays[f"in_{name}"] = arr
        args[name] = nc.dram_tensor(f"in_{name}", arr.shape, _mybir.dt.from_np(arr.dtype), kind="ExternalInput").ap()
    out = nc.dram_tensor("out_0", (N, D), F32, kind="ExternalOutput").ap()
    features = [nc.dram_tensor(f"features{k + 1}", (N, D), F32, kind="Internal").ap() for k in range(3)]
    aggregates = [nc.dram_tensor(f"aggregates{k}", (N, D), F32, kind="Internal").ap() for k in range(4)]
    labelled = nc.dram_tensor("labelled", (N, 72), F32, kind="Internal").ap()
    sorted_ = [nc.dram_tensor(f"sorted{k}", (E, REC), F32, kind="Internal").ap() for k in range(2)]
    build(nc, args, out, features, aggregates, labelled, sorted_)
    r = _run(nc, [arrays], core_ids=[0])
    return r.results[0]["out_0"]
```
